# Optimizing a Trainium2 kernel written in Bass

```python
import numpy as np
import jax
import jax.numpy as jnp

def _softmax(x, axis=-1):
    return jax.nn.softmax(x, axis=axis)

def _gelu(x):
    return jax.nn.gelu(x, approximate=True)

def _silu(x):
    return jax.nn.silu(x)

def _sigmoid(x):
    return jax.nn.sigmoid(x)

def _layernorm(x, axis=-1, eps=1e-05):
    m = jnp.mean(x, axis=axis, keepdims=True)
    v = jnp.var(x, axis=axis, keepdims=True)
    return (x - m) / jnp.sqrt(v + eps)

def _scatter_add(tgt, idx, src, axis=0):
    return tgt.at[idx].add(src)

def _segment_sum(src, seg, n):
    return jax.ops.segment_sum(src, seg, n)
kernel_name = 'mk_hybrid_d1_jaxref_r8_367097'

def setup_inputs(seed: int=0):
    np.random.seed(seed)
    _w = jnp.asarray

    def _L0_attn_a_setup():
        import jax, jax.numpy as jnp
        import numpy as np
        import math
        N_EMBD = 128
        N_HEAD = 16
        HEAD_DIM = N_EMBD // N_HEAD // 2
        DEPTH = 1
        LAMBDA_INIT = 0.8 - 0.6 * math.exp(-0.3 * (DEPTH - 1))
        EPS = 1e-05
        key = jax.random.key(seed)
        ks = jax.random.split(key, 8)
        B, T, C = (4, 128, N_EMBD)
        x = jax.random.normal(ks[0], (B, T, C), dtype=jnp.float32)
        w_attn = jax.random.normal(ks[1], (C, 3 * C), dtype=jnp.float32) * (1.0 / math.sqrt(C))
        w_proj = jax.random.normal(ks[2], (C, C), dtype=jnp.float32) * (1.0 / math.sqrt(C))
        lambda_q1 = jax.random.normal(ks[3], (HEAD_DIM,), dtype=jnp.float32) * 0.1
        lambda_q2 = jax.random.normal(ks[4], (HEAD_DIM,), dtype=jnp.float32) * 0.1
        lambda_k1 = jax.random.normal(ks[5], (HEAD_DIM,), dtype=jnp.float32) * 0.1
        lambda_k2 = jax.random.normal(ks[6], (HEAD_DIM,), dtype=jnp.float32) * 0.1
        gamma = jnp.ones((2 * HEAD_DIM,), dtype=jnp.float32)
        return {'x': x, 'w_attn': w_attn, 'w_proj': w_proj, 'lambda_q1': lambda_q1, 'lambda_q2': lambda_q2, 'lambda_k1': lambda_k1, 'lambda_k2': lambda_k2, 'gamma': gamma}
    _L0_attn_a_in = _L0_attn_a_setup()

    def _L0_attn_b_setup():
        import jax, jax.numpy as jnp
        import numpy as np
        B, S, D = (4, 256, 128)
        H, C = (16, 64)
        HID = H * C
        key = jax.random.key(seed)
        ks = jax.random.split(key, 9)
        scale = 0.02
        return {'x': jax.random.normal(ks[0], (B, S, D), dtype=jnp.float32), 'Wq': jax.random.normal(ks[1], (D, HID), dtype=jnp.float32) * scale, 'bq': jnp.zeros((HID,), dtype=jnp.float32), 'Wk': jax.random.normal(ks[2], (D, HID), dtype=jnp.float32) * scale, 'bk': jnp.zeros((HID,), dtype=jnp.float32), 'Wv': jax.random.normal(ks[3], (D, HID), dtype=jnp.float32) * scale, 'bv': jnp.zeros((HID,), dtype=jnp.float32), 'Wo': jax.random.normal(ks[4], (HID, D), dtype=jnp.float32) * scale, 'bo': jnp.zeros((D,), dtype=jnp.float32)}
    _L0_attn_b_in = _L0_attn_b_setup()

    def _L0_ffn_setup():
        import jax, jax.numpy as jnp
        import numpy as np
        B, C, D, O = (4, 512, 128, 128)
        PROJ = 32
        RANKS = [1, 2, 4, 8]
        E = len(RANKS)
        CLAMP_MAX = float(np.log(1.0 / 0.01))

        def _l2norm(v, axis):
            return v / jnp.maximum(jnp.linalg.norm(v, axis=axis, keepdims=True), 1e-12)
        key = jax.random.key(seed)
        ks = jax.random.split(key, 16)
        inp = {'x': jax.random.normal(ks[0], (B, C, D), dtype=jnp.float32), 'W': jax.random.normal(ks[1], (O, D), dtype=jnp.float32) / np.sqrt(D), 'Wp': jax.random.normal(ks[2], (PROJ, D), dtype=jnp.float32) / np.sqrt(D), 'bp': jnp.zeros((PROJ,), dtype=jnp.float32), 'sim': jax.random.normal(ks[3], (PROJ, E), dtype=jnp.float32) * 0.01, 'temp': jnp.full((1,), np.log(1.0 / 0.5), dtype=jnp.float32)}
        for i, r in enumerate(RANKS):
            inp[f'Wd{i}'] = jax.random.normal(ks[4 + 2 * i], (r, D), dtype=jnp.float32) / r
            inp[f'Wu{i}'] = jax.random.normal(ks[5 + 2 * i], (O, r), dtype=jnp.float32) * 0.01
        return inp
    _L0_ffn_in = _L0_ffn_setup()
    _d = {'L0_attn_a_x': _L0_attn_a_in['x'], 'L0_attn_a_w_attn': _L0_attn_a_in['w_attn'], 'L0_attn_a_w_proj': _L0_attn_a_in['w_proj'], 'L0_attn_a_lambda_q1': _L0_attn_a_in['lambda_q1'], 'L0_attn_a_lambda_q2': _L0_attn_a_in['lambda_q2'], 'L0_attn_a_lambda_k1': _L0_attn_a_in['lambda_k1'], 'L0_attn_a_lambda_k2': _L0_attn_a_in['lambda_k2'], 'L0_attn_a_gamma': _L0_attn_a_in['gamma'], 'L0_attn_b_Wq': _L0_attn_b_in['Wq'], 'L0_attn_b_bq': _L0_attn_b_in['bq'], 'L0_attn_b_Wk': _L0_attn_b_in['Wk'], 'L0_attn_b_bk': _L0_attn_b_in['bk'], 'L0_attn_b_Wv': _L0_attn_b_in['Wv'], 'L0_attn_b_bv': _L0_attn_b_in['bv'], 'L0_attn_b_Wo': _L0_attn_b_in['Wo'], 'L0_attn_b_bo': _L0_attn_b_in['bo'], 'L0_ffn_W': _L0_ffn_in['W'], 'L0_ffn_Wp': _L0_ffn_in['Wp'], 'L0_ffn_bp': _L0_ffn_in['bp'], 'L0_ffn_sim': _L0_ffn_in['sim'], 'L0_ffn_temp': _L0_ffn_in['temp'], 'L0_ffn_Wd0': _L0_ffn_in['Wd0'], 'L0_ffn_Wu0': _L0_ffn_in['Wu0'], 'L0_ffn_Wd1': _L0_ffn_in['Wd1'], 'L0_ffn_Wu1': _L0_ffn_in['Wu1'], 'L0_ffn_Wd2': _L0_ffn_in['Wd2'], 'L0_ffn_Wu2': _L0_ffn_in['Wu2'], 'L0_ffn_Wd3': _L0_ffn_in['Wd3'], 'L0_ffn_Wu3': _L0_ffn_in['Wu3']}
    _x0 = _d['L0_attn_a_x']
    _d['L0_attn_a_x'] = jax.random.normal(jax.random.fold_in(jax.random.key(seed), 1), (2, 1024, 128), dtype=_x0.dtype)
    del _x0
    return _d

def reference(L0_attn_a_x, L0_attn_a_w_attn, L0_attn_a_w_proj, L0_attn_a_lambda_q1, L0_attn_a_lambda_q2, L0_attn_a_lambda_k1, L0_attn_a_lambda_k2, L0_attn_a_gamma, L0_attn_b_Wq, L0_attn_b_bq, L0_attn_b_Wk, L0_attn_b_bk, L0_attn_b_Wv, L0_attn_b_bv, L0_attn_b_Wo, L0_attn_b_bo, L0_ffn_W, L0_ffn_Wp, L0_ffn_bp, L0_ffn_sim, L0_ffn_temp, L0_ffn_Wd0, L0_ffn_Wu0, L0_ffn_Wd1, L0_ffn_Wu1, L0_ffn_Wd2, L0_ffn_Wu2, L0_ffn_Wd3, L0_ffn_Wu3):

    def _L0_attn_a_ref(x, w_attn, w_proj, lambda_q1, lambda_q2, lambda_k1, lambda_k2, gamma):
        import jax, jax.numpy as jnp
        import numpy as np
        import math
        N_EMBD = 128
        N_HEAD = 16
        HEAD_DIM = N_EMBD // N_HEAD // 2
        DEPTH = 1
        LAMBDA_INIT = 0.8 - 0.6 * math.exp(-0.3 * (DEPTH - 1))
        EPS = 1e-05
        B, T, C = x.shape
        H, hd = (N_HEAD, HEAD_DIM)
        qkv = x @ w_attn
        q, k, v = jnp.split(qkv, 3, axis=-1)
        q = q.reshape(B, T, 2 * H, hd).transpose(0, 2, 1, 3)
        k = k.reshape(B, T, 2 * H, hd).transpose(0, 2, 1, 3)
        v = v.reshape(B, T, H, 2 * hd).transpose(0, 2, 1, 3)
        q = q * hd ** (-0.5)
        att = jnp.einsum('bhtd,bhsd->bhts', q, k) * (1.0 / math.sqrt(hd))
        causal = jnp.tril(jnp.ones((T, T), dtype=bool))
        att = jnp.where(causal, att, -jnp.inf)
        att = jax.nn.softmax(att, axis=-1)
        lam1 = jnp.exp(jnp.sum(lambda_q1 * lambda_k1))
        lam2 = jnp.exp(jnp.sum(lambda_q2 * lambda_k2))
        lambda_full = lam1 - lam2 + LAMBDA_INIT
        att = att.reshape(B, H, 2, T, T)
        att = att[:, :, 0] - lambda_full * att[:, :, 1]
        out = jnp.einsum('bhts,bhsd->bhtd', att, v)
        rms = jax.lax.rsqrt(jnp.mean(out * out, axis=-1, keepdims=True) + EPS)
        out = out * rms * gamma
        out = (1.0 - LAMBDA_INIT) * out
        out = out.transpose(0, 2, 1, 3).reshape(B, T, C)
        return out @ w_proj

    def _L0_attn_b_ref(x, Wq, bq, Wk, bk, Wv, bv, Wo, bo):
        import jax, jax.numpy as jnp
        import numpy as np
        B, S, D = (4, 256, 128)
        H, C = (16, 64)
        HID = H * C
        b, s, _ = x.shape
        inv_sqrt_c = jnp.asarray(1.0 / C ** 0.5, dtype=x.dtype)
        Q = (x @ Wq + bq).reshape(b, s, H, C) * inv_sqrt_c
        K = (x @ Wk + bk).reshape(b, s, H, C)
        V = (x @ Wv + bv).reshape(b, s, H, C)
        scores = jnp.einsum('bshq,bshk->bshqk', Q, K)
        mask = jnp.triu(jnp.ones((C, C), dtype=bool), 1)
        scores = jnp.where(mask, jnp.asarray(-jnp.inf, scores.dtype), scores)
        w = jax.nn.softmax(scores, axis=-1)
        attn = jnp.einsum('bshqk,bshk->bshq', w, V)
        attn = attn.reshape(b, s, HID)
        return attn @ Wo + bo

    def _L0_ffn_ref(x, W, Wp, bp, sim, temp, Wd0, Wu0, Wd1, Wu1, Wd2, Wu2, Wd3, Wu3):
        import jax, jax.numpy as jnp
        import numpy as np
        B, C, D, O = (4, 512, 128, 128)
        PROJ = 32
        RANKS = [1, 2, 4, 8]
        E = len(RANKS)
        CLAMP_MAX = float(np.log(1.0 / 0.01))

        def _l2norm(v, axis):
            return v / jnp.maximum(jnp.linalg.norm(v, axis=axis, keepdims=True), 1e-12)
        base = jnp.einsum('bcd,od->bco', x, W)
        xf = x.reshape(-1, x.shape[-1])
        proj = _l2norm(xf @ Wp.T + bp, axis=1)
        simn = _l2norm(sim, axis=0)
        scale = jnp.exp(jnp.minimum(temp, CLAMP_MAX))
        logits = proj @ simn * scale
        lw = jax.nn.softmax(logits, axis=1)
        top1 = jnp.argmax(lw, axis=1)
        ret = jnp.where(jnp.arange(E)[None, :] == top1[:, None], lw, 0.0)
        ret = ret.reshape(x.shape[0], x.shape[1], E)
        downs = (Wd0, Wd1, Wd2, Wd3)
        ups = (Wu0, Wu1, Wu2, Wu3)
        l = jnp.stack([jnp.einsum('bcr,or->bco', jnp.einsum('bcd,rd->bcr', x, d), u) for d, u in zip(downs, ups)], axis=2)
        res = jnp.sum(ret[..., None] * l, axis=2)
        return base + res
    x = L0_attn_a_x
    x = x + _L0_attn_a_ref(_layernorm(x, axis=-1), L0_attn_a_w_attn, L0_attn_a_w_proj, L0_attn_a_lambda_q1, L0_attn_a_lambda_q2, L0_attn_a_lambda_k1, L0_attn_a_lambda_k2, L0_attn_a_gamma)
    x = x + _L0_ffn_ref(_layernorm(x, axis=-1), L0_ffn_W, L0_ffn_Wp, L0_ffn_bp, L0_ffn_sim, L0_ffn_temp, L0_ffn_Wd0, L0_ffn_Wu0, L0_ffn_Wd1, L0_ffn_Wu1, L0_ffn_Wd2, L0_ffn_Wu2, L0_ffn_Wd3, L0_ffn_Wu3)
    x = x + _L0_attn_b_ref(_layernorm(x, axis=-1), L0_attn_b_Wq, L0_attn_b_bq, L0_attn_b_Wk, L0_attn_b_bk, L0_attn_b_Wv, L0_attn_b_bv, L0_attn_b_Wo, L0_attn_b_bo)
    x = x + _L0_ffn_ref(_layernorm(x, axis=-1), L0_ffn_W, L0_ffn_Wp, L0_ffn_bp, L0_ffn_sim, L0_ffn_temp, L0_ffn_Wd0, L0_ffn_Wu0, L0_ffn_Wd1, L0_ffn_Wu1, L0_ffn_Wd2, L0_ffn_Wu2, L0_ffn_Wd3, L0_ffn_Wu3)
    return x

_drawn_inputs = setup_inputs


def setup_inputs(seed=0):
    import zlib

    import numpy as np

    out = dict(_drawn_inputs(seed))
    spreads = {'L0_attn_a_gamma': (1.0, 0.2),
     'L0_attn_b_bq': (0.0, 0.8),
     'L0_attn_b_bk': (0.0, 0.8),
     'L0_attn_b_bv': (0.0, 0.8),
     'L0_attn_b_bo': (0.0, 0.1),
     'L0_ffn_bp': (0.0, 0.8)}
    factors = {'L0_attn_a_lambda_q1': 8.0,
     'L0_attn_a_lambda_q2': 8.0,
     'L0_attn_a_lambda_k1': 8.0,
     'L0_attn_a_lambda_k2': 8.0,
     'L0_attn_b_Wq': 8.0,
     'L0_attn_b_Wk': 8.0,
     'L0_attn_b_Wv': 2.749,
     'L0_ffn_Wp': 2.907,
     'L0_ffn_sim': 2.767,
     'L0_ffn_Wd0': 4.291,
     'L0_ffn_Wu0': 3.719,
     'L0_ffn_Wd1': 5.04,
     'L0_ffn_Wu1': 5.19,
     'L0_ffn_Wd2': 5.623,
     'L0_ffn_Wu2': 6.193,
     'L0_ffn_Wd3': 8.0,
     'L0_ffn_Wu3': 8.0}
    for name, (base, spread) in spreads.items():
        noise = np.random.default_rng([zlib.crc32(name.encode()), seed]).standard_normal(out[name].shape)
        drawn = base * np.exp(spread * noise) if base else spread * noise
        out[name] = jnp.asarray(drawn.astype(out[name].dtype))
    for name, factor in factors.items():
        out[name] = (out[name] * factor).astype(out[name].dtype)
    return out
```

```python
from contextlib import ExitStack

import concourse.bass as bass
from concourse import mybir

F32 = mybir.dt.float32
BF16 = mybir.dt.bfloat16
ALU = mybir.AluOpType
ACT = mybir.ActivationFunctionType
X = mybir.AxisListType.X

P = 128
D = 128
BATCH = 2
T = 1024
NT = T // P
TILES = BATCH * NT
EPS = 1e-5
NEG = -1e30
BIG = 3e38
LAMBDA_INIT = 0.2

A_HD = 4
A_V = 8
GROUPS = 8
TERM_Q = (0, 0, 1, 0, 1, 2)
TERM_K = (0, 1, 0, 2, 1, 0)
M_ROW = len(TERM_Q) * A_HD

H = 16
C = 64
HID = H * C
JB = 4
CHUNKS = C // JB
POOL_HEADS = 5
P_RING = 4
EV_RING = 2

PROJ = 32
E = 4
R_PAD = 8
CLAMP_MAX = 4.605170185988092
FT = 4


class Count:

    def __init__(self, sem, per, first=0):
        self.sem, self.per, self.first, self.n = sem, per, first, 0

    def at(self, it, k):
        return it * self.per + (self.first + k)

    def next(self, it):
        self.n += 1
        return self.at(it, self.n)

    def check(self):
        assert self.n == self.per, (self.sem, self.n, self.per)


def phase_a1(nc, x_all, w, ident, rows_q, rows_k, v_nat, pw):
    S = TILES // FT
    with ExitStack() as ctx:
        sb = lambda n, s, d=F32: ctx.enter_context(nc.sbuf_tensor("a1_" + n, s, d))
        sem = lambda n, per: Count(ctx.enter_context(nc.semaphore("a1_" + n)), per)
        xn = sb("xn", [P, FT, D])
        sq = sb("sq", [P, FT, D])
        st = sb("st", [P, 4, FT])
        xnT = sb("xnT", [P, FT * P])
        res = sb("res", [P, FT * P])
        ps_t = ctx.enter_context(nc.psum_tensor("a1_ps_t", [P, FT * P], F32))
        ps = ctx.enter_context(nc.psum_tensor("a1_ps", [P, 3, FT * P], F32))
        dve_step = sem("dve_step", 19)
        rstd_ready = sem("rstd_ready", 1)
        xnT_psum = sem("xnT_psum", 1)
        xnT_ready = sem("xnT_ready", 1)
        qkv_psum = sem("qkv_psum", 3)
        block = ctx.enter_context(nc.Block())

        @block.vector
        def _(dve):
            with dve.Fori(0, S) as s:
                layernorm(nc, dve, dve_step, x_all[:, bass.ds(s * FT, FT), :], xn, sq, st, rstd_ready, s)
                for i, rows in enumerate((rows_q, rows_k)):
                    dve.wait_ge(qkv_psum.sem, qkv_psum.at(s, i + 1))
                    nc.vector.tensor_scalar(res[:], ps[:, i, :], 1.0 / A_HD if i == 0 else 1.0, None, ALU.mult).then_inc(dve_step.sem, 1)
                    dve.wait_ge(dve_step.sem, dve_step.next(s))
                    for part in range(3):
                        dst = rows[:, part, bass.ds(s * FT * P, FT * P)]
                        nc.vector.tensor_copy(dst, res[:]).then_inc(dve_step.sem, 1)
                        dve.wait_ge(dve_step.sem, dve_step.next(s))
                        if part < 2:
                            nc.vector.tensor_tensor(res[:], res[:], dst, ALU.subtract).then_inc(dve_step.sem, 1)
                            dve.wait_ge(dve_step.sem, dve_step.next(s))
                dve.wait_ge(qkv_psum.sem, qkv_psum.at(s, 3))
                nc.vector.tensor_copy(v_nat[:, bass.ds(s * FT, FT), :], ps[:, 2, :].rearrange("p (n d) -> p n d", n=FT)).then_inc(dve_step.sem, 1)
                dve.wait_ge(dve_step.sem, dve_step.next(s))
            dve_step.check()

        @block.gpsimd
        def _(pool):
            with pool.Fori(0, S) as s:
                pool.wait_ge(dve_step.sem, dve_step.at(s, 5))
                nc.gpsimd.tensor_tensor(st[:, 3, :], st[:, 2, :], pw[:, 0:FT], ALU.pow).then_inc(rstd_ready.sem, 1)

        @block.scalar
        def _(act):
            with act.Fori(0, S) as s:
                act.wait_ge(xnT_psum.sem, xnT_psum.at(s, 1))
                nc.scalar.copy(xnT[:], ps_t[:]).then_inc(xnT_ready.sem, 1)

        @block.tensor
        def _(pe):
            with pe.Fori(0, S) as s:
                pe.wait_ge(dve_step.sem, dve_step.at(s, 6))
                for n in range(FT):
                    last = nc.tensor.transpose(ps_t[:, n * P:(n + 1) * P], xn[:, n, :], ident[:])
                last.then_inc(xnT_psum.sem, 1)
                pe.wait_ge(xnT_ready.sem, xnT_ready.at(s, 1))
                for i in range(2):
                    nc.tensor.matmul(ps[:, i, :], w[:, i * D:(i + 1) * D], xnT[:], start=True, stop=True).then_inc(qkv_psum.sem, 1)
                for n in range(FT):
                    last = nc.tensor.matmul(ps[:, 2, n * P:(n + 1) * P], xnT[:, n * P:(n + 1) * P], w[:, 2 * D:3 * D],
                                            start=True, stop=True)
                last.then_inc(qkv_psum.sem, 1)


def layernorm(nc, dve, dve_step, x, xn, sq, st, rstd_ready, s):
    n = xn.shape[1]
    bc = lambda i: st[:, i, :].unsqueeze(2).broadcast_to([P, n, D])
    nc.vector.tensor_reduce(st[:, 0, :], x, X, ALU.add).then_inc(dve_step.sem, 1)
    dve.wait_ge(dve_step.sem, dve_step.next(s))
    nc.vector.scalar_tensor_tensor(xn[:], bc(0), -1.0 / D, x, ALU.mult, ALU.add).then_inc(dve_step.sem, 1)
    dve.wait_ge(dve_step.sem, dve_step.next(s))
    nc.vector.tensor_tensor(sq[:], xn[:], xn[:], ALU.mult).then_inc(dve_step.sem, 1)
    dve.wait_ge(dve_step.sem, dve_step.next(s))
    nc.vector.tensor_reduce(st[:, 1, :], sq[:], X, ALU.add).then_inc(dve_step.sem, 1)
    dve.wait_ge(dve_step.sem, dve_step.next(s))
    nc.vector.tensor_scalar(st[:, 2, :], st[:, 1, :], 1.0 / D, EPS, ALU.mult, ALU.add).then_inc(dve_step.sem, 1)
    dve.wait_ge(dve_step.sem, dve_step.next(s))
    dve.wait_ge(rstd_ready.sem, rstd_ready.at(s, 1))
    nc.vector.tensor_tensor(xn[:], xn[:], bc(3), ALU.mult).then_inc(dve_step.sem, 1)
    dve.wait_ge(dve_step.sem, dve_step.next(s))


def phase_a2(nc, rows_q, rows_k, v_nat, att, k):
    with ExitStack() as ctx:
        sb = lambda n, s, d=F32: ctx.enter_context(nc.sbuf_tensor("a2_" + n, s, d))
        sem = lambda n, per, first=0: Count(ctx.enter_context(nc.semaphore("a2_" + n)), per, first)
        rq = sb("rq", [P, T], BF16)
        rk = sb("rk", [P, T], BF16)
        v1 = sb("v1", [P, NT, 2, 32])
        negm = sb("negm", [P, NT, 4])
        mrows = sb("mrows", [P, NT, P], BF16)
        ex = sb("ex", [P, 4, T])
        o_sb = sb("o_sb", [P, T])
        rd = sb("rd", [P, NT, 4])
        oh = sb("oh", [P, NT, 4, A_V])
        ps = ctx.enter_context(nc.psum_tensor("a2_ps", [P, 8, 512], F32))
        ready = sem("ready", 2)
        dve_step = sem("dve_step", 12, 1)
        rows_psum = sem("rows_psum", 3)
        rows_sb = sem("rows_sb", 3)
        units = [(t, (0, 1, 2, 3)) for t in range(4)] + [(t, hh) for t in range(4, NT) for hh in ((0, 1), (2, 3))]
        sc_psum = sem("sc_psum", len(units))
        max_done = sem("max_done", len(units))
        steps = [(sbk, hh) for sbk in range(NT) for hh in range(4)]
        st_psum = sem("st_psum", len(steps))
        exp_done = sem("exp_done", len(steps))
        av_done = sem("av_done", len(steps), 1)
        o_copied = sem("o_copied", 1)
        oT_psum = sem("oT_psum", 1)
        v1_ready = sem("v1_ready", 1)
        block = ctx.enter_context(nc.Block())

        def base(u):
            return 4 * (u % 2)

        @block.gpsimd
        def _(pool):
            nc.gpsimd.memset(mrows[:], 0.0).then_inc(ready.sem, 1)
            nc.gpsimd.memset(v1[:, :, :, A_V + 1:], 0.0)
            nc.gpsimd.memset(v1[:, :, :, 0:A_V], 0.0)
            nc.gpsimd.memset(v1[:, :, :, A_V:A_V + 1], 1.0).then_inc(ready.sem, 1)

        @block.tensor
        def _(pe):
            pe.wait_ge(ready.sem, 2)
            pe.sem_inc(av_done.sem, 1)
            with pe.Fori(0, BATCH) as b, pe.Fori(0, GROUPS) as g:
                it = b * GROUPS + g

                def spread(sel, rows, bank, stop):
                    for half in range(2):
                        for part in range(3):
                            last = nc.tensor.matmul(ps[:, bank + half, :], sel[:, part, bass.ds(g * P, P)],
                                                    rows[:, part, bass.ds(b * T + half * 512, 512)],
                                                    start=part == 0, stop=stop and part == 2)
                    return last

                pe.wait_ge(dve_step.sem, dve_step.at(it, 0))
                spread(k["sel_q"], rows_q, 0, True).then_inc(rows_psum.sem, 1)
                spread(k["sel_k"], rows_k, 2, True).then_inc(rows_psum.sem, 1)
                pe.wait_ge(rows_sb.sem, rows_sb.at(it, 2))
                for u, (t, heads) in enumerate(units):
                    if u >= 2:
                        pe.wait_ge(max_done.sem, max_done.at(it, u - 1))
                    n = (t + 1) * P
                    for i, hh in enumerate(heads):
                        r = slice(32 * hh, 32 * hh + 32)
                        bank = base(u) + i * (4 // len(heads))
                        for c in range(0, n, 512):
                            w = min(512, n - c)
                            nc.tensor.matmul(ps[:, bank + c // 512, 0:w], rq[r, t * P:(t + 1) * P], rk[r, c:c + w],
                                             start=True, stop=c + w < n)
                        c = t * P
                        last = nc.tensor.matmul(ps[:, bank + c // 512, c % 512:c % 512 + P], k["ident_b"][:], k["mask"][:],
                                                start=False, stop=True)
                    last.then_inc(sc_psum.sem, 1)
                pe.wait_ge(dve_step.sem, dve_step.at(it, 5))
                spread(k["sel_q"], rows_q, 0, False)
                for t in range(NT):
                    last = nc.tensor.matmul(ps[:, t // 4, t % 4 * P:(t % 4 + 1) * P], mrows[:, t, :], k["ident_b"][:],
                                            start=False, stop=t % 4 == 3)
                last.then_inc(rows_psum.sem, 1)
                pe.wait_ge(rows_sb.sem, rows_sb.at(it, 3))
                pe.wait_ge(v1_ready.sem, v1_ready.at(it, 1))
                LAG = 3

                def values(n):
                    sbk, hh = steps[n]
                    pe.wait_ge(exp_done.sem, exp_done.at(it, n + 1))
                    t0 = sbk * P
                    for lo, hi in ((0, 512), (512, T)):
                        lo = max(lo, t0)
                        if lo < hi:
                            last = nc.tensor.matmul(ps[32 * hh:32 * hh + 32, 6 + lo // 512, lo % 512:(hi - 1) % 512 + 1],
                                                    v1[:, sbk, hh // 2, :], ex[:, n % 4, lo - t0:hi - t0],
                                                    start=sbk == 0, stop=sbk == (3 if hi == 512 else NT - 1))
                    last.then_inc(av_done.sem, 1)

                for n, (sbk, hh) in enumerate(steps):
                    if n >= 3:
                        pe.wait_ge(exp_done.sem, exp_done.at(it, n - 2))
                    r = slice(32 * hh, 32 * hh + 32)
                    width = T - sbk * P
                    bank = 2 * (n % 3)
                    for c in range(0, width, 512):
                        w = min(512, width - c)
                        last = nc.tensor.matmul(ps[:, bank + c // 512, 0:w], rk[r, sbk * P:(sbk + 1) * P],
                                                rq[r, sbk * P + c:sbk * P + c + w], start=True, stop=c > 0)
                        if c == 0:
                            last = nc.tensor.matmul(ps[:, bank, 0:P], k["ident_b"][:], k["mask_t"][:], start=False, stop=True)
                    last.then_inc(st_psum.sem, 1)
                    if n >= LAG:
                        values(n - LAG)
                for n in range(len(steps) - LAG, len(steps)):
                    values(n)
                pe.wait_ge(o_copied.sem, o_copied.at(it, 1))
                for t in range(NT):
                    last = nc.tensor.transpose(ps[:, t // 4, t % 4 * P:(t % 4 + 1) * P], o_sb[:, t * P:(t + 1) * P], k["ident"][:])
                last.then_inc(oT_psum.sem, 1)

        @block.scalar
        def _(act):
            with act.Fori(0, BATCH) as b, act.Fori(0, GROUPS) as g:
                it = b * GROUPS + g
                flat = lambda lo: ps[:, lo:lo + 2, :].rearrange("p a b -> p (a b)")
                act.wait_ge(rows_psum.sem, rows_psum.at(it, 1))
                nc.scalar.copy(rq[:], flat(0)).then_inc(rows_sb.sem, 1)
                act.wait_ge(rows_psum.sem, rows_psum.at(it, 2))
                nc.scalar.activation(rk[:], flat(2), ACT.Identity, bias=k["one_rows"][:]).then_inc(rows_sb.sem, 1)
                act.wait_ge(rows_psum.sem, rows_psum.at(it, 3))
                nc.scalar.copy(rq[:], flat(0)).then_inc(rows_sb.sem, 1)
                for n, (sbk, hh) in enumerate(steps):
                    act.wait_ge(st_psum.sem, st_psum.at(it, n + 1))
                    if n >= 4:
                        act.wait_ge(av_done.sem, av_done.at(it, n - 3))
                    width = T - sbk * P
                    nc.scalar.activation(ex[:, n % 4, 0:width], flat(2 * (n % 3))[:, 0:width], ACT.Exp).then_inc(exp_done.sem, 1)
                act.wait_ge(av_done.sem, av_done.at(it, len(steps)))
                nc.scalar.copy(o_sb[:], flat(6)).then_inc(o_copied.sem, 1)

        @block.vector
        def _(dve):
            dve.wait_ge(ready.sem, 2)
            dve.sem_inc(dve_step.sem, 1)
            with dve.Fori(0, BATCH) as b, dve.Fori(0, GROUPS) as g:
                it = b * GROUPS + g
                dve.wait_ge(av_done.sem, av_done.at(it, 0))
                nc.vector.tensor_copy(
                    v1[:, :, :, 0:A_V],
                    v_nat[:, bass.ds(b * NT, NT), bass.ds(g * 2 * A_V, 2 * A_V)].rearrange("p n (v c) -> p n v c", v=2)).then_inc(v1_ready.sem, 1)
                for u, (t, heads) in enumerate(units):
                    dve.wait_ge(sc_psum.sem, sc_psum.at(it, u + 1))
                    n = (t + 1) * P
                    src = ps[:, base(u):base(u) + 4, :].rearrange("p (h a) c -> p h (a c)", h=len(heads))[:, :, 0:n]
                    nc.vector.tensor_reduce(negm[:, t, heads[0]:heads[-1] + 1], src, X, ALU.max, negate=True).then_inc(max_done.sem, 1)
                dve.wait_ge(max_done.sem, max_done.at(it, len(units)))
                for part in range(3):
                    dst = mrows[:].rearrange("p n (h r) -> p n h r", h=4)[:, :, :, M_ROW + part]
                    nc.vector.tensor_copy(dst, negm[:]).then_inc(dve_step.sem, 1)
                    dve.wait_ge(dve_step.sem, dve_step.next(it))
                    if part < 2:
                        nc.vector.tensor_tensor(negm[:], negm[:], dst, ALU.subtract).then_inc(dve_step.sem, 1)
                        dve.wait_ge(dve_step.sem, dve_step.next(it))
                dve.wait_ge(oT_psum.sem, oT_psum.at(it, 1))
                o4 = ps[:, 0:2, :].rearrange("p a (n h c) -> p (a n) h c", n=4, h=4)
                nc.vector.reciprocal(rd[:], o4[:, :, :, A_V]).then_inc(dve_step.sem, 1)
                dve.wait_ge(dve_step.sem, dve_step.next(it))
                sub1 = rd[:].rearrange("p n (v s) -> p n v s", s=2)[:, :, :, 1]
                nc.vector.tensor_scalar(sub1, sub1, k["lam"][:], None, ALU.mult).then_inc(dve_step.sem, 1)
                dve.wait_ge(dve_step.sem, dve_step.next(it))
                for n in range(0, NT, 2):
                    nc.vector.tensor_tensor(oh[:, n:n + 2], o4[:, n:n + 2, :, 0:A_V],
                                            rd[:, n:n + 2].unsqueeze(3).broadcast_to([P, 2, 4, A_V]), ALU.mult).then_inc(dve_step.sem, 1)
                    dve.wait_ge(dve_step.sem, dve_step.next(it))
                oh5 = oh[:].rearrange("p n (v s) c -> p n v s c", s=2)
                dst = att[:, bass.ds(b * NT, NT), bass.ds(g * 2 * A_V, 2 * A_V)].rearrange("p n (v c) -> p n v c", v=2)
                nc.vector.tensor_tensor(dst, oh5[:, :, :, 0, :], oh5[:, :, :, 1, :], ALU.subtract).then_inc(dve_step.sem, 1)
                dve.wait_ge(dve_step.sem, dve_step.next(it))
            dve_step.check()


def phase_a3(nc, x_all, att, w_proj, ident, gamma8, pw):
    S = TILES // FT
    HV = D // A_V
    with ExitStack() as ctx:
        sb = lambda n, s, d=F32: ctx.enter_context(nc.sbuf_tensor("a3_" + n, s, d))
        sem = lambda n, per: Count(ctx.enter_context(nc.semaphore("a3_" + n)), per)
        sq = sb("sq", [P, FT * HV, A_V])
        ms = sb("ms", [P, 3, FT * HV])
        nrm = sb("nrm", [P, FT * HV, A_V])
        nT = sb("nT", [P, FT * P])
        ps_t = ctx.enter_context(nc.psum_tensor("a3_ps_t", [P, FT * P], F32))
        ps_o = ctx.enter_context(nc.psum_tensor("a3_ps_o", [P, FT, D], F32))
        dve_step = sem("dve_step", 6)
        rms_ready = sem("rms_ready", 1)
        nT_psum = sem("nT_psum", 1)
        nT_ready = sem("nT_ready", 1)
        o_psum = sem("o_psum", 1)
        block = ctx.enter_context(nc.Block())

        @block.vector
        def _(dve):
            with dve.Fori(0, S) as s:
                a = att[:, bass.ds(s * FT, FT), :].rearrange("p n (h c) -> p (n h) c", c=A_V)
                nc.vector.tensor_tensor(sq[:], a, a, ALU.mult).then_inc(dve_step.sem, 1)
                dve.wait_ge(dve_step.sem, dve_step.next(s))
                nc.vector.tensor_reduce(ms[:, 0, :], sq[:], X, ALU.add).then_inc(dve_step.sem, 1)
                dve.wait_ge(dve_step.sem, dve_step.next(s))
                nc.vector.tensor_scalar(ms[:, 1, :], ms[:, 0, :], 1.0 / A_V, EPS, ALU.mult, ALU.add).then_inc(dve_step.sem, 1)
                dve.wait_ge(dve_step.sem, dve_step.next(s))
                dve.wait_ge(rms_ready.sem, rms_ready.at(s, 1))
                nc.vector.tensor_tensor(nrm[:], a, ms[:, 2, :].unsqueeze(2).broadcast_to([P, FT * HV, A_V]), ALU.mult).then_inc(dve_step.sem, 1)
                dve.wait_ge(dve_step.sem, dve_step.next(s))
                nc.vector.tensor_tensor(nrm[:], nrm[:], gamma8[:].unsqueeze(1).broadcast_to([P, FT * HV, A_V]), ALU.mult).then_inc(dve_step.sem, 1)
                dve.wait_ge(dve_step.sem, dve_step.next(s))
                dve.wait_ge(o_psum.sem, o_psum.at(s, 1))
                xs = x_all[:, bass.ds(s * FT, FT), :]
                nc.vector.tensor_tensor(xs, ps_o[:], xs, ALU.add).then_inc(dve_step.sem, 1)
                dve.wait_ge(dve_step.sem, dve_step.next(s))
            dve_step.check()

        @block.gpsimd
        def _(pool):
            with pool.Fori(0, S) as s:
                pool.wait_ge(dve_step.sem, dve_step.at(s, 3))
                nc.gpsimd.tensor_tensor(ms[:, 2, :], ms[:, 1, :], pw[:, 0:FT * HV], ALU.pow).then_inc(rms_ready.sem, 1)

        @block.scalar
        def _(act):
            with act.Fori(0, S) as s:
                act.wait_ge(nT_psum.sem, nT_psum.at(s, 1))
                nc.scalar.copy(nT[:], ps_t[:]).then_inc(nT_ready.sem, 1)

        @block.tensor
        def _(pe):
            with pe.Fori(0, S) as s:
                pe.wait_ge(dve_step.sem, dve_step.at(s, 5))
                for n in range(FT):
                    last = nc.tensor.transpose(ps_t[:, n * P:(n + 1) * P],
                                               nrm[:, n * HV:(n + 1) * HV, :].rearrange("p h c -> p (h c)"), ident[:])
                last.then_inc(nT_psum.sem, 1)
                pe.wait_ge(nT_ready.sem, nT_ready.at(s, 1))
                for n in range(FT):
                    last = nc.tensor.matmul(ps_o[:, n, :], nT[:, n * P:(n + 1) * P], w_proj[:], start=True, stop=True)
                last.then_inc(o_psum.sem, 1)


def phase_f(nc, tag, x_all, k, out_dram):
    S = TILES // FT
    with ExitStack() as ctx:
        sb = lambda n, s, d=F32: ctx.enter_context(nc.sbuf_tensor(f"{tag}_{n}", s, d))
        sem = lambda n, per: Count(ctx.enter_context(nc.semaphore(f"{tag}_{n}")), per)
        xn = sb("xn", [P, FT, D])
        sq = sb("sq", [P, FT, D])
        st = sb("st", [P, 4, FT])
        xnT = sb("xnT", [P, FT * P])
        pr = sb("pr", [PROJ, 2, FT * P])
        lg = sb("lg", [P, FT, 8])
        g = sb("g", [P, 6, FT, E])
        r1 = sb("r1", [P, 8, FT])
        down = sb("down", [P, FT, E, R_PAD])
        downT = sb("downT", [E * R_PAD, FT * P])
        psum = lambda n, s: ctx.enter_context(nc.psum_tensor(f"{tag}_{n}", s, F32))
        ps_t = psum("ps_t", [P, FT * P])
        ps_p = psum("ps_p", [PROJ, FT * P])
        ps_l = psum("ps_l", [P, FT, 8])
        ps_d = psum("ps_d", [P, FT, E * R_PAD])
        ps_dT = psum("ps_dT", [E * R_PAD, FT * P])
        ps_o = psum("ps_o", [P, FT, D])
        dve_step = sem("dve_step", 25)
        rstd_ready = sem("rstd_ready", 2)
        xnT_psum = sem("xnT_psum", 1)
        xnT_ready = sem("xnT_ready", 1)
        p_psum = sem("p_psum", 1)
        l_psum = sem("l_psum", 1)
        exp_done = sem("exp_done", 1)
        dT_psum = sem("dT_psum", 1)
        dT_ready = sem("dT_ready", 1)
        o_psum = sem("o_psum", 1)
        stored = ctx.enter_context(nc.semaphore(f"{tag}_stored"))
        block = ctx.enter_context(nc.Block())

        @block.vector
        def _(dve):
            with dve.Fori(0, S) as s:
                xs = x_all[:, bass.ds(s * FT, FT), :]
                row = lambda i: r1[:, i, :]
                bc = lambda i: r1[:, i, :].unsqueeze(2).broadcast_to([P, FT, E])
                layernorm(nc, dve, dve_step, xs, xn, sq, st, rstd_ready, s)
                dve.wait_ge(p_psum.sem, p_psum.at(s, 1))
                nc.vector.tensor_scalar(pr[:, 0, :], ps_p[:], k["bp"][:], None, ALU.add).then_inc(dve_step.sem, 1)
                dve.wait_ge(dve_step.sem, dve_step.next(s))
                nc.vector.tensor_tensor(pr[:, 1, :], pr[:, 0, :], pr[:, 0, :], ALU.mult).then_inc(dve_step.sem, 1)
                dve.wait_ge(dve_step.sem, dve_step.next(s))
                dve.wait_ge(l_psum.sem, l_psum.at(s, 1))
                nc.vector.tensor_copy(lg[:, :, 0:E + 1], ps_l[:, :, 0:E + 1]).then_inc(dve_step.sem, 1)
                dve.wait_ge(dve_step.sem, dve_step.next(s))
                dve.wait_ge(rstd_ready.sem, rstd_ready.at(s, 2))
                nc.vector.tensor_scalar(row(0), row(7), 1e-12, None, ALU.max).then_inc(dve_step.sem, 1)
                dve.wait_ge(dve_step.sem, dve_step.next(s))
                nc.vector.reciprocal(row(1), row(0)).then_inc(dve_step.sem, 1)
                dve.wait_ge(dve_step.sem, dve_step.next(s))
                nc.vector.tensor_tensor(g[:, 0], lg[:, :, 0:E], bc(1), ALU.mult).then_inc(dve_step.sem, 1)
                dve.wait_ge(dve_step.sem, dve_step.next(s))
                nc.vector.tensor_reduce(row(2), g[:, 0], X, ALU.max).then_inc(dve_step.sem, 1)
                dve.wait_ge(dve_step.sem, dve_step.next(s))
                nc.vector.tensor_tensor(g[:, 1], g[:, 0], bc(2), ALU.subtract).then_inc(dve_step.sem, 1)
                dve.wait_ge(dve_step.sem, dve_step.next(s))
                dve.wait_ge(exp_done.sem, exp_done.at(s, 1))
                nc.vector.tensor_reduce(row(3), g[:, 2], X, ALU.add).then_inc(dve_step.sem, 1)
                dve.wait_ge(dve_step.sem, dve_step.next(s))
                nc.vector.reciprocal(row(4), row(3)).then_inc(dve_step.sem, 1)
                dve.wait_ge(dve_step.sem, dve_step.next(s))
                nc.vector.tensor_tensor(g[:, 3], g[:, 2], bc(4), ALU.mult).then_inc(dve_step.sem, 1)
                dve.wait_ge(dve_step.sem, dve_step.next(s))
                nc.vector.tensor_reduce(row(5), g[:, 3], X, ALU.max).then_inc(dve_step.sem, 1)
                dve.wait_ge(dve_step.sem, dve_step.next(s))
                nc.vector.tensor_tensor(g[:, 4], g[:, 3], bc(5), ALU.is_equal).then_inc(dve_step.sem, 1)
                dve.wait_ge(dve_step.sem, dve_step.next(s))
                nc.vector.tensor_tensor(g[:, 5], g[:, 4], k["rank4"][:].unsqueeze(1).broadcast_to([P, FT, E]), ALU.mult).then_inc(dve_step.sem, 1)
                dve.wait_ge(dve_step.sem, dve_step.next(s))
                nc.vector.tensor_reduce(row(6), g[:, 5], X, ALU.max).then_inc(dve_step.sem, 1)
                dve.wait_ge(dve_step.sem, dve_step.next(s))
                nc.vector.tensor_tensor(g[:, 4], g[:, 5], bc(6), ALU.is_equal).then_inc(dve_step.sem, 1)
                dve.wait_ge(dve_step.sem, dve_step.next(s))
                nc.vector.tensor_tensor(g[:, 5], g[:, 4], g[:, 3], ALU.mult).then_inc(dve_step.sem, 1)
                dve.wait_ge(dve_step.sem, dve_step.next(s))
                nc.vector.tensor_tensor(down[:].rearrange("p n e r -> p (n e) r"),
                                        ps_d[:].rearrange("p n (e r) -> p (n e) r", e=E),
                                        g[:, 5].rearrange("p n e -> p (n e)").unsqueeze(2)
                                        .broadcast_to([P, FT * E, R_PAD]), ALU.mult).then_inc(dve_step.sem, 1)
                dve.wait_ge(dve_step.sem, dve_step.next(s))
                dve.wait_ge(o_psum.sem, o_psum.at(s, 1))
                nc.vector.tensor_tensor(xs, ps_o[:], xs, ALU.add).then_inc(dve_step.sem, 1)
                dve.wait_ge(dve_step.sem, dve_step.next(s))
            dve_step.check()

        @block.gpsimd
        def _(pool):
            with pool.Fori(0, S) as s:
                pool.wait_ge(dve_step.sem, dve_step.at(s, 5))
                nc.gpsimd.tensor_tensor(st[:, 3, :], st[:, 2, :], k["pw"][:, 0:FT], ALU.pow).then_inc(rstd_ready.sem, 1)
                pool.wait_ge(dve_step.sem, dve_step.at(s, 9))
                nc.gpsimd.tensor_tensor(r1[:, 7, :], lg[:, :, E], k["ph"][:, 0:FT], ALU.pow).then_inc(rstd_ready.sem, 1)

        @block.scalar
        def _(act):
            with act.Fori(0, S) as s:
                act.wait_ge(xnT_psum.sem, xnT_psum.at(s, 1))
                nc.scalar.copy(xnT[:], ps_t[:]).then_inc(xnT_ready.sem, 1)
                act.wait_ge(dve_step.sem, dve_step.at(s, 14))
                nc.scalar.activation(g[:, 2], g[:, 1], ACT.Exp).then_inc(exp_done.sem, 1)
                act.wait_ge(dT_psum.sem, dT_psum.at(s, 1))
                nc.scalar.copy(downT[:], ps_dT[:]).then_inc(dT_ready.sem, 1)

        @block.tensor
        def _(pe):
            with pe.Fori(0, S) as s:
                tile = lambda n: slice(n * P, (n + 1) * P)
                pe.wait_ge(dve_step.sem, dve_step.at(s, 6))
                for n in range(FT):
                    last = nc.tensor.transpose(ps_t[:, tile(n)], xn[:, n, :], k["ident"][:])
                last.then_inc(xnT_psum.sem, 1)
                pe.wait_ge(xnT_ready.sem, xnT_ready.at(s, 1))
                nc.tensor.matmul(ps_p[:], k["wpT"][:], xnT[:], start=True, stop=True).then_inc(p_psum.sem, 1)
                for n in range(FT):
                    nc.tensor.matmul(ps_d[:, n, :], xnT[:, tile(n)], k["wdT"][:], start=True, stop=True)
                pe.wait_ge(dve_step.sem, dve_step.at(s, 8))
                for n in range(FT):
                    nc.tensor.matmul(ps_l[:, n, 0:E], pr[:, 0, tile(n)], k["simn"][:], start=True, stop=True)
                    last = nc.tensor.matmul(ps_l[:, n, E:E + 1], pr[:, 1, tile(n)], k["ones32"][:, 0:1], start=True, stop=True)
                last.then_inc(l_psum.sem, 1)
                pe.wait_ge(dve_step.sem, dve_step.at(s, 24))
                for n in range(FT):
                    last = nc.tensor.transpose(ps_dT[:, tile(n)], down[:, n].rearrange("p e r -> p (e r)"), k["ident"][:])
                last.then_inc(dT_psum.sem, 1)
                pe.wait_ge(dT_ready.sem, dT_ready.at(s, 1))
                for n in range(FT):
                    nc.tensor.matmul(ps_o[:, n, :], xnT[:, tile(n)], k["wT"][:], start=True, stop=False)
                    last = nc.tensor.matmul(ps_o[:, n, :], downT[:, tile(n)], k["wu"][:], start=False, stop=True)
                last.then_inc(o_psum.sem, 1)

        if out_dram is not None:
            @block.sync
            def _(sp):
                for s in range(S):
                    sp.wait_ge(dve_step.sem, (s + 1) * dve_step.per)
                    sp.dma_start(out_dram[:, s * FT:(s + 1) * FT, :], x_all[:, s * FT:(s + 1) * FT, :]).then_inc(stored, 16)
                sp.wait_ge(stored, 16 * S)


def phase_b(nc, x_all, k):
    with ExitStack() as ctx:
        sb = lambda n, s, d=F32: ctx.enter_context(nc.sbuf_tensor("b_" + n, s, d))
        sem = lambda n, per: Count(ctx.enter_context(nc.semaphore("b_" + n)), per)
        xn = sb("xn", [P, 1, D])
        sq = sb("sq", [P, 1, D])
        st = sb("st", [P, 4, 1])
        xnT = sb("xnT", [P, P])
        q = sb("q", [P, H, C])
        key = sb("key", [P, H, C])
        val = sb("val", [P, H, C])
        m = sb("m", [P, H, C])
        kmin = sb("kmin", [P, H, C])
        p_ring = sb("p_ring", [P, P_RING, H * JB * C])
        ev_ring = sb("ev_ring", [P, EV_RING, H * JB * C])
        atT = sb("atT", [P, HID])
        acc = ctx.enter_context(nc.psum_tensor("b_acc", [P, 4, H, C // 2], F32))
        stage = ctx.enter_context(nc.psum_tensor("b_stage", [P, 4, 512], F32))
        dve_step = sem("dve_step", 17)
        rstd_ready = sem("rstd_ready", 1)
        xnT_psum = sem("xnT_psum", 1)
        xnT_ready = sem("xnT_ready", 1)
        qkv_psum = sem("qkv_psum", 3)
        qkv_taken = sem("qkv_taken", 3)
        product = sem("product", 2 * CHUNKS)
        shifted = sem("shifted", CHUNKS)
        exp_done = sem("exp_done", CHUNKS)
        ev_dve = sem("ev_dve", CHUNKS)
        ev_pool = sem("ev_pool", CHUNKS)
        paired = sem("paired", 2 * CHUNKS)
        summed = sem("summed", CHUNKS)
        atT_psum = sem("atT_psum", 1)
        atT_ready = sem("atT_ready", 1)
        o_psum = sem("o_psum", 1)
        block = ctx.enter_context(nc.Block())
        DH = H - POOL_HEADS
        flat = lambda t: t[:].rearrange("p h c -> p (h c)")

        def chunk(ring, c):
            n = C - JB * c
            return ring[:, c % ring.shape[1], 0:H * JB * n].rearrange("p (h j i) -> p h j i", h=H, j=JB)

        def keys(t, c, h=slice(0, H)):
            n = C - JB * c
            return t[:, h, JB * c:JB * c + JB].unsqueeze(3).broadcast_to([P, t[:, h].shape[1], JB, n])

        def queries(t, c):
            n = C - JB * c
            return t[:, :, JB * c:C].unsqueeze(2).broadcast_to([P, H, JB, n])

        @block.vector
        def _(dve):
            with dve.Fori(0, TILES) as it:

                def multiply(c):
                    if c >= P_RING:
                        dve.wait_ge(summed.sem, summed.at(it, c - P_RING + 1))
                    pc = chunk(p_ring, c)
                    nc.vector.tensor_tensor(pc, queries(q, c), keys(key, c), ALU.mult).then_inc(product.sem, 1)
                    dve.wait_ge(product.sem, product.at(it, 2 * c + 1))
                    corner = pc[:, :, :, 0:JB]
                    nc.vector.tensor_tensor(corner, corner, k["corner"][:].unsqueeze(1).broadcast_to([P, H, JB, JB]),
                                            ALU.min).then_inc(product.sem, 1)

                layernorm(nc, dve, dve_step, x_all[:, bass.ds(it, 1), :], xn, sq, st, rstd_ready, it)
                for i, (dst, bias) in enumerate(((q, "bq8"), (key, "bk"), (val, "bv"))):
                    dve.wait_ge(qkv_psum.sem, qkv_psum.at(it, i + 1))
                    src = stage[:, 2 * (i % 2):2 * (i % 2) + 2, :].rearrange("p a b -> p (a b)")
                    nc.vector.scalar_tensor_tensor(flat(dst), src, 0.125 if i == 0 else 1.0, k[bias][:],
                                                   ALU.mult, ALU.add).then_inc(qkv_taken.sem, 1)
                dve.wait_ge(qkv_taken.sem, qkv_taken.at(it, 3))
                nc.vector.tensor_tensor_scan(flat(m), k["reset_max"][:], flat(key), 0.0, ALU.min, ALU.max).then_inc(dve_step.sem, 1)
                dve.wait_ge(dve_step.sem, dve_step.next(it))
                nc.vector.tensor_tensor_scan(flat(kmin), k["reset_min"][:], flat(key), 0.0, ALU.max, ALU.min).then_inc(dve_step.sem, 1)
                dve.wait_ge(dve_step.sem, dve_step.next(it))
                nc.vector.tensor_tensor(m[:], m[:], q[:], ALU.mult).then_inc(dve_step.sem, 1)
                dve.wait_ge(dve_step.sem, dve_step.next(it))
                nc.vector.tensor_tensor(kmin[:], kmin[:], q[:], ALU.mult).then_inc(dve_step.sem, 1)
                dve.wait_ge(dve_step.sem, dve_step.next(it))
                nc.vector.tensor_tensor(m[:], m[:], kmin[:], ALU.max).then_inc(dve_step.sem, 1)
                dve.wait_ge(dve_step.sem, dve_step.next(it))
                multiply(0)
                multiply(1)
                for c in range(CHUNKS):
                    if c + 2 < CHUNKS:
                        multiply(c + 2)
                    pc, ev = chunk(p_ring, c), chunk(ev_ring, c)
                    dve.wait_ge(exp_done.sem, exp_done.at(it, c + 1))
                    if c >= EV_RING:
                        dve.wait_ge(summed.sem, summed.at(it, c - EV_RING + 1))
                    nc.vector.tensor_tensor(ev[:, 0:DH], pc[:, 0:DH], keys(val, c, slice(0, DH)), ALU.mult).then_inc(ev_dve.sem, 1)
                    dve.wait_ge(ev_dve.sem, ev_dve.at(it, c + 1))
                    dve.wait_ge(ev_pool.sem, ev_pool.at(it, c + 1))
                    nc.vector.tensor_tensor(pc[:, :, 0:2], pc[:, :, 0:2], pc[:, :, 2:4], ALU.add).then_inc(paired.sem, 1)
                    nc.vector.tensor_tensor(ev[:, :, 0:2], ev[:, :, 0:2], ev[:, :, 2:4], ALU.add).then_inc(paired.sem, 1)
                dve.wait_ge(summed.sem, summed.at(it, CHUNKS))
                for half in range(2):
                    i0 = half * (C // 2)
                    nc.vector.reciprocal(kmin[:, :, i0:i0 + C // 2], acc[:, 2 + half]).then_inc(dve_step.sem, 1)
                    dve.wait_ge(dve_step.sem, dve_step.next(it))
                for half in range(2):
                    i0 = half * (C // 2)
                    nc.vector.tensor_tensor(m[:, :, i0:i0 + C // 2], acc[:, half], kmin[:, :, i0:i0 + C // 2], ALU.mult).then_inc(dve_step.sem, 1)
                    dve.wait_ge(dve_step.sem, dve_step.next(it))
                dve.wait_ge(o_psum.sem, o_psum.at(it, 1))
                nc.vector.tensor_tensor(sq[:, 0, :], stage[:, 2, 0:D], k["bo"][:], ALU.add).then_inc(dve_step.sem, 1)
                dve.wait_ge(dve_step.sem, dve_step.next(it))
                xs = x_all[:, bass.ds(it, 1), :]
                nc.vector.tensor_tensor(xs, xs, sq[:], ALU.add).then_inc(dve_step.sem, 1)
                dve.wait_ge(dve_step.sem, dve_step.next(it))
            dve_step.check()

        @block.gpsimd
        def _(pool):
            with pool.Fori(0, TILES) as it:
                pool.wait_ge(dve_step.sem, dve_step.at(it, 5))
                nc.gpsimd.tensor_tensor(st[:, 3, :], st[:, 2, :], k["pw"][:, 0:1], ALU.pow).then_inc(rstd_ready.sem, 1)

                def shift(c):
                    pool.wait_ge(product.sem, product.at(it, 2 * c + 2))
                    pc = chunk(p_ring, c)
                    nc.gpsimd.tensor_tensor(pc, pc, queries(m, c), ALU.subtract).then_inc(shifted.sem, 1)

                shift(0)
                for c in range(CHUNKS):
                    if c + 1 < CHUNKS:
                        shift(c + 1)
                    pool.wait_ge(exp_done.sem, exp_done.at(it, c + 1))
                    if c >= EV_RING:
                        pool.wait_ge(summed.sem, summed.at(it, c - EV_RING + 1))
                    pc, ev = chunk(p_ring, c), chunk(ev_ring, c)
                    nc.gpsimd.tensor_tensor(ev[:, DH:H], pc[:, DH:H], keys(val, c, slice(DH, H)), ALU.mult).then_inc(ev_pool.sem, 1)

        @block.scalar
        def _(act):
            with act.Fori(0, TILES) as it:
                act.wait_ge(xnT_psum.sem, xnT_psum.at(it, 1))
                nc.scalar.copy(xnT[:], stage[:, 0, 0:P]).then_inc(xnT_ready.sem, 1)
                for c in range(CHUNKS):
                    act.wait_ge(shifted.sem, shifted.at(it, c + 1))
                    pc = p_ring[:, c % P_RING, 0:H * JB * (C - JB * c)]
                    nc.scalar.activation(pc, pc, ACT.Exp).then_inc(exp_done.sem, 1)
                act.wait_ge(atT_psum.sem, atT_psum.at(it, 1))
                nc.scalar.copy(atT[:], stage[:, 0:2, :].rearrange("p a b -> p (a b)")).then_inc(atT_ready.sem, 1)

        @block.tensor
        def _(pe):
            with pe.Fori(0, TILES) as it:
                pe.wait_ge(dve_step.sem, dve_step.at(it, 6))
                nc.tensor.transpose(stage[:, 0, 0:P], xn[:, 0, :], k["ident"][:]).then_inc(xnT_psum.sem, 1)
                pe.wait_ge(xnT_ready.sem, xnT_ready.at(it, 1))
                for i in range(3):
                    if i == 2:
                        pe.wait_ge(qkv_taken.sem, qkv_taken.at(it, 1))
                    for half in range(2):
                        last = nc.tensor.matmul(stage[:, 2 * (i % 2) + half, :], xnT[:],
                                                k["wqkv"][:, i, half * 512:(half + 1) * 512], start=True, stop=True)
                    last.then_inc(qkv_psum.sem, 1)
                for c in range(CHUNKS):
                    pe.wait_ge(paired.sem, paired.at(it, 2 * c + 2))
                    j0, n = JB * c, C - JB * c
                    for w, ring in enumerate((ev_ring, p_ring)):
                        src = chunk(ring, c)
                        for half in range(2):
                            lo, hi = max(j0, half * 32), half * 32 + 32
                            if lo >= hi:
                                continue
                            for j in range(2):
                                last = nc.tensor.matmul(acc[:, 2 * w + half, :, lo - 32 * half:], k["ident"][:],
                                                        src[:, :, j, lo - j0:hi - j0],
                                                        start=c == 0 and j == 0, stop=hi - j0 <= JB and j == 1)
                    last.then_inc(summed.sem, 1)
                pe.wait_ge(dve_step.sem, dve_step.at(it, 15))
                for i in range(HID // P):
                    last = nc.tensor.transpose(stage[:, i // 4, i % 4 * P:(i % 4 + 1) * P], flat(m)[:, i * P:(i + 1) * P],
                                               k["ident"][:])
                last.then_inc(atT_psum.sem, 1)
                pe.wait_ge(atT_ready.sem, atT_ready.at(it, 1))
                for i in range(HID // P):
                    last = nc.tensor.matmul(stage[:, 2, 0:D], atT[:, i * P:(i + 1) * P], k["wo"][:, i, :],
                                            start=i == 0, stop=i == HID // P - 1)
                last.then_inc(o_psum.sem, 1)


def build(nc, a, out):
    with ExitStack() as ctx:
        sb = lambda n, s, d=F32: ctx.enter_context(nc.sbuf_tensor(n, s, d))
        x_all = sb("x_all", [P, TILES, D])
        k = {}
        for name, shape, dt in (
            ("w_attn", [P, 3 * D], F32), ("w_proj", [P, D], F32), ("ident", [P, P], F32), ("ident_b", [P, P], BF16),
            ("mask", [P, P], BF16), ("mask_t", [P, P], BF16), ("sel_q", [P, 3, GROUPS * P], BF16),
            ("sel_k", [P, 3, GROUPS * P], BF16), ("one_rows", [P, 1], F32), ("lams", [P, 4, A_HD], F32),
            ("gamma", [P, A_V], F32), ("wT", [P, D], F32), ("wpT", [P, PROJ], F32), ("wdT", [P, E * R_PAD], F32),
            ("wu", [E * R_PAD, D], F32), ("bp", [PROJ, 1], F32), ("sim", [PROJ, E], F32), ("temp", [PROJ, 1], F32),
            ("rank4", [P, E], F32), ("wqkv", [P, 3, HID], F32), ("bq", [P, HID], F32), ("bk", [P, HID], F32),
            ("bv", [P, HID], F32), ("bo", [P, D], F32), ("wo", [P, HID // P, D], F32), ("corner", [P, JB, JB], F32),
            ("reset_max", [P, HID], F32), ("reset_min", [P, HID], F32),
        ):
            k[name] = sb("k_" + name, shape, dt)
        loads = list(k)
        for name, shape in (("pw", [P, 64]), ("ph", [P, 64]), ("ones32", [PROJ, PROJ]), ("simn", [PROJ, E]), ("lam", [P, 1]),
                            ("bq8", [P, HID]), ("gamma8", [P, A_V]), ("tmp", [P, 4, A_HD])):
            k[name] = sb("k_" + name, shape)
        t32 = sb("t32", [PROJ, 6, E])
        loaded = ctx.enter_context(nc.semaphore("loaded"))
        filled = ctx.enter_context(nc.semaphore("filled"))
        dve_step = Count(ctx.enter_context(nc.semaphore("k_dve_step")), 0)
        act_step = Count(ctx.enter_context(nc.semaphore("k_act_step")), 0)
        pool_step = Count(ctx.enter_context(nc.semaphore("k_pool_step")), 0)
        norm_psum = ctx.enter_context(nc.semaphore("norm_psum"))

        with ExitStack() as ctx2:
            ps = ctx2.enter_context(nc.psum_tensor("k_ps", [PROJ, E], F32))
            block = ctx2.enter_context(nc.Block())
            n_loads = 16 * (len(loads) + 1)

            @block.sync
            def _(sp):
                sp.dma_start(x_all[:], a["x"]).then_inc(loaded, 16)
                for name in loads[0::2]:
                    sp.dma_start(k[name][:], a[name]).then_inc(loaded, 16)

            @block.scalar
            def _(act):
                for name in loads[1::2]:
                    act.dma_start(k[name][:], a[name]).then_inc(loaded, 16)
                act.wait_ge(dve_step.sem, dve_step.at(0, 2))
                nc.scalar.activation(k["lams"][:, 0, 0:2], k["lams"][:, 2, 0:2], ACT.Exp).then_inc(act_step.sem, 1)
                act.wait_ge(dve_step.sem, dve_step.at(0, 3))
                nc.scalar.activation(t32[:, 4, 1:2], t32[:, 4, 0:1], ACT.Exp).then_inc(act_step.sem, 1)

            @block.gpsimd
            def _(pool):
                nc.gpsimd.memset(k["pw"][:], -0.5).then_inc(filled, 1)
                nc.gpsimd.memset(k["ph"][:], 0.5).then_inc(filled, 1)
                nc.gpsimd.memset(k["ones32"][:], 1.0).then_inc(filled, 1)
                pool.wait_ge(filled, 3)
                pool.wait_ge(dve_step.sem, dve_step.at(0, 5))
                nc.gpsimd.tensor_tensor(t32[:, 2, :], t32[:, 1, :], k["ph"][0:PROJ, 0:E], ALU.pow).then_inc(pool_step.sem, 1)

            @block.tensor
            def _(pe):
                pe.wait_ge(filled, 3)
                pe.wait_ge(dve_step.sem, dve_step.at(0, 4))
                nc.tensor.matmul(ps[:], k["ones32"][:], t32[:, 0, :], start=True, stop=True).then_inc(norm_psum, 1)

            @block.vector
            def _(dve):
                dve.wait_ge(loaded, n_loads)
                lams = k["lams"]
                nc.vector.tensor_tensor(k["tmp"][:, 0:2, :], lams[:, 0:4:2, :], lams[:, 1:4:2, :], ALU.mult).then_inc(dve_step.sem, 1)
                dve.wait_ge(dve_step.sem, dve_step.next(0))
                nc.vector.tensor_reduce(lams[:, 2, 0:2], k["tmp"][:, 0:2, :], X, ALU.add).then_inc(dve_step.sem, 1)
                dve.wait_ge(dve_step.sem, dve_step.next(0))
                nc.vector.tensor_scalar(t32[:, 4, 0:1], k["temp"][:], CLAMP_MAX, None, ALU.min).then_inc(dve_step.sem, 1)
                dve.wait_ge(dve_step.sem, dve_step.next(0))
                nc.vector.tensor_tensor(t32[:, 0, :], k["sim"][:], k["sim"][:], ALU.mult).then_inc(dve_step.sem, 1)
                dve.wait_ge(dve_step.sem, dve_step.next(0))
                dve.wait_ge(norm_psum, 1)
                nc.vector.tensor_copy(t32[:, 1, :], ps[:]).then_inc(dve_step.sem, 1)
                dve.wait_ge(dve_step.sem, dve_step.next(0))
                dve.wait_ge(pool_step.sem, pool_step.at(0, 1))
                nc.vector.tensor_scalar(t32[:, 3, :], t32[:, 2, :], 1e-12, None, ALU.max).then_inc(dve_step.sem, 1)
                dve.wait_ge(dve_step.sem, dve_step.next(0))
                nc.vector.reciprocal(t32[:, 5, :], t32[:, 3, :]).then_inc(dve_step.sem, 1)
                dve.wait_ge(dve_step.sem, dve_step.next(0))
                nc.vector.tensor_tensor(t32[:, 0, :], k["sim"][:], t32[:, 5, :], ALU.mult).then_inc(dve_step.sem, 1)
                dve.wait_ge(dve_step.sem, dve_step.next(0))
                dve.wait_ge(act_step.sem, act_step.at(0, 2))
                nc.vector.tensor_scalar(k["simn"][:], t32[:, 0, :], t32[:, 4, 1:2], None, ALU.mult).then_inc(dve_step.sem, 1)
                dve.wait_ge(dve_step.sem, dve_step.next(0))
                nc.vector.tensor_tensor(k["tmp"][:, 3, 0:1], lams[:, 0, 0:1], lams[:, 0, 1:2], ALU.subtract).then_inc(dve_step.sem, 1)
                dve.wait_ge(dve_step.sem, dve_step.next(0))
                nc.vector.tensor_scalar(k["lam"][:], k["tmp"][:, 3, 0:1], LAMBDA_INIT, None, ALU.add).then_inc(dve_step.sem, 1)
                dve.wait_ge(dve_step.sem, dve_step.next(0))
                nc.vector.tensor_scalar(k["bq8"][:], k["bq"][:], 0.125, None, ALU.mult).then_inc(dve_step.sem, 1)
                dve.wait_ge(dve_step.sem, dve_step.next(0))
                nc.vector.tensor_scalar(k["gamma8"][:], k["gamma"][:], 1.0 - LAMBDA_INIT, None, ALU.mult).then_inc(dve_step.sem, 1)
                dve.wait_ge(dve_step.sem, dve_step.next(0))

        with ExitStack() as ctx3:
            sb3 = lambda n, s, d=F32: ctx3.enter_context(nc.sbuf_tensor(n, s, d))
            rows_q = sb3("rows_q", [P, 3, BATCH * T], BF16)
            rows_k = sb3("rows_k", [P, 3, BATCH * T], BF16)
            v_nat = sb3("v_nat", [P, TILES, D])
            att = sb3("att", [P, TILES, D])
            phase_a1(nc, x_all, k["w_attn"], k["ident"], rows_q, rows_k, v_nat, k["pw"])
            phase_a2(nc, rows_q, rows_k, v_nat, att, k)
            phase_a3(nc, x_all, att, k["w_proj"], k["ident"], k["gamma8"], k["pw"])
        phase_f(nc, "f1", x_all, k, None)
        phase_b(nc, x_all, k)
        phase_f(nc, "f2", x_all, k, out)


def kernel(**inputs):
    import ml_dtypes
    import numpy as np
    import concourse.bacc as bacc
    from concourse.bass_utils import run_bass_kernel_spmd as run

    i = {n: np.asarray(v) for n, v in inputs.items()}
    A, B, F = "L0_attn_a_", "L0_attn_b_", "L0_ffn_"
    bf = ml_dtypes.bfloat16
    rows = lambda v, n=P: np.ascontiguousarray(np.broadcast_to(v, (n,) + v.shape))
    x = i[A + "x"]
    arrays = {
        "x": x, "w_attn": i[A + "w_attn"], "w_proj": i[A + "w_proj"],
        "lams": rows(np.stack([i[A + "lambda_q1"], i[A + "lambda_k1"], i[A + "lambda_q2"], i[A + "lambda_k2"]])),
        "gamma": rows(i[A + "gamma"]),
        "wT": i[F + "W"].T, "wpT": i[F + "Wp"].T, "bp": i[F + "bp"][:, None], "sim": i[F + "sim"],
        "temp": rows(i[F + "temp"], PROJ),
        "wqkv": np.stack([i[B + "Wq"], i[B + "Wk"], i[B + "Wv"]], 1),
        "bq": rows(i[B + "bq"]), "bk": rows(i[B + "bk"]), "bv": rows(i[B + "bv"]), "bo": rows(i[B + "bo"]),
        "wo": i[B + "Wo"].reshape(HID // P, P, D).transpose(1, 0, 2),
    }
    wd = np.zeros((E, R_PAD, D), np.float32)
    wu = np.zeros((E, R_PAD, D), np.float32)
    for e in range(E):
        d, u = i[F + f"Wd{e}"], i[F + f"Wu{e}"]
        wd[e, :d.shape[0]] = d
        wu[e, :u.shape[1]] = u.T
    arrays["wdT"] = wd.reshape(E * R_PAD, D).T
    arrays["wu"] = wu.reshape(E * R_PAD, D)
    arrays["ident"] = np.eye(P, dtype=np.float32)
    arrays["ident_b"] = np.eye(P, dtype=np.float32).astype(bf)
    later = np.triu(np.ones((P, P), np.float32), 1)
    arrays["mask"] = (NEG * later).astype(bf)
    arrays["mask_t"] = (NEG * later.T).astype(bf)
    for name, terms in (("sel_q", TERM_Q), ("sel_k", TERM_K)):
        sel = np.zeros((P, 3, GROUPS, 4, 32), np.float32)
        for g in range(GROUPS):
            for h in range(4):
                for t, part in enumerate(terms):
                    for d in range(A_HD):
                        sel[(4 * g + h) * A_HD + d, part, g, h, t * A_HD + d] = 1.0
        arrays[name] = sel.reshape(P, 3, GROUPS * P).astype(bf)
    one = np.zeros((4, 32, 1), np.float32)
    one[:, M_ROW:M_ROW + 3] = 1.0
    arrays["one_rows"] = one.reshape(P, 1)
    arrays["rank4"] = rows(np.arange(E, 0, -1).astype(np.float32))
    corner = np.full((JB, JB), BIG, np.float32)
    for j in range(JB):
        corner[j, :j] = -1e38
    arrays["corner"] = rows(corner)
    first = (np.arange(HID) % C == 0)
    arrays["reset_max"] = rows(np.where(first, -BIG, BIG).astype(np.float32))
    arrays["reset_min"] = rows(np.where(first, BIG, -BIG).astype(np.float32))

    nc = bacc.Bacc("TRN2", target_bir_lowering=False, num_devices=1)
    feeds, args = {}, {}
    for name, v in arrays.items():
        v = np.ascontiguousarray(v)
        feeds[f"in_{name}"] = v
        args[name] = nc.dram_tensor(f"in_{name}", v.shape, mybir.dt.from_np(v.dtype), kind="ExternalInput").ap()
    args["x"] = args["x"].rearrange("b (n p) d -> p (b n) d", p=P)
    out = nc.dram_tensor("out", x.shape, F32, kind="ExternalOutput").ap()
    build(nc, args, out.rearrange("b (n p) d -> p (b n) d", p=P))
    r = run(nc, [feeds], core_ids=[0])
    return r.results[0]["out"]
```

```python
from contextlib import ExitStack

import concourse.bass as bass
from concourse import mybir

F32 = mybir.dt.float32
BF16 = mybir.dt.bfloat16
ALU = mybir.AluOpType
ACT = mybir.ActivationFunctionType
X = mybir.AxisListType.X

P = 128
D = 128
BATCH = 2
T = 1024
NT = T // P
TILES = BATCH * NT
EPS = 1e-5
NEG = -1e30
BIG = 3e38
LAMBDA_INIT = 0.2

A_HD = 4
A_V = 8
GROUPS = 8
TERM_Q = (0, 0, 1, 0, 1, 2)
TERM_K = (0, 1, 0, 2, 1, 0)
M_ROW = len(TERM_Q) * A_HD

H = 16
C = 64
HID = H * C
JB = 2
CHUNKS = C // JB
POOL_HEADS = 5
ORDER = tuple(c for i in range(CHUNKS // 2) for c in (i, CHUNKS - 1 - i))
P_RING = 16
EV_RING = 4
MULTIPLY_AHEAD = 8
SHIFT_AHEAD = 5
FOLD_EV = tuple(range(CHUNKS))
FOLD_P = tuple(range(24, CHUNKS))
DIVIDE_AT, TURN_O_AT, COPY_O_AT, PROJECT_AT, RESIDUAL_AT = 1, 3, 6, 7, 9
NORM_AT, TURN_XN_AT, COPY_XN_AT = 6, 7, 10
QKV_AT = (10, 11, 14)
TAKE_AT = (13, 14, 17)
MAX_AT = (18, 19, 20)

PROJ = 32
E = 4
R_PAD = 8
CLAMP_MAX = 4.605170185988092
FT = 4


class Count:

    def __init__(self, sem, per, first=0):
        self.sem, self.per, self.first, self.n = sem, per, first, 0

    def at(self, it, k):
        return it * self.per + (self.first + k)

    def next(self, it):
        self.n += 1
        return self.at(it, self.n)

    def check(self):
        assert self.n == self.per, (self.sem, self.n, self.per)


def phase_a1(nc, x_all, w, ident, rows_q, rows_k, v_nat, pw):
    S = TILES // FT
    with ExitStack() as ctx:
        sb = lambda n, s, d=F32: ctx.enter_context(nc.sbuf_tensor("a1_" + n, s, d))
        sem = lambda n, per: Count(ctx.enter_context(nc.semaphore("a1_" + n)), per)
        xn = sb("xn", [P, FT, D])
        sq = sb("sq", [P, FT, D])
        st = sb("st", [P, 4, FT])
        xnT = sb("xnT", [P, FT * P])
        res = sb("res", [P, FT * P])
        ps_t = ctx.enter_context(nc.psum_tensor("a1_ps_t", [P, FT * P], F32))
        ps = ctx.enter_context(nc.psum_tensor("a1_ps", [P, 3, FT * P], F32))
        dve_step = sem("dve_step", 19)
        rstd_ready = sem("rstd_ready", 1)
        xnT_psum = sem("xnT_psum", 1)
        xnT_ready = sem("xnT_ready", 1)
        qkv_psum = sem("qkv_psum", 3)
        block = ctx.enter_context(nc.Block())

        @block.vector
        def _(dve):
            with dve.Fori(0, S) as s:
                layernorm(nc, dve, dve_step, x_all[:, bass.ds(s * FT, FT), :], xn, sq, st, rstd_ready, s)
                for i, rows in enumerate((rows_q, rows_k)):
                    dve.wait_ge(qkv_psum.sem, qkv_psum.at(s, i + 1))
                    nc.vector.tensor_scalar(res[:], ps[:, i, :], 1.0 / A_HD if i == 0 else 1.0, None, ALU.mult).then_inc(dve_step.sem, 1)
                    dve.wait_ge(dve_step.sem, dve_step.next(s))
                    for part in range(3):
                        dst = rows[:, part, bass.ds(s * FT * P, FT * P)]
                        nc.vector.tensor_copy(dst, res[:]).then_inc(dve_step.sem, 1)
                        dve.wait_ge(dve_step.sem, dve_step.next(s))
                        if part < 2:
                            nc.vector.tensor_tensor(res[:], res[:], dst, ALU.subtract).then_inc(dve_step.sem, 1)
                            dve.wait_ge(dve_step.sem, dve_step.next(s))
                dve.wait_ge(qkv_psum.sem, qkv_psum.at(s, 3))
                nc.vector.tensor_copy(v_nat[:, bass.ds(s * FT, FT), :], ps[:, 2, :].rearrange("p (n d) -> p n d", n=FT)).then_inc(dve_step.sem, 1)
                dve.wait_ge(dve_step.sem, dve_step.next(s))
            dve_step.check()

        @block.gpsimd
        def _(pool):
            with pool.Fori(0, S) as s:
                pool.wait_ge(dve_step.sem, dve_step.at(s, 5))
                nc.gpsimd.tensor_tensor(st[:, 3, :], st[:, 2, :], pw[:, 0:FT], ALU.pow).then_inc(rstd_ready.sem, 1)

        @block.scalar
        def _(act):
            with act.Fori(0, S) as s:
                act.wait_ge(xnT_psum.sem, xnT_psum.at(s, 1))
                nc.scalar.copy(xnT[:], ps_t[:]).then_inc(xnT_ready.sem, 1)

        @block.tensor
        def _(pe):
            with pe.Fori(0, S) as s:
                pe.wait_ge(dve_step.sem, dve_step.at(s, 6))
                for n in range(FT):
                    last = nc.tensor.transpose(ps_t[:, n * P:(n + 1) * P], xn[:, n, :], ident[:])
                last.then_inc(xnT_psum.sem, 1)
                pe.wait_ge(xnT_ready.sem, xnT_ready.at(s, 1))
                for i in range(2):
                    nc.tensor.matmul(ps[:, i, :], w[:, i * D:(i + 1) * D], xnT[:], start=True, stop=True).then_inc(qkv_psum.sem, 1)
                for n in range(FT):
                    last = nc.tensor.matmul(ps[:, 2, n * P:(n + 1) * P], xnT[:, n * P:(n + 1) * P], w[:, 2 * D:3 * D],
                                            start=True, stop=True)
                last.then_inc(qkv_psum.sem, 1)


def layernorm(nc, dve, dve_step, x, xn, sq, st, rstd_ready, s):
    n = xn.shape[1]
    bc = lambda i: st[:, i, :].unsqueeze(2).broadcast_to([P, n, D])
    nc.vector.tensor_reduce(st[:, 0, :], x, X, ALU.add).then_inc(dve_step.sem, 1)
    dve.wait_ge(dve_step.sem, dve_step.next(s))
    nc.vector.scalar_tensor_tensor(xn[:], bc(0), -1.0 / D, x, ALU.mult, ALU.add).then_inc(dve_step.sem, 1)
    dve.wait_ge(dve_step.sem, dve_step.next(s))
    nc.vector.tensor_tensor(sq[:], xn[:], xn[:], ALU.mult).then_inc(dve_step.sem, 1)
    dve.wait_ge(dve_step.sem, dve_step.next(s))
    nc.vector.tensor_reduce(st[:, 1, :], sq[:], X, ALU.add).then_inc(dve_step.sem, 1)
    dve.wait_ge(dve_step.sem, dve_step.next(s))
    nc.vector.tensor_scalar(st[:, 2, :], st[:, 1, :], 1.0 / D, EPS, ALU.mult, ALU.add).then_inc(dve_step.sem, 1)
    dve.wait_ge(dve_step.sem, dve_step.next(s))
    dve.wait_ge(rstd_ready.sem, rstd_ready.at(s, 1))
    nc.vector.tensor_tensor(xn[:], xn[:], bc(3), ALU.mult).then_inc(dve_step.sem, 1)
    dve.wait_ge(dve_step.sem, dve_step.next(s))


def phase_a2(nc, rows_q, rows_k, v_nat, att, k):
    with ExitStack() as ctx:
        sb = lambda n, s, d=F32: ctx.enter_context(nc.sbuf_tensor("a2_" + n, s, d))
        sem = lambda n, per, first=0: Count(ctx.enter_context(nc.semaphore("a2_" + n)), per, first)
        rq = sb("rq", [P, T], BF16)
        rk = sb("rk", [P, T], BF16)
        v1 = sb("v1", [P, NT, 2, 32])
        negm = sb("negm", [P, NT, 4])
        mrows = sb("mrows", [P, NT, P], BF16)
        ex = sb("ex", [P, 4, T])
        o_sb = sb("o_sb", [P, T])
        rd = sb("rd", [P, NT, 4])
        oh = sb("oh", [P, NT, 4, A_V])
        ps = ctx.enter_context(nc.psum_tensor("a2_ps", [P, 8, 512], F32))
        ready = sem("ready", 2)
        bias_parts = sb("bias_parts", [1, 3, 3 * HID], BF16)
        bias_step = sem("bias_step", 5)
        bias_moved = ctx.enter_context(nc.semaphore("a2_bias_moved"))
        dve_step = sem("dve_step", 12, 1)
        rows_psum = sem("rows_psum", 3)
        rows_sb = sem("rows_sb", 3)
        units = [(t, (0, 1, 2, 3)) for t in range(4)] + [(t, hh) for t in range(4, NT) for hh in ((0, 1), (2, 3))]
        sc_psum = sem("sc_psum", len(units))
        max_done = sem("max_done", len(units))
        steps = [(sbk, hh) for sbk in range(NT) for hh in range(4)]
        st_psum = sem("st_psum", len(steps))
        exp_done = sem("exp_done", len(steps))
        av_done = sem("av_done", len(steps), 1)
        o_copied = sem("o_copied", 1)
        oT_psum = sem("oT_psum", 1)
        v1_ready = sem("v1_ready", 1)
        block = ctx.enter_context(nc.Block())

        def base(u):
            return 4 * (u % 2)

        @block.gpsimd
        def _(pool):
            nc.gpsimd.memset(mrows[:], 0.0).then_inc(ready.sem, 1)
            nc.gpsimd.memset(v1[:, :, :, A_V + 1:], 0.0)
            nc.gpsimd.memset(v1[:, :, :, 0:A_V], 0.0)
            nc.gpsimd.memset(v1[:, :, :, A_V:A_V + 1], 1.0).then_inc(ready.sem, 1)
            for part in range(3):
                nc.gpsimd.tensor_copy(bias_parts[:, part, :], k["bias"][:]).then_inc(bias_step.sem, 1)
                pool.wait_ge(bias_step.sem, bias_step.next(0))
                if part < 2:
                    nc.gpsimd.tensor_tensor(k["bias"][:], k["bias"][:], bias_parts[:, part, :],
                                            ALU.subtract).then_inc(bias_step.sem, 1)
                    pool.wait_ge(bias_step.sem, bias_step.next(0))

        @block.sync
        def _(sp):
            sp.wait_ge(bias_step.sem, 5)
            for part in range(3):
                sp.dma_start(k["bias3"][part:part + 1].rearrange("p i c -> p (i c)"), bias_parts[:, part, :]).then_inc(bias_moved, 16)
            sp.wait_ge(bias_moved, 48)

        @block.tensor
        def _(pe):
            pe.wait_ge(ready.sem, 2)
            pe.sem_inc(av_done.sem, 1)
            with pe.Fori(0, BATCH) as b, pe.Fori(0, GROUPS) as g:
                it = b * GROUPS + g

                def spread(sel, rows, bank, stop):
                    for half in range(2):
                        for part in range(3):
                            last = nc.tensor.matmul(ps[:, bank + half, :], sel[:, part, bass.ds(g * P, P)],
                                                    rows[:, part, bass.ds(b * T + half * 512, 512)],
                                                    start=part == 0, stop=stop and part == 2)
                    return last

                pe.wait_ge(dve_step.sem, dve_step.at(it, 0))
                spread(k["sel_q"], rows_q, 0, True).then_inc(rows_psum.sem, 1)
                spread(k["sel_k"], rows_k, 2, True).then_inc(rows_psum.sem, 1)
                pe.wait_ge(rows_sb.sem, rows_sb.at(it, 2))
                for u, (t, heads) in enumerate(units):
                    if u >= 2:
                        pe.wait_ge(max_done.sem, max_done.at(it, u - 1))
                    n = (t + 1) * P
                    for i, hh in enumerate(heads):
                        r = slice(32 * hh, 32 * hh + 32)
                        bank = base(u) + i * (4 // len(heads))
                        for c in range(0, n, 512):
                            w = min(512, n - c)
                            nc.tensor.matmul(ps[:, bank + c // 512, 0:w], rq[r, t * P:(t + 1) * P], rk[r, c:c + w],
                                             start=True, stop=c + w < n)
                        c = t * P
                        last = nc.tensor.matmul(ps[:, bank + c // 512, c % 512:c % 512 + P], k["ident_b"][:], k["mask"][:],
                                                start=False, stop=True)
                    last.then_inc(sc_psum.sem, 1)
                pe.wait_ge(dve_step.sem, dve_step.at(it, 5))
                spread(k["sel_q"], rows_q, 0, False)
                for t in range(NT):
                    last = nc.tensor.matmul(ps[:, t // 4, t % 4 * P:(t % 4 + 1) * P], mrows[:, t, :], k["ident_b"][:],
                                            start=False, stop=t % 4 == 3)
                last.then_inc(rows_psum.sem, 1)
                pe.wait_ge(rows_sb.sem, rows_sb.at(it, 3))
                pe.wait_ge(v1_ready.sem, v1_ready.at(it, 1))
                LAG = 3

                def values(n):
                    sbk, hh = steps[n]
                    pe.wait_ge(exp_done.sem, exp_done.at(it, n + 1))
                    t0 = sbk * P
                    for lo, hi in ((0, 512), (512, T)):
                        lo = max(lo, t0)
                        if lo < hi:
                            last = nc.tensor.matmul(ps[32 * hh:32 * hh + 32, 6 + lo // 512, lo % 512:(hi - 1) % 512 + 1],
                                                    v1[:, sbk, hh // 2, :], ex[:, n % 4, lo - t0:hi - t0],
                                                    start=sbk == 0, stop=sbk == (3 if hi == 512 else NT - 1))
                    last.then_inc(av_done.sem, 1)

                for n, (sbk, hh) in enumerate(steps):
                    if n >= 3:
                        pe.wait_ge(exp_done.sem, exp_done.at(it, n - 2))
                    r = slice(32 * hh, 32 * hh + 32)
                    width = T - sbk * P
                    bank = 2 * (n % 3)
                    for c in range(0, width, 512):
                        w = min(512, width - c)
                        last = nc.tensor.matmul(ps[:, bank + c // 512, 0:w], rk[r, sbk * P:(sbk + 1) * P],
                                                rq[r, sbk * P + c:sbk * P + c + w], start=True, stop=c > 0)
                        if c == 0:
                            last = nc.tensor.matmul(ps[:, bank, 0:P], k["ident_b"][:], k["mask_t"][:], start=False, stop=True)
                    last.then_inc(st_psum.sem, 1)
                    if n >= LAG:
                        values(n - LAG)
                for n in range(len(steps) - LAG, len(steps)):
                    values(n)
                pe.wait_ge(o_copied.sem, o_copied.at(it, 1))
                for t in range(NT):
                    last = nc.tensor.transpose(ps[:, t // 4, t % 4 * P:(t % 4 + 1) * P], o_sb[:, t * P:(t + 1) * P], k["ident"][:])
                last.then_inc(oT_psum.sem, 1)

        @block.scalar
        def _(act):
            with act.Fori(0, BATCH) as b, act.Fori(0, GROUPS) as g:
                it = b * GROUPS + g
                flat = lambda lo: ps[:, lo:lo + 2, :].rearrange("p a b -> p (a b)")
                act.wait_ge(rows_psum.sem, rows_psum.at(it, 1))
                nc.scalar.copy(rq[:], flat(0)).then_inc(rows_sb.sem, 1)
                act.wait_ge(rows_psum.sem, rows_psum.at(it, 2))
                nc.scalar.activation(rk[:], flat(2), ACT.Identity, bias=k["one_rows"][:]).then_inc(rows_sb.sem, 1)
                act.wait_ge(rows_psum.sem, rows_psum.at(it, 3))
                nc.scalar.copy(rq[:], flat(0)).then_inc(rows_sb.sem, 1)
                for n, (sbk, hh) in enumerate(steps):
                    act.wait_ge(st_psum.sem, st_psum.at(it, n + 1))
                    if n >= 4:
                        act.wait_ge(av_done.sem, av_done.at(it, n - 3))
                    width = T - sbk * P
                    nc.scalar.activation(ex[:, n % 4, 0:width], flat(2 * (n % 3))[:, 0:width], ACT.Exp).then_inc(exp_done.sem, 1)
                act.wait_ge(av_done.sem, av_done.at(it, len(steps)))
                nc.scalar.copy(o_sb[:], flat(6)).then_inc(o_copied.sem, 1)

        @block.vector
        def _(dve):
            dve.wait_ge(ready.sem, 2)
            dve.sem_inc(dve_step.sem, 1)
            with dve.Fori(0, BATCH) as b, dve.Fori(0, GROUPS) as g:
                it = b * GROUPS + g
                dve.wait_ge(av_done.sem, av_done.at(it, 0))
                nc.vector.tensor_copy(
                    v1[:, :, :, 0:A_V],
                    v_nat[:, bass.ds(b * NT, NT), bass.ds(g * 2 * A_V, 2 * A_V)].rearrange("p n (v c) -> p n v c", v=2)).then_inc(v1_ready.sem, 1)
                for u, (t, heads) in enumerate(units):
                    dve.wait_ge(sc_psum.sem, sc_psum.at(it, u + 1))
                    n = (t + 1) * P
                    src = ps[:, base(u):base(u) + 4, :].rearrange("p (h a) c -> p h (a c)", h=len(heads))[:, :, 0:n]
                    nc.vector.tensor_reduce(negm[:, t, heads[0]:heads[-1] + 1], src, X, ALU.max, negate=True).then_inc(max_done.sem, 1)
                dve.wait_ge(max_done.sem, max_done.at(it, len(units)))
                for part in range(3):
                    dst = mrows[:].rearrange("p n (h r) -> p n h r", h=4)[:, :, :, M_ROW + part]
                    nc.vector.tensor_copy(dst, negm[:]).then_inc(dve_step.sem, 1)
                    dve.wait_ge(dve_step.sem, dve_step.next(it))
                    if part < 2:
                        nc.vector.tensor_tensor(negm[:], negm[:], dst, ALU.subtract).then_inc(dve_step.sem, 1)
                        dve.wait_ge(dve_step.sem, dve_step.next(it))
                dve.wait_ge(oT_psum.sem, oT_psum.at(it, 1))
                o4 = ps[:, 0:2, :].rearrange("p a (n h c) -> p (a n) h c", n=4, h=4)
                nc.vector.reciprocal(rd[:], o4[:, :, :, A_V]).then_inc(dve_step.sem, 1)
                dve.wait_ge(dve_step.sem, dve_step.next(it))
                sub1 = rd[:].rearrange("p n (v s) -> p n v s", s=2)[:, :, :, 1]
                nc.vector.tensor_scalar(sub1, sub1, k["lam"][:], None, ALU.mult).then_inc(dve_step.sem, 1)
                dve.wait_ge(dve_step.sem, dve_step.next(it))
                for n in range(0, NT, 2):
                    nc.vector.tensor_tensor(oh[:, n:n + 2], o4[:, n:n + 2, :, 0:A_V],
                                            rd[:, n:n + 2].unsqueeze(3).broadcast_to([P, 2, 4, A_V]), ALU.mult).then_inc(dve_step.sem, 1)
                    dve.wait_ge(dve_step.sem, dve_step.next(it))
                oh5 = oh[:].rearrange("p n (v s) c -> p n v s c", s=2)
                dst = att[:, bass.ds(b * NT, NT), bass.ds(g * 2 * A_V, 2 * A_V)].rearrange("p n (v c) -> p n v c", v=2)
                nc.vector.tensor_tensor(dst, oh5[:, :, :, 0, :], oh5[:, :, :, 1, :], ALU.subtract).then_inc(dve_step.sem, 1)
                dve.wait_ge(dve_step.sem, dve_step.next(it))
            dve_step.check()


def phase_a3(nc, x_all, att, w_proj, ident, gamma8, pw):
    S = TILES // FT
    HV = D // A_V
    with ExitStack() as ctx:
        sb = lambda n, s, d=F32: ctx.enter_context(nc.sbuf_tensor("a3_" + n, s, d))
        sem = lambda n, per: Count(ctx.enter_context(nc.semaphore("a3_" + n)), per)
        sq = sb("sq", [P, FT * HV, A_V])
        ms = sb("ms", [P, 3, FT * HV])
        nrm = sb("nrm", [P, FT * HV, A_V])
        nT = sb("nT", [P, FT * P])
        ps_t = ctx.enter_context(nc.psum_tensor("a3_ps_t", [P, FT * P], F32))
        ps_o = ctx.enter_context(nc.psum_tensor("a3_ps_o", [P, FT, D], F32))
        dve_step = sem("dve_step", 6)
        rms_ready = sem("rms_ready", 1)
        nT_psum = sem("nT_psum", 1)
        nT_ready = sem("nT_ready", 1)
        o_psum = sem("o_psum", 1)
        block = ctx.enter_context(nc.Block())

        @block.vector
        def _(dve):
            with dve.Fori(0, S) as s:
                a = att[:, bass.ds(s * FT, FT), :].rearrange("p n (h c) -> p (n h) c", c=A_V)
                nc.vector.tensor_tensor(sq[:], a, a, ALU.mult).then_inc(dve_step.sem, 1)
                dve.wait_ge(dve_step.sem, dve_step.next(s))
                nc.vector.tensor_reduce(ms[:, 0, :], sq[:], X, ALU.add).then_inc(dve_step.sem, 1)
                dve.wait_ge(dve_step.sem, dve_step.next(s))
                nc.vector.tensor_scalar(ms[:, 1, :], ms[:, 0, :], 1.0 / A_V, EPS, ALU.mult, ALU.add).then_inc(dve_step.sem, 1)
                dve.wait_ge(dve_step.sem, dve_step.next(s))
                dve.wait_ge(rms_ready.sem, rms_ready.at(s, 1))
                nc.vector.tensor_tensor(nrm[:], a, ms[:, 2, :].unsqueeze(2).broadcast_to([P, FT * HV, A_V]), ALU.mult).then_inc(dve_step.sem, 1)
                dve.wait_ge(dve_step.sem, dve_step.next(s))
                nc.vector.tensor_tensor(nrm[:], nrm[:], gamma8[:].unsqueeze(1).broadcast_to([P, FT * HV, A_V]), ALU.mult).then_inc(dve_step.sem, 1)
                dve.wait_ge(dve_step.sem, dve_step.next(s))
                dve.wait_ge(o_psum.sem, o_psum.at(s, 1))
                xs = x_all[:, bass.ds(s * FT, FT), :]
                nc.vector.tensor_tensor(xs, ps_o[:], xs, ALU.add).then_inc(dve_step.sem, 1)
                dve.wait_ge(dve_step.sem, dve_step.next(s))
            dve_step.check()

        @block.gpsimd
        def _(pool):
            with pool.Fori(0, S) as s:
                pool.wait_ge(dve_step.sem, dve_step.at(s, 3))
                nc.gpsimd.tensor_tensor(ms[:, 2, :], ms[:, 1, :], pw[:, 0:FT * HV], ALU.pow).then_inc(rms_ready.sem, 1)

        @block.scalar
        def _(act):
            with act.Fori(0, S) as s:
                act.wait_ge(nT_psum.sem, nT_psum.at(s, 1))
                nc.scalar.copy(nT[:], ps_t[:]).then_inc(nT_ready.sem, 1)

        @block.tensor
        def _(pe):
            with pe.Fori(0, S) as s:
                pe.wait_ge(dve_step.sem, dve_step.at(s, 5))
                for n in range(FT):
                    last = nc.tensor.transpose(ps_t[:, n * P:(n + 1) * P],
                                               nrm[:, n * HV:(n + 1) * HV, :].rearrange("p h c -> p (h c)"), ident[:])
                last.then_inc(nT_psum.sem, 1)
                pe.wait_ge(nT_ready.sem, nT_ready.at(s, 1))
                for n in range(FT):
                    last = nc.tensor.matmul(ps_o[:, n, :], nT[:, n * P:(n + 1) * P], w_proj[:], start=True, stop=True)
                last.then_inc(o_psum.sem, 1)


def phase_f(nc, tag, x_all, k, out_dram):
    S = TILES // FT
    with ExitStack() as ctx:
        sb = lambda n, s, d=F32: ctx.enter_context(nc.sbuf_tensor(f"{tag}_{n}", s, d))
        sem = lambda n, per: Count(ctx.enter_context(nc.semaphore(f"{tag}_{n}")), per)
        xn = sb("xn", [P, FT, D])
        sq = sb("sq", [P, FT, D])
        st = sb("st", [P, 4, FT])
        xnT = sb("xnT", [P, FT * P])
        pr = sb("pr", [PROJ, 2, FT * P])
        lg = sb("lg", [P, FT, 8])
        g = sb("g", [P, 6, FT, E])
        r1 = sb("r1", [P, 8, FT])
        down = sb("down", [P, FT, E, R_PAD])
        downT = sb("downT", [E * R_PAD, FT * P])
        psum = lambda n, s: ctx.enter_context(nc.psum_tensor(f"{tag}_{n}", s, F32))
        ps_t = psum("ps_t", [P, FT * P])
        ps_p = psum("ps_p", [PROJ, FT * P])
        ps_l = psum("ps_l", [P, FT, 8])
        ps_d = psum("ps_d", [P, FT, E * R_PAD])
        ps_dT = psum("ps_dT", [E * R_PAD, FT * P])
        ps_o = psum("ps_o", [P, FT, D])
        dve_step = sem("dve_step", 25)
        rstd_ready = sem("rstd_ready", 2)
        xnT_psum = sem("xnT_psum", 1)
        xnT_ready = sem("xnT_ready", 1)
        p_psum = sem("p_psum", 1)
        l_psum = sem("l_psum", 1)
        exp_done = sem("exp_done", 1)
        dT_psum = sem("dT_psum", 1)
        dT_ready = sem("dT_ready", 1)
        o_psum = sem("o_psum", 1)
        stored = ctx.enter_context(nc.semaphore(f"{tag}_stored"))
        block = ctx.enter_context(nc.Block())

        @block.vector
        def _(dve):
            with dve.Fori(0, S) as s:
                xs = x_all[:, bass.ds(s * FT, FT), :]
                row = lambda i: r1[:, i, :]
                bc = lambda i: r1[:, i, :].unsqueeze(2).broadcast_to([P, FT, E])
                layernorm(nc, dve, dve_step, xs, xn, sq, st, rstd_ready, s)
                dve.wait_ge(p_psum.sem, p_psum.at(s, 1))
                nc.vector.tensor_scalar(pr[:, 0, :], ps_p[:], k["bp"][:], None, ALU.add).then_inc(dve_step.sem, 1)
                dve.wait_ge(dve_step.sem, dve_step.next(s))
                nc.vector.tensor_tensor(pr[:, 1, :], pr[:, 0, :], pr[:, 0, :], ALU.mult).then_inc(dve_step.sem, 1)
                dve.wait_ge(dve_step.sem, dve_step.next(s))
                dve.wait_ge(l_psum.sem, l_psum.at(s, 1))
                nc.vector.tensor_copy(lg[:, :, 0:E + 1], ps_l[:, :, 0:E + 1]).then_inc(dve_step.sem, 1)
                dve.wait_ge(dve_step.sem, dve_step.next(s))
                dve.wait_ge(rstd_ready.sem, rstd_ready.at(s, 2))
                nc.vector.tensor_scalar(row(0), row(7), 1e-12, None, ALU.max).then_inc(dve_step.sem, 1)
                dve.wait_ge(dve_step.sem, dve_step.next(s))
                nc.vector.reciprocal(row(1), row(0)).then_inc(dve_step.sem, 1)
                dve.wait_ge(dve_step.sem, dve_step.next(s))
                nc.vector.tensor_tensor(g[:, 0], lg[:, :, 0:E], bc(1), ALU.mult).then_inc(dve_step.sem, 1)
                dve.wait_ge(dve_step.sem, dve_step.next(s))
                nc.vector.tensor_reduce(row(2), g[:, 0], X, ALU.max).then_inc(dve_step.sem, 1)
                dve.wait_ge(dve_step.sem, dve_step.next(s))
                nc.vector.tensor_tensor(g[:, 1], g[:, 0], bc(2), ALU.subtract).then_inc(dve_step.sem, 1)
                dve.wait_ge(dve_step.sem, dve_step.next(s))
                dve.wait_ge(exp_done.sem, exp_done.at(s, 1))
                nc.vector.tensor_reduce(row(3), g[:, 2], X, ALU.add).then_inc(dve_step.sem, 1)
                dve.wait_ge(dve_step.sem, dve_step.next(s))
                nc.vector.reciprocal(row(4), row(3)).then_inc(dve_step.sem, 1)
                dve.wait_ge(dve_step.sem, dve_step.next(s))
                nc.vector.tensor_tensor(g[:, 3], g[:, 2], bc(4), ALU.mult).then_inc(dve_step.sem, 1)
                dve.wait_ge(dve_step.sem, dve_step.next(s))
                nc.vector.tensor_reduce(row(5), g[:, 3], X, ALU.max).then_inc(dve_step.sem, 1)
                dve.wait_ge(dve_step.sem, dve_step.next(s))
                nc.vector.tensor_tensor(g[:, 4], g[:, 3], bc(5), ALU.is_equal).then_inc(dve_step.sem, 1)
                dve.wait_ge(dve_step.sem, dve_step.next(s))
                nc.vector.tensor_tensor(g[:, 5], g[:, 4], k["rank4"][:].unsqueeze(1).broadcast_to([P, FT, E]), ALU.mult).then_inc(dve_step.sem, 1)
                dve.wait_ge(dve_step.sem, dve_step.next(s))
                nc.vector.tensor_reduce(row(6), g[:, 5], X, ALU.max).then_inc(dve_step.sem, 1)
                dve.wait_ge(dve_step.sem, dve_step.next(s))
                nc.vector.tensor_tensor(g[:, 4], g[:, 5], bc(6), ALU.is_equal).then_inc(dve_step.sem, 1)
                dve.wait_ge(dve_step.sem, dve_step.next(s))
                nc.vector.tensor_tensor(g[:, 5], g[:, 4], g[:, 3], ALU.mult).then_inc(dve_step.sem, 1)
                dve.wait_ge(dve_step.sem, dve_step.next(s))
                nc.vector.tensor_tensor(down[:].rearrange("p n e r -> p (n e) r"),
                                        ps_d[:].rearrange("p n (e r) -> p (n e) r", e=E),
                                        g[:, 5].rearrange("p n e -> p (n e)").unsqueeze(2)
                                        .broadcast_to([P, FT * E, R_PAD]), ALU.mult).then_inc(dve_step.sem, 1)
                dve.wait_ge(dve_step.sem, dve_step.next(s))
                dve.wait_ge(o_psum.sem, o_psum.at(s, 1))
                nc.vector.tensor_tensor(xs, ps_o[:], xs, ALU.add).then_inc(dve_step.sem, 1)
                dve.wait_ge(dve_step.sem, dve_step.next(s))
            dve_step.check()

        @block.gpsimd
        def _(pool):
            with pool.Fori(0, S) as s:
                pool.wait_ge(dve_step.sem, dve_step.at(s, 5))
                nc.gpsimd.tensor_tensor(st[:, 3, :], st[:, 2, :], k["pw"][:, 0:FT], ALU.pow).then_inc(rstd_ready.sem, 1)
                pool.wait_ge(dve_step.sem, dve_step.at(s, 9))
                nc.gpsimd.tensor_tensor(r1[:, 7, :], lg[:, :, E], k["ph"][:, 0:FT], ALU.pow).then_inc(rstd_ready.sem, 1)

        @block.scalar
        def _(act):
            with act.Fori(0, S) as s:
                act.wait_ge(xnT_psum.sem, xnT_psum.at(s, 1))
                nc.scalar.copy(xnT[:], ps_t[:]).then_inc(xnT_ready.sem, 1)
                act.wait_ge(dve_step.sem, dve_step.at(s, 14))
                nc.scalar.activation(g[:, 2], g[:, 1], ACT.Exp).then_inc(exp_done.sem, 1)
                act.wait_ge(dT_psum.sem, dT_psum.at(s, 1))
                nc.scalar.copy(downT[:], ps_dT[:]).then_inc(dT_ready.sem, 1)

        @block.tensor
        def _(pe):
            with pe.Fori(0, S) as s:
                tile = lambda n: slice(n * P, (n + 1) * P)
                pe.wait_ge(dve_step.sem, dve_step.at(s, 6))
                for n in range(FT):
                    last = nc.tensor.transpose(ps_t[:, tile(n)], xn[:, n, :], k["ident"][:])
                last.then_inc(xnT_psum.sem, 1)
                pe.wait_ge(xnT_ready.sem, xnT_ready.at(s, 1))
                nc.tensor.matmul(ps_p[:], k["wpT"][:], xnT[:], start=True, stop=True).then_inc(p_psum.sem, 1)
                for n in range(FT):
                    nc.tensor.matmul(ps_d[:, n, :], xnT[:, tile(n)], k["wdT"][:], start=True, stop=True)
                pe.wait_ge(dve_step.sem, dve_step.at(s, 8))
                for n in range(FT):
                    nc.tensor.matmul(ps_l[:, n, 0:E], pr[:, 0, tile(n)], k["simn"][:], start=True, stop=True)
                    last = nc.tensor.matmul(ps_l[:, n, E:E + 1], pr[:, 1, tile(n)], k["ones32"][:, 0:1], start=True, stop=True)
                last.then_inc(l_psum.sem, 1)
                pe.wait_ge(dve_step.sem, dve_step.at(s, 24))
                for n in range(FT):
                    last = nc.tensor.transpose(ps_dT[:, tile(n)], down[:, n].rearrange("p e r -> p (e r)"), k["ident"][:])
                last.then_inc(dT_psum.sem, 1)
                pe.wait_ge(dT_ready.sem, dT_ready.at(s, 1))
                for n in range(FT):
                    nc.tensor.matmul(ps_o[:, n, :], xnT[:, tile(n)], k["wT"][:], start=True, stop=False)
                    last = nc.tensor.matmul(ps_o[:, n, :], downT[:, tile(n)], k["wu"][:], start=False, stop=True)
                last.then_inc(o_psum.sem, 1)

        if out_dram is not None:
            @block.sync
            def _(sp):
                for s in range(S):
                    sp.wait_ge(dve_step.sem, (s + 1) * dve_step.per)
                    sp.dma_start(out_dram[:, s * FT:(s + 1) * FT, :], x_all[:, s * FT:(s + 1) * FT, :]).then_inc(stored, 16)
                sp.wait_ge(stored, 16 * S)


def phase_b(nc, x_all, k):
    with ExitStack() as ctx:
        sb = lambda n, s, d=F32: ctx.enter_context(nc.sbuf_tensor("b_" + n, s, d))
        sem = lambda n, per: Count(ctx.enter_context(nc.semaphore("b_" + n)), per)
        xn = sb("xn", [P, 1, D])
        sq = sb("sq", [P, 1, D])
        st = sb("st", [P, 4, 1])
        xnT = sb("xnT", [P, P])
        q = sb("q", [P, 2, H, C])
        key = sb("key", [P, 2, H, C])
        val = sb("val", [P, 2, H, C])
        m = sb("m", [P, 2, H, C])
        kmin = sb("kmin", [P, H, C])
        sums = sb("sums", [P, 2, H, C])
        osum = sb("osum", [P, 1, D])
        p_ring = (sb("p_long", [P, P_RING // 2, H * JB * C]), sb("p_short", [P, P_RING // 2, H * JB * C // 2]))
        ev_ring = (sb("ev_long", [P, EV_RING // 2, H * JB * C]), sb("ev_short", [P, EV_RING // 2, H * JB * C // 2]))
        oT = sb("oT", [P, HID])
        acc = ctx.enter_context(nc.psum_tensor("b_acc", [P, 4, H, C // 2], F32))
        stage = ctx.enter_context(nc.psum_tensor("b_stage", [P, 4, 512], F32))
        xn_step = sem("xn_step", 6)
        m_step = sem("m_step", 5)
        sums_taken = sem("sums_taken", 2)
        divided = sem("divided", 2)
        x_step = sem("x_step", 2)
        rstd_ready = sem("rstd_ready", 1)
        xnT_psum = sem("xnT_psum", 1)
        xnT_ready = sem("xnT_ready", 1)
        qkv_psum = sem("qkv_psum", 3)
        qkv_taken = sem("qkv_taken", 3)
        product = sem("product", 2 * CHUNKS)
        shifted = sem("shifted", CHUNKS)
        exp_done = sem("exp_done", CHUNKS)
        ev_dve = sem("ev_dve", CHUNKS)
        ev_pool = sem("ev_pool", CHUNKS)
        folded = sem("folded", len(FOLD_EV) + len(FOLD_P))
        summed = sem("summed", CHUNKS)
        oT_psum = sem("oT_psum", 1)
        oT_ready = sem("oT_ready", 1)
        o_psum = sem("o_psum", 1)
        block = ctx.enter_context(nc.Block())
        DH = H - POOL_HEADS

        def all_tiles(eng, tile):
            tile(0, 0, True, False)
            with eng.Fori(0, (TILES - 2) // 2) as u:
                tile(2 * u + 1, 1, False, False)
                tile(2 * u + 2, 0, False, False)
            tile(TILES - 1, 1, False, True)

        def chunk_flat(ring, at):
            slots = ring[at % 2]
            return slots[:, at // 2 % slots.shape[1], 0:H * JB * (C - JB * ORDER[at])]

        def chunk(ring, at):
            return chunk_flat(ring, at).rearrange("p (h j i) -> p h j i", h=H, j=JB)

        def keys(t, buf, at, h=slice(0, H)):
            c = ORDER[at]
            n = C - JB * c
            return t[:, buf, h, JB * c:JB * c + JB].unsqueeze(3).broadcast_to([P, t[:, buf, h].shape[1], JB, n])

        def queries(t, buf, at):
            c = ORDER[at]
            n = C - JB * c
            return t[:, buf, :, JB * c:C].unsqueeze(2).broadcast_to([P, H, JB, n])

        def flat(t, buf):
            return t[:, buf].rearrange("p h c -> p (h c)")

        def folds_until(at):
            return sum((c in FOLD_EV) + (c in FOLD_P) for c in ORDER[:at + 1])

        def ahead_of(it, buf, last, c, lag):
            if c + lag < CHUNKS:
                return it, buf, c + lag
            return None if last else (it + 1, 1 - buf, c + lag - CHUNKS)

        @block.vector
        def _(dve):
            def multiply(it, buf, c, first):
                if c >= P_RING or not first:
                    dve.wait_ge(summed.sem, summed.at(it, c - P_RING + 1))
                pc = chunk(p_ring, c)
                nc.vector.tensor_tensor(pc, queries(q, buf, c), keys(key, buf, c), ALU.mult).then_inc(product.sem, 1)
                dve.wait_ge(product.sem, product.at(it, 2 * c + 1))
                corner = pc[:, :, :, 0:JB]
                nc.vector.tensor_tensor(corner, corner, k["corner"][:].unsqueeze(1).broadcast_to([P, H, JB, JB]),
                                        ALU.min).then_inc(product.sem, 1)

            def fold(it, c):
                if ORDER[c] in FOLD_EV or ORDER[c] in FOLD_P:
                    dve.wait_ge(ev_dve.sem, ev_dve.at(it, c + 1))
                    dve.wait_ge(ev_pool.sem, ev_pool.at(it, c + 1))
                for ring, which in ((ev_ring, FOLD_EV), (p_ring, FOLD_P)):
                    if ORDER[c] in which:
                        t = chunk(ring, c)
                        nc.vector.tensor_tensor(t[:, :, 0], t[:, :, 0], t[:, :, 1], ALU.add).then_inc(folded.sem, 1)

            def norm(it):
                xn_step.n = 0
                layernorm(nc, dve, xn_step, x_all[:, bass.ds(it, 1), :], xn, sq, st, rstd_ready, it)

            def maxima(it, buf, part):
                if part == 0:
                    dve.wait_ge(qkv_taken.sem, qkv_taken.at(it, 2))
                    nc.vector.tensor_tensor_scan(flat(m, buf), k["reset_max"][:], flat(key, buf), 0.0,
                                                 ALU.min, ALU.max).then_inc(m_step.sem, 1)
                elif part == 1:
                    nc.vector.tensor_tensor_scan(kmin[:].rearrange("p h c -> p (h c)"), k["reset_min"][:], flat(key, buf), 0.0,
                                                 ALU.max, ALU.min).then_inc(m_step.sem, 1)
                else:
                    dve.wait_ge(m_step.sem, m_step.at(it, 2))
                    nc.vector.tensor_tensor(m[:, buf], m[:, buf], q[:, buf], ALU.mult).then_inc(m_step.sem, 1)
                    nc.vector.tensor_tensor(kmin[:], kmin[:], q[:, buf], ALU.mult).then_inc(m_step.sem, 1)
                    dve.wait_ge(m_step.sem, m_step.at(it, 4))
                    nc.vector.tensor_tensor(m[:, buf], m[:, buf], kmin[:], ALU.max).then_inc(m_step.sem, 1)
                    dve.wait_ge(m_step.sem, m_step.at(it, 5))

            def divide(it):
                dve.wait_ge(sums_taken.sem, sums_taken.at(it, 2))
                nc.vector.reciprocal(sums[:, 1], sums[:, 1]).then_inc(divided.sem, 1)
                dve.wait_ge(divided.sem, divided.at(it, 1))
                nc.vector.tensor_tensor(sums[:, 0], sums[:, 0], sums[:, 1], ALU.mult).then_inc(divided.sem, 1)

            def residual(it):
                dve.wait_ge(o_psum.sem, o_psum.at(it, 1))
                nc.vector.tensor_tensor(osum[:, 0, :], stage[:, 2, 0:D], k["bo"][:], ALU.add).then_inc(x_step.sem, 1)
                dve.wait_ge(x_step.sem, x_step.at(it, 1))
                xs = x_all[:, bass.ds(it, 1), :]
                nc.vector.tensor_tensor(xs, xs, osum[:], ALU.add).then_inc(x_step.sem, 1)

            def tile(it, buf, first, last):
                for c in range(CHUNKS):
                    coming = ahead_of(it, buf, last, c, MULTIPLY_AHEAD)
                    if coming:
                        multiply(*coming, first and c + MULTIPLY_AHEAD < CHUNKS)
                    pc, ev = chunk(p_ring, c), chunk(ev_ring, c)
                    if c == 0:
                        dve.wait_ge(qkv_taken.sem, qkv_taken.at(it, 3))
                    dve.wait_ge(exp_done.sem, exp_done.at(it, c + 1))
                    if c >= EV_RING or not first:
                        dve.wait_ge(summed.sem, summed.at(it, c - EV_RING + 1))
                    nc.vector.tensor_tensor(ev[:, 0:DH], pc[:, 0:DH], keys(val, buf, c, slice(0, DH)),
                                            ALU.mult).then_inc(ev_dve.sem, 1)
                    if c > 0:
                        fold(it, c - 1)
                    if not first and c == DIVIDE_AT:
                        divide(it - 1)
                    if not first and c == RESIDUAL_AT:
                        residual(it - 1)
                    if last:
                        continue
                    if c == NORM_AT:
                        norm(it + 1)
                    if c in MAX_AT:
                        maxima(it + 1, 1 - buf, MAX_AT.index(c))
                fold(it, CHUNKS - 1)

            norm(0)
            for part in range(3):
                maxima(0, 0, part)
            for c in range(MULTIPLY_AHEAD):
                multiply(0, 0, c, True)
            all_tiles(dve, tile)
            divide(TILES - 1)
            residual(TILES - 1)

        @block.gpsimd
        def _(pool):
            def root(it):
                pool.wait_ge(xn_step.sem, xn_step.at(it, 5))
                nc.gpsimd.tensor_tensor(st[:, 3, :], st[:, 2, :], k["pw"][:, 0:1], ALU.pow).then_inc(rstd_ready.sem, 1)

            def shift(it, buf, c):
                pool.wait_ge(product.sem, product.at(it, 2 * c + 2))
                pc = chunk(p_ring, c)
                nc.gpsimd.tensor_tensor(pc, pc, queries(m, buf, c), ALU.subtract).then_inc(shifted.sem, 1)

            def tile(it, buf, first, last):
                for c in range(CHUNKS):
                    coming = ahead_of(it, buf, last, c, SHIFT_AHEAD)
                    if coming:
                        shift(*coming)
                    pool.wait_ge(exp_done.sem, exp_done.at(it, c + 1))
                    if c >= EV_RING or not first:
                        pool.wait_ge(summed.sem, summed.at(it, c - EV_RING + 1))
                    pc, ev = chunk(p_ring, c), chunk(ev_ring, c)
                    nc.gpsimd.tensor_tensor(ev[:, DH:H], pc[:, DH:H], keys(val, buf, c, slice(DH, H)),
                                            ALU.mult).then_inc(ev_pool.sem, 1)
                    if not last and c == NORM_AT:
                        root(it + 1)

            root(0)
            for c in range(SHIFT_AHEAD):
                shift(0, 0, c)
            all_tiles(pool, tile)

        @block.scalar
        def _(act):
            def copy_xnT(it):
                act.wait_ge(xnT_psum.sem, xnT_psum.at(it, 1))
                nc.scalar.copy(xnT[:], stage[:, 0, 0:P]).then_inc(xnT_ready.sem, 1)

            def take(it, buf, i):
                act.wait_ge(qkv_psum.sem, qkv_psum.at(it, i + 1))
                src = stage[:, 2 * (i % 2):2 * (i % 2) + 2, :].rearrange("p a b -> p (a b)")
                nc.scalar.activation(flat((q, key, val)[i], buf), src, ACT.Copy,
                                     scale=0.125 if i == 0 else 1.0).then_inc(qkv_taken.sem, 1)

            def copy_oT(it):
                act.wait_ge(oT_psum.sem, oT_psum.at(it, 1))
                nc.scalar.copy(oT[:], stage[:, 0:2, :].rearrange("p a b -> p (a b)")).then_inc(oT_ready.sem, 1)

            def tile(it, buf, first, last):
                for c in range(CHUNKS):
                    act.wait_ge(shifted.sem, shifted.at(it, c + 1))
                    pc = chunk_flat(p_ring, c)
                    nc.scalar.activation(pc, pc, ACT.Exp).then_inc(exp_done.sem, 1)
                    if not first and c == COPY_O_AT:
                        copy_oT(it - 1)
                    if not last and c == COPY_XN_AT:
                        copy_xnT(it + 1)
                    if not last and c in TAKE_AT:
                        take(it + 1, 1 - buf, TAKE_AT.index(c))
                act.wait_ge(summed.sem, summed.at(it, CHUNKS))
                for w in range(2):
                    nc.scalar.copy(sums[:, w].rearrange("p h (a i) -> p a h i", a=2),
                                   acc[:, 2 * w:2 * w + 2]).then_inc(sums_taken.sem, 1)

            copy_xnT(0)
            for i in range(3):
                take(0, 0, i)
            all_tiles(act, tile)
            copy_oT(TILES - 1)

        @block.tensor
        def _(pe):
            def turn_xn(it):
                pe.wait_ge(xn_step.sem, xn_step.at(it, 6))
                nc.tensor.transpose(stage[:, 0, 0:P], xn[:, 0, :], k["ident"][:]).then_inc(xnT_psum.sem, 1)

            def qkv(it, i):
                pe.wait_ge(xnT_ready.sem, xnT_ready.at(it, 1))
                if i == 2:
                    pe.wait_ge(qkv_taken.sem, qkv_taken.at(it, 1))
                for half in range(2):
                    last = nc.tensor.matmul(stage[:, 2 * (i % 2) + half, :], xnT[:],
                                            k["wqkv"][:, i, half * 512:(half + 1) * 512], start=True, stop=False)
                    last = nc.tensor.matmul(stage[:, 2 * (i % 2) + half, :], k["ones3"][:],
                                            k["bias3"][:, i, half * 512:(half + 1) * 512], start=False, stop=True)
                last.then_inc(qkv_psum.sem, 1)

            def turn_o(it):
                pe.wait_ge(divided.sem, divided.at(it, 2))
                of = sums[:, 0].rearrange("p h c -> p (h c)")
                for i in range(HID // P):
                    last = nc.tensor.transpose(stage[:, i // 4, i % 4 * P:(i % 4 + 1) * P], of[:, i * P:(i + 1) * P],
                                               k["ident"][:])
                last.then_inc(oT_psum.sem, 1)

            def project(it):
                pe.wait_ge(oT_ready.sem, oT_ready.at(it, 1))
                for i in range(HID // P):
                    last = nc.tensor.matmul(stage[:, 2, 0:D], oT[:, i * P:(i + 1) * P], k["wo"][:, i, :],
                                            start=i == 0, stop=i == HID // P - 1)
                last.then_inc(o_psum.sem, 1)

            def tile(it, buf, first, last_tile):
                for c in range(CHUNKS):
                    if c == 0 and not first:
                        pe.wait_ge(sums_taken.sem, sums_taken.at(it - 1, 2))
                    pe.wait_ge(ev_dve.sem, ev_dve.at(it, c + 1))
                    pe.wait_ge(ev_pool.sem, ev_pool.at(it, c + 1))
                    if ORDER[c] in FOLD_EV or ORDER[c] in FOLD_P:
                        pe.wait_ge(folded.sem, folded.at(it, folds_until(c)))
                    j0 = JB * ORDER[c]
                    for w, (ring, which) in enumerate(((ev_ring, FOLD_EV), (p_ring, FOLD_P))):
                        src = chunk(ring, c)
                        last_j = 0 if ORDER[c] in which else JB - 1
                        for half in range(2):
                            lo, hi = max(j0, half * 32), half * 32 + 32
                            if lo >= hi:
                                continue
                            closes = all(max(JB * d, half * 32) >= hi for d in ORDER[c + 1:])
                            for j in range(last_j + 1):
                                last = nc.tensor.matmul(acc[:, 2 * w + half, :, lo - 32 * half:], k["ident"][:],
                                                        src[:, :, j, lo - j0:hi - j0],
                                                        start=c == 0 and j == 0, stop=closes and j == last_j)
                    last.then_inc(summed.sem, 1)
                    if not first and c == TURN_O_AT:
                        turn_o(it - 1)
                    if not first and c == PROJECT_AT:
                        project(it - 1)
                    if last_tile:
                        continue
                    if c == TURN_XN_AT:
                        turn_xn(it + 1)
                    if c in QKV_AT:
                        qkv(it + 1, QKV_AT.index(c))

            turn_xn(0)
            for i in range(3):
                qkv(0, i)
            all_tiles(pe, tile)
            turn_o(TILES - 1)
            project(TILES - 1)


def build(nc, a, out):
    with ExitStack() as ctx, ExitStack() as ctx_a:
        sb = lambda n, s, d=F32: ctx.enter_context(nc.sbuf_tensor(n, s, d))
        sb_a = lambda n, s, d=F32: ctx_a.enter_context(nc.sbuf_tensor(n, s, d))
        x_all = sb("x_all", [P, TILES, D])
        k = {}
        for name, shape, dt in (
            ("ident", [P, P], F32), ("wT", [P, D], F32), ("wpT", [P, PROJ], F32), ("wdT", [P, E * R_PAD], F32),
            ("wu", [E * R_PAD, D], F32), ("bp", [PROJ, 1], F32), ("sim", [PROJ, E], F32), ("temp", [PROJ, 1], F32),
            ("rank4", [P, E], F32), ("wqkv", [P, 3, HID], F32), ("bo", [P, D], F32), ("wo", [P, HID // P, D], F32), ("corner", [P, JB, JB], F32),
            ("reset_max", [P, HID], BF16), ("reset_min", [P, HID], BF16),
        ):
            k[name] = sb("k_" + name, shape, dt)
        loads = list(k)
        for name, shape in (("pw", [P, 64]), ("ph", [P, 64]), ("ones32", [PROJ, PROJ]), ("simn", [PROJ, E]), ("lam", [P, 1]),
                            ("gamma8", [P, A_V]), ("tmp", [P, 4, A_HD])):
            k[name] = sb("k_" + name, shape)
        k["ones3"] = sb("ones3", [3, P], BF16)
        k["bias3"] = sb("bias3", [3, 3, HID], BF16)
        t32 = sb("t32", [PROJ, 6, E])
        for name, shape, dt in (
            ("w_attn", [P, 3 * D], F32), ("w_proj", [P, D], F32), ("ident_b", [P, P], BF16), ("mask", [P, P], BF16),
            ("mask_t", [P, P], BF16), ("sel_q", [P, 3, GROUPS * P], BF16), ("sel_k", [P, 3, GROUPS * P], BF16),
            ("one_rows", [P, 1], F32), ("bias", [1, 3 * HID], F32), ("lams", [P, 4, A_HD], F32), ("gamma", [P, A_V], F32),
        ):
            k[name] = sb_a("k_" + name, shape, dt)
            loads.append(name)
        loaded = ctx.enter_context(nc.semaphore("loaded"))
        filled = ctx.enter_context(nc.semaphore("filled"))
        dve_step = Count(ctx.enter_context(nc.semaphore("k_dve_step")), 0)
        act_step = Count(ctx.enter_context(nc.semaphore("k_act_step")), 0)
        pool_step = Count(ctx.enter_context(nc.semaphore("k_pool_step")), 0)
        norm_psum = ctx.enter_context(nc.semaphore("norm_psum"))

        with ExitStack() as ctx2:
            ps = ctx2.enter_context(nc.psum_tensor("k_ps", [PROJ, E], F32))
            block = ctx2.enter_context(nc.Block())
            n_loads = 16 * (len(loads) + 1)

            @block.sync
            def _(sp):
                sp.dma_start(x_all[:], a["x"]).then_inc(loaded, 16)
                for name in loads[0::2]:
                    sp.dma_start(k[name][:], a[name]).then_inc(loaded, 16)

            @block.scalar
            def _(act):
                for name in loads[1::2]:
                    act.dma_start(k[name][:], a[name]).then_inc(loaded, 16)
                act.wait_ge(dve_step.sem, dve_step.at(0, 2))
                nc.scalar.activation(k["lams"][:, 0, 0:2], k["lams"][:, 2, 0:2], ACT.Exp).then_inc(act_step.sem, 1)
                act.wait_ge(dve_step.sem, dve_step.at(0, 3))
                nc.scalar.activation(t32[:, 4, 1:2], t32[:, 4, 0:1], ACT.Exp).then_inc(act_step.sem, 1)

            @block.gpsimd
            def _(pool):
                nc.gpsimd.memset(k["pw"][:], -0.5).then_inc(filled, 1)
                nc.gpsimd.memset(k["ph"][:], 0.5).then_inc(filled, 1)
                nc.gpsimd.memset(k["ones3"][:], 1.0).then_inc(filled, 1)
                nc.gpsimd.memset(k["ones32"][:], 1.0).then_inc(filled, 1)
                pool.wait_ge(filled, 4)
                pool.wait_ge(dve_step.sem, dve_step.at(0, 5))
                nc.gpsimd.tensor_tensor(t32[:, 2, :], t32[:, 1, :], k["ph"][0:PROJ, 0:E], ALU.pow).then_inc(pool_step.sem, 1)

            @block.tensor
            def _(pe):
                pe.wait_ge(filled, 4)
                pe.wait_ge(dve_step.sem, dve_step.at(0, 4))
                nc.tensor.matmul(ps[:], k["ones32"][:], t32[:, 0, :], start=True, stop=True).then_inc(norm_psum, 1)

            @block.vector
            def _(dve):
                dve.wait_ge(loaded, n_loads)
                lams = k["lams"]
                nc.vector.tensor_tensor(k["tmp"][:, 0:2, :], lams[:, 0:4:2, :], lams[:, 1:4:2, :], ALU.mult).then_inc(dve_step.sem, 1)
                dve.wait_ge(dve_step.sem, dve_step.next(0))
                nc.vector.tensor_reduce(lams[:, 2, 0:2], k["tmp"][:, 0:2, :], X, ALU.add).then_inc(dve_step.sem, 1)
                dve.wait_ge(dve_step.sem, dve_step.next(0))
                nc.vector.tensor_scalar(t32[:, 4, 0:1], k["temp"][:], CLAMP_MAX, None, ALU.min).then_inc(dve_step.sem, 1)
                dve.wait_ge(dve_step.sem, dve_step.next(0))
                nc.vector.tensor_tensor(t32[:, 0, :], k["sim"][:], k["sim"][:], ALU.mult).then_inc(dve_step.sem, 1)
                dve.wait_ge(dve_step.sem, dve_step.next(0))
                dve.wait_ge(norm_psum, 1)
                nc.vector.tensor_copy(t32[:, 1, :], ps[:]).then_inc(dve_step.sem, 1)
                dve.wait_ge(dve_step.sem, dve_step.next(0))
                dve.wait_ge(pool_step.sem, pool_step.at(0, 1))
                nc.vector.tensor_scalar(t32[:, 3, :], t32[:, 2, :], 1e-12, None, ALU.max).then_inc(dve_step.sem, 1)
                dve.wait_ge(dve_step.sem, dve_step.next(0))
                nc.vector.reciprocal(t32[:, 5, :], t32[:, 3, :]).then_inc(dve_step.sem, 1)
                dve.wait_ge(dve_step.sem, dve_step.next(0))
                nc.vector.tensor_tensor(t32[:, 0, :], k["sim"][:], t32[:, 5, :], ALU.mult).then_inc(dve_step.sem, 1)
                dve.wait_ge(dve_step.sem, dve_step.next(0))
                dve.wait_ge(act_step.sem, act_step.at(0, 2))
                nc.vector.tensor_scalar(k["simn"][:], t32[:, 0, :], t32[:, 4, 1:2], None, ALU.mult).then_inc(dve_step.sem, 1)
                dve.wait_ge(dve_step.sem, dve_step.next(0))
                nc.vector.tensor_tensor(k["tmp"][:, 3, 0:1], lams[:, 0, 0:1], lams[:, 0, 1:2], ALU.subtract).then_inc(dve_step.sem, 1)
                dve.wait_ge(dve_step.sem, dve_step.next(0))
                nc.vector.tensor_scalar(k["lam"][:], k["tmp"][:, 3, 0:1], LAMBDA_INIT, None, ALU.add).then_inc(dve_step.sem, 1)
                dve.wait_ge(dve_step.sem, dve_step.next(0))
                nc.vector.tensor_scalar(k["gamma8"][:], k["gamma"][:], 1.0 - LAMBDA_INIT, None, ALU.mult).then_inc(dve_step.sem, 1)
                dve.wait_ge(dve_step.sem, dve_step.next(0))

        rows_q = sb_a("rows_q", [P, 3, BATCH * T], BF16)
        rows_k = sb_a("rows_k", [P, 3, BATCH * T], BF16)
        v_nat = sb_a("v_nat", [P, TILES, D])
        att = sb_a("att", [P, TILES, D])
        phase_a1(nc, x_all, k["w_attn"], k["ident"], rows_q, rows_k, v_nat, k["pw"])
        phase_a2(nc, rows_q, rows_k, v_nat, att, k)
        phase_a3(nc, x_all, att, k["w_proj"], k["ident"], k["gamma8"], k["pw"])
        ctx_a.close()
        phase_f(nc, "f1", x_all, k, None)
        phase_b(nc, x_all, k)
        phase_f(nc, "f2", x_all, k, out)


def kernel(**inputs):
    import ml_dtypes
    import numpy as np
    import concourse.bacc as bacc
    from concourse.bass_utils import run_bass_kernel_spmd as run

    i = {n: np.asarray(v) for n, v in inputs.items()}
    A, B, F = "L0_attn_a_", "L0_attn_b_", "L0_ffn_"
    bf = ml_dtypes.bfloat16
    rows = lambda v, n=P: np.ascontiguousarray(np.broadcast_to(v, (n,) + v.shape))
    x = i[A + "x"]
    arrays = {
        "x": x, "w_attn": i[A + "w_attn"], "w_proj": i[A + "w_proj"],
        "lams": rows(np.stack([i[A + "lambda_q1"], i[A + "lambda_k1"], i[A + "lambda_q2"], i[A + "lambda_k2"]])),
        "gamma": rows(i[A + "gamma"]),
        "wT": i[F + "W"].T, "wpT": i[F + "Wp"].T, "bp": i[F + "bp"][:, None], "sim": i[F + "sim"],
        "temp": rows(i[F + "temp"], PROJ),
        "wqkv": np.stack([i[B + "Wq"], i[B + "Wk"], i[B + "Wv"]], 1),
        "bias": np.concatenate([i[B + "bq"], i[B + "bk"], i[B + "bv"]])[None], "bo": rows(i[B + "bo"]),
        "wo": i[B + "Wo"].reshape(HID // P, P, D).transpose(1, 0, 2),
    }
    wd = np.zeros((E, R_PAD, D), np.float32)
    wu = np.zeros((E, R_PAD, D), np.float32)
    for e in range(E):
        d, u = i[F + f"Wd{e}"], i[F + f"Wu{e}"]
        wd[e, :d.shape[0]] = d
        wu[e, :u.shape[1]] = u.T
    arrays["wdT"] = wd.reshape(E * R_PAD, D).T
    arrays["wu"] = wu.reshape(E * R_PAD, D)
    arrays["ident"] = np.eye(P, dtype=np.float32)
    arrays["ident_b"] = np.eye(P, dtype=np.float32).astype(bf)
    later = np.triu(np.ones((P, P), np.float32), 1)
    arrays["mask"] = (NEG * later).astype(bf)
    arrays["mask_t"] = (NEG * later.T).astype(bf)
    for name, terms in (("sel_q", TERM_Q), ("sel_k", TERM_K)):
        sel = np.zeros((P, 3, GROUPS, 4, 32), np.float32)
        for g in range(GROUPS):
            for h in range(4):
                for t, part in enumerate(terms):
                    for d in range(A_HD):
                        sel[(4 * g + h) * A_HD + d, part, g, h, t * A_HD + d] = 1.0
        arrays[name] = sel.reshape(P, 3, GROUPS * P).astype(bf)
    one = np.zeros((4, 32, 1), np.float32)
    one[:, M_ROW:M_ROW + 3] = 1.0
    arrays["one_rows"] = one.reshape(P, 1)
    arrays["rank4"] = rows(np.arange(E, 0, -1).astype(np.float32))
    corner = np.full((JB, JB), BIG, np.float32)
    for j in range(JB):
        corner[j, :j] = -1e38
    arrays["corner"] = rows(corner)
    first = (np.arange(HID) % C == 0)
    arrays["reset_max"] = rows(np.where(first, -BIG, BIG).astype(bf))
    arrays["reset_min"] = rows(np.where(first, BIG, -BIG).astype(bf))

    nc = bacc.Bacc("TRN2", target_bir_lowering=False, num_devices=1)
    feeds, args = {}, {}
    for name, v in arrays.items():
        v = np.ascontiguousarray(v)
        feeds[f"in_{name}"] = v
        args[name] = nc.dram_tensor(f"in_{name}", v.shape, mybir.dt.from_np(v.dtype), kind="ExternalInput").ap()
    args["x"] = args["x"].rearrange("b (n p) d -> p (b n) d", p=P)
    out = nc.dram_tensor("out", x.shape, F32, kind="ExternalOutput").ap()
    build(nc, args, out.rearrange("b (n p) d -> p (b n) d", p=P))
    r = run(nc, [feeds], core_ids=[0])
    return r.results[0]["out"]
```

```python
from contextlib import ExitStack

import concourse.bass as bass
from concourse import mybir

F32 = mybir.dt.float32
BF16 = mybir.dt.bfloat16
ALU = mybir.AluOpType
ACT = mybir.ActivationFunctionType
X = mybir.AxisListType.X

P = 128
D = 128
BATCH = 2
T = 1024
NT = T // P
TILES = BATCH * NT
EPS = 1e-5
NEG = -1e30
BIG = 3e38
LAMBDA_INIT = 0.2

A_HD = 4
A_V = 8
GROUPS = 8
TERM_Q = (0, 0, 1, 0, 1, 2)
TERM_K = (0, 1, 0, 2, 1, 0)
M_ROW = len(TERM_Q) * A_HD

H = 16
C = 64
HID = H * C
JB = 2
MASKED = -1e38
CHUNKS = C // JB
POOL_HEADS = 7
ORDER = tuple(c for i in range(CHUNKS // 2) for c in (i, CHUNKS - 1 - i))
P_RING = 16
EV_RING = 8
MULTIPLY_AHEAD = 8
SHIFT_AHEAD = 4
FOLD_EV = tuple(range(2, CHUNKS))
FOLD_P = tuple(range(22, CHUNKS))
TAKE_SUMS_AT, DIVIDE_AT, TURN_O_AT, COPY_O_AT, PROJECT_AT, RESIDUAL_AT = 3, 3, 4, 7, 8, 11
NORM_AT, ROOT_AT, SCALE_AT, TURN_XN_AT, COPY_XN_AT = 6, 7, 8, 9, 12
QKV_AT = (12, 13, 16)
TAKE_AT = (15, 16, 19)
MAX_AT = (20, 21, 22)

PROJ = 32
E = 4
R_PAD = 8
CLAMP_MAX = 4.605170185988092
FT = 4


class Count:

    def __init__(self, sem, per, first=0):
        self.sem, self.per, self.first, self.n = sem, per, first, 0

    def at(self, it, k):
        return it * self.per + (self.first + k)

    def next(self, it):
        self.n += 1
        return self.at(it, self.n)

    def check(self):
        assert self.n == self.per, (self.sem, self.n, self.per)


def phase_a1(nc, a, loads, x_all, k, t32, rows_q, rows_k, v_nat):
    S = TILES // FT
    with ExitStack() as ctx:
        sb = lambda n, s, d=F32: ctx.enter_context(nc.sbuf_tensor("a1_" + n, s, d))
        sem = lambda n, per=0: Count(ctx.enter_context(nc.semaphore("a1_" + n)), per)
        xn = sb("xn", [P, TILES, D])
        sq = sb("sq", [P, TILES, D])
        st = sb("st", [P, 4, TILES])
        xnT = sb("xnT", [P, TILES * P])
        qk = sb("qk", [P, 2, TILES * P])
        ps_t = ctx.enter_context(nc.psum_tensor("a1_ps_t", [P, 2, FT * P], F32))
        ps_qk = ctx.enter_context(nc.psum_tensor("a1_ps_qk", [P, 2, 2, FT * P], F32))
        ps_v = ctx.enter_context(nc.psum_tensor("a1_ps_v", [P, FT * P], F32))
        ps_n = ctx.enter_context(nc.psum_tensor("a1_ps_n", [PROJ, E], F32))
        x_loaded = sem("x_loaded")
        first_loaded = sem("first_loaded")
        loaded = sem("loaded")
        filled = sem("filled")
        stat_step = sem("stat_step", 5)
        rstd_ready = sem("rstd_ready", 1)
        xn_ready = sem("xn_ready", S)
        xnT_psum = sem("xnT_psum", S)
        xnT_ready = sem("xnT_ready", S)
        qkv_psum = sem("qkv_psum", 3 * S)
        qkv_taken = sem("qkv_taken", 3 * S)
        q_step = sem("q_step", 5 * S)
        k_step = sem("k_step", 5 * S)
        const_step = sem("const_step", 12)
        exps_done = sem("exps_done", 2)
        norm_ready = sem("norm_ready", 1)
        norm_psum = sem("norm_psum", 1)
        block = ctx.enter_context(nc.Block())
        piece = lambda s: slice(s * FT, (s + 1) * FT)
        cols = lambda s: slice(s * FT * P, (s + 1) * FT * P)
        first = ("ident", "w_attn")
        rest = [name for name in loads if name not in first]

        @block.sync
        def _(sp):
            sp.dma_start(x_all[:], a["x"]).then_inc(x_loaded.sem, 16)
            for name in rest[0::2]:
                sp.dma_start(k[name][:], a[name]).then_inc(loaded.sem, 16)
            sp.wait_ge(loaded.sem, 16 * len(rest))

        def parts(eng_ns, eng, step, rows, i, s):
            left = qk[:, i, cols(s)]
            for part in range(3):
                dst = rows[:, part, cols(s)]
                eng_ns.tensor_copy(dst, left).then_inc(step.sem, 1)
                eng.wait_ge(step.sem, step.next(0))
                if part < 2:
                    eng_ns.tensor_tensor(left, left, dst, ALU.subtract).then_inc(step.sem, 1)
                    eng.wait_ge(step.sem, step.next(0))

        @block.vector
        def _(dve):
            nc.vector.memset(k["ones3"][:], 1.0)
            dve.wait_ge(x_loaded.sem, 16)
            layernorm_statistics(nc, dve, stat_step, x_all[:], xn, sq, st, 0)
            dve.wait_ge(rstd_ready.sem, 1)
            for s in range(S):
                nc.vector.tensor_tensor(xn[:, piece(s)], xn[:, piece(s)],
                                        st[:, 3, piece(s)].unsqueeze(2).broadcast_to([P, FT, D]), ALU.mult).then_inc(xn_ready.sem, 1)
            dve.wait_ge(loaded.sem, 16 * len(rest))
            lams = k["lams"]
            nc.vector.tensor_tensor(k["tmp"][:, 0:2, :], lams[:, 0:4:2, :], lams[:, 1:4:2, :], ALU.mult).then_inc(const_step.sem, 1)
            dve.wait_ge(const_step.sem, const_step.next(0))
            nc.vector.tensor_reduce(lams[:, 2, 0:2], k["tmp"][:, 0:2, :], X, ALU.add).then_inc(const_step.sem, 1)
            dve.wait_ge(const_step.sem, const_step.next(0))
            nc.vector.tensor_scalar(t32[:, 4, 0:1], k["temp"][:], CLAMP_MAX, None, ALU.min).then_inc(const_step.sem, 1)
            dve.wait_ge(const_step.sem, const_step.next(0))
            nc.vector.tensor_tensor(t32[:, 0, :], k["sim"][:], k["sim"][:], ALU.mult).then_inc(const_step.sem, 1)
            dve.wait_ge(const_step.sem, const_step.next(0))
            for s in range(S):
                dve.wait_ge(qkv_taken.sem, 3 * s + 1)
                parts(nc.vector, dve, q_step, rows_q, 0, s)
            dve.wait_ge(norm_psum.sem, 1)
            nc.vector.tensor_copy(t32[:, 1, :], ps_n[:]).then_inc(const_step.sem, 1)
            dve.wait_ge(const_step.sem, const_step.next(0))
            dve.wait_ge(norm_ready.sem, 1)
            nc.vector.tensor_scalar(t32[:, 3, :], t32[:, 2, :], 1e-12, None, ALU.max).then_inc(const_step.sem, 1)
            dve.wait_ge(const_step.sem, const_step.next(0))
            nc.vector.reciprocal(t32[:, 5, :], t32[:, 3, :]).then_inc(const_step.sem, 1)
            dve.wait_ge(const_step.sem, const_step.next(0))
            nc.vector.tensor_tensor(t32[:, 0, :], k["sim"][:], t32[:, 5, :], ALU.mult).then_inc(const_step.sem, 1)
            dve.wait_ge(const_step.sem, const_step.next(0))
            dve.wait_ge(exps_done.sem, 2)
            nc.vector.tensor_scalar(k["simn"][:], t32[:, 0, :], t32[:, 4, 1:2], None, ALU.mult).then_inc(const_step.sem, 1)
            dve.wait_ge(const_step.sem, const_step.next(0))
            nc.vector.tensor_tensor(k["tmp"][:, 3, 0:1], lams[:, 0, 0:1], lams[:, 0, 1:2], ALU.subtract).then_inc(const_step.sem, 1)
            dve.wait_ge(const_step.sem, const_step.next(0))
            nc.vector.tensor_scalar(k["lam"][:], k["tmp"][:, 3, 0:1], LAMBDA_INIT, None, ALU.add).then_inc(const_step.sem, 1)
            dve.wait_ge(const_step.sem, const_step.next(0))
            nc.vector.tensor_scalar(k["gamma8"][:], k["gamma"][:], 1.0 - LAMBDA_INIT, None, ALU.mult).then_inc(const_step.sem, 1)
            dve.wait_ge(const_step.sem, const_step.next(0))
            const_step.check()

        @block.gpsimd
        def _(pool):
            nc.gpsimd.memset(k["pw"][:], -0.5).then_inc(filled.sem, 1)
            nc.gpsimd.memset(k["ph"][:], 0.5).then_inc(filled.sem, 1)
            nc.gpsimd.memset(k["ones32"][:], 1.0).then_inc(filled.sem, 1)
            pool.wait_ge(filled.sem, 3)
            pool.wait_ge(stat_step.sem, 5)
            nc.gpsimd.tensor_tensor(st[:, 3, :], st[:, 2, :], k["pw"][:, 0:TILES], ALU.pow).then_inc(rstd_ready.sem, 1)
            for s in range(S):
                pool.wait_ge(qkv_taken.sem, 3 * s + 2)
                parts(nc.gpsimd, pool, k_step, rows_k, 1, s)
            pool.wait_ge(const_step.sem, 5)
            nc.gpsimd.tensor_tensor(t32[:, 2, :], t32[:, 1, :], k["ph"][0:PROJ, 0:E], ALU.pow).then_inc(norm_ready.sem, 1)

        @block.scalar
        def _(act):
            for name in first:
                act.dma_start(k[name][:], a[name]).then_inc(first_loaded.sem, 16)
            for name in rest[1::2]:
                act.dma_start(k[name][:], a[name]).then_inc(loaded.sem, 16)

            def copy_xnT(s):
                act.wait_ge(xnT_psum.sem, s + 1)
                nc.scalar.copy(xnT[:, cols(s)], ps_t[:, s % 2]).then_inc(xnT_ready.sem, 1)

            copy_xnT(0)
            for s in range(S):
                if s + 1 < S:
                    copy_xnT(s + 1)
                act.wait_ge(qkv_psum.sem, 3 * s + 1)
                nc.scalar.activation(qk[:, 0, cols(s)], ps_qk[:, s % 2, 0], ACT.Copy, scale=1.0 / A_HD).then_inc(qkv_taken.sem, 1)
                act.wait_ge(qkv_psum.sem, 3 * s + 2)
                nc.scalar.copy(qk[:, 1, cols(s)], ps_qk[:, s % 2, 1]).then_inc(qkv_taken.sem, 1)
                act.wait_ge(qkv_psum.sem, 3 * s + 3)
                nc.scalar.copy(v_nat[:, piece(s)], ps_v[:].rearrange("p (n d) -> p n d", n=FT)).then_inc(qkv_taken.sem, 1)
            act.wait_ge(const_step.sem, 3)
            nc.scalar.activation(k["lams"][:, 0, 0:2], k["lams"][:, 2, 0:2], ACT.Exp).then_inc(exps_done.sem, 1)
            nc.scalar.activation(t32[:, 4, 1:2], t32[:, 4, 0:1], ACT.Exp).then_inc(exps_done.sem, 1)

        @block.tensor
        def _(pe):
            def turn(s):
                pe.wait_ge(xn_ready.sem, s + 1)
                if s >= 2:
                    pe.wait_ge(xnT_ready.sem, s - 1)
                for n in range(FT):
                    last = nc.tensor.transpose(ps_t[:, s % 2, n * P:(n + 1) * P], xn[:, s * FT + n, :], k["ident"][:])
                last.then_inc(xnT_psum.sem, 1)

            pe.wait_ge(first_loaded.sem, 16 * len(first))
            turn(0)
            for s in range(S):
                if s + 1 < S:
                    turn(s + 1)
                pe.wait_ge(xnT_ready.sem, s + 1)
                for i in range(2):
                    if s >= 2:
                        pe.wait_ge(qkv_taken.sem, 3 * (s - 2) + i + 1)
                    nc.tensor.matmul(ps_qk[:, s % 2, i], k["w_attn"][:, i * D:(i + 1) * D], xnT[:, cols(s)],
                                     start=True, stop=True).then_inc(qkv_psum.sem, 1)
                if s >= 1:
                    pe.wait_ge(qkv_taken.sem, 3 * s)
                for n in range(FT):
                    last = nc.tensor.matmul(ps_v[:, n * P:(n + 1) * P], xnT[:, (s * FT + n) * P:(s * FT + n + 1) * P],
                                            k["w_attn"][:, 2 * D:3 * D], start=True, stop=True)
                last.then_inc(qkv_psum.sem, 1)
            pe.wait_ge(filled.sem, 3)
            pe.wait_ge(const_step.sem, 4)
            nc.tensor.matmul(ps_n[:], k["ones32"][:], t32[:, 0, :], start=True, stop=True).then_inc(norm_psum.sem, 1)


def layernorm_statistics(nc, dve, step, x, xn, sq, st, it):
    n = xn.shape[1]
    step.n = 0
    nc.vector.tensor_reduce(st[:, 0, :], x, X, ALU.add).then_inc(step.sem, 1)
    dve.wait_ge(step.sem, step.next(it))
    nc.vector.scalar_tensor_tensor(xn[:], st[:, 0, :].unsqueeze(2).broadcast_to([P, n, D]), -1.0 / D, x,
                                   ALU.mult, ALU.add).then_inc(step.sem, 1)
    dve.wait_ge(step.sem, step.next(it))
    nc.vector.tensor_tensor(sq[:], xn[:], xn[:], ALU.mult).then_inc(step.sem, 1)
    dve.wait_ge(step.sem, step.next(it))
    nc.vector.tensor_reduce(st[:, 1, :], sq[:], X, ALU.add).then_inc(step.sem, 1)
    dve.wait_ge(step.sem, step.next(it))
    nc.vector.tensor_scalar(st[:, 2, :], st[:, 1, :], 1.0 / D, EPS, ALU.mult, ALU.add).then_inc(step.sem, 1)


def phase_a2(nc, rows_q, rows_k, v_nat, att, k):
    JOBS = BATCH * GROUPS
    with ExitStack() as ctx:
        sb = lambda n, s, d=F32: ctx.enter_context(nc.sbuf_tensor("a2_" + n, s, d))
        sem = lambda n, per, first=0: Count(ctx.enter_context(nc.semaphore("a2_" + n)), per, first)
        rq = sb("rq", [P, 2, T], BF16)
        rk = sb("rk", [P, 2, T], BF16)
        v1 = sb("v1", [P, NT, 2, 32])
        negm = sb("negm", [P, NT, 4])
        mrows = sb("mrows", [P, NT, P], BF16)
        ex = sb("ex", [P, 4, T])
        o_sb = sb("o_sb", [P, T])
        rd = sb("rd", [P, NT, 4])
        oh = sb("oh", [P, NT, 4, A_V])
        turned = sb("turned", [P, NT, P])
        bias_parts = sb("bias_parts", [1, 3, 3 * HID], BF16)
        ps = ctx.enter_context(nc.psum_tensor("a2_ps", [P, 8, 512], F32))
        ready = sem("ready", 3)
        bias_step = sem("bias_step", 5)
        bias_moved = ctx.enter_context(nc.semaphore("a2_bias_moved"))
        units = [(t, (0, 1, 2, 3)) for t in range(4)] + [(t, hh) for t in range(4, NT) for hh in ((0, 1), (2, 3))]
        steps = [(sbk, hh) for sbk in range(NT) for hh in range(4)]
        LAG = 3
        Q_BANK, K_BANK, MAX_BANK, TURN_BANK, O_BANK = 4, 0, 0, 4, 6
        rows_psum = sem("rows_psum", 3)
        rows_sb = sem("rows_sb", 2)
        sc_psum = sem("sc_psum", len(units))
        max_done = sem("max_done", len(units))
        max_step = sem("max_step", 5)
        max_added = sem("max_added", 1)
        v1_ready = sem("v1_ready", 1)
        st_psum = sem("st_psum", len(steps))
        exp_done = sem("exp_done", len(steps))
        av_done = sem("av_done", len(steps))
        o_copied = sem("o_copied", 1, 1)
        oT_psum = sem("oT_psum", 1)
        turned_ready = sem("turned_ready", 1)
        out_step = sem("out_step", 7, 8)
        block = ctx.enter_context(nc.Block())

        def base(u):
            return 4 * ((u + 1) % 2)

        def pair(bank):
            return ps[:, bank:bank + 2, :].rearrange("p a b -> p (a b)")

        def all_jobs(eng, job):
            with eng.Fori(0, GROUPS - 1) as g:
                job(g, 0, 2 * g, (g, 1, 2 * g + 1))
                job(g, 1, 2 * g + 1, (g + 1, 0, 2 * g + 2))
            job(GROUPS - 1, 0, JOBS - 2, (GROUPS - 1, 1, JOBS - 1))
            job(GROUPS - 1, 1, JOBS - 1, None)

        @block.gpsimd
        def _(pool):
            nc.gpsimd.memset(mrows[:], 0.0).then_inc(ready.sem, 1)
            nc.gpsimd.memset(o_sb[:], 0.0).then_inc(ready.sem, 1)
            nc.gpsimd.memset(v1[:, :, :, A_V + 1:], 0.0)
            nc.gpsimd.memset(v1[:, :, :, A_V:A_V + 1], 1.0).then_inc(ready.sem, 1)
            for part in range(3):
                nc.gpsimd.tensor_copy(bias_parts[:, part, :], k["bias"][:]).then_inc(bias_step.sem, 1)
                pool.wait_ge(bias_step.sem, bias_step.next(0))
                if part < 2:
                    nc.gpsimd.tensor_tensor(k["bias"][:], k["bias"][:], bias_parts[:, part, :],
                                            ALU.subtract).then_inc(bias_step.sem, 1)
                    pool.wait_ge(bias_step.sem, bias_step.next(0))

        @block.sync
        def _(sp):
            sp.wait_ge(bias_step.sem, 5)
            for part in range(3):
                sp.dma_start(k["bias3"][part:part + 1].rearrange("p i c -> p (i c)"), bias_parts[:, part, :]).then_inc(bias_moved, 16)
            sp.wait_ge(bias_moved, 48)

        @block.tensor
        def _(pe):
            pe.wait_ge(ready.sem, 3)

            def spread(g, b, it, sel, rows, bank):
                for half in range(2):
                    for part in range(3):
                        last = nc.tensor.matmul(ps[:, bank + half, :], sel[:, part, bass.ds(g * P, P)],
                                                rows[:, part, b * T + half * 512:b * T + half * 512 + 512],
                                                start=part == 0, stop=part == 2)
                last.then_inc(rows_psum.sem, 1)

            def maxima_scores(b, it):
                pe.wait_ge(rows_sb.sem, rows_sb.at(it, 2))
                for u, (t, heads) in enumerate(units):
                    if u >= 2:
                        pe.wait_ge(max_done.sem, max_done.at(it, u - 1))
                    n = (t + 1) * P
                    banks = {hh: base(u) + i * (4 // len(heads)) for i, hh in enumerate(heads)}
                    for c in range(0, n, 512):
                        w = min(512, n - c)
                        for hh in heads:
                            r = slice(32 * hh, 32 * hh + 32)
                            nc.tensor.matmul(ps[:, banks[hh] + c // 512, 0:w], rq[r, b, t * P:(t + 1) * P], rk[r, b, c:c + w],
                                             start=True, stop=c + w < n)
                    c = t * P
                    for hh in heads:
                        last = nc.tensor.matmul(ps[:, banks[hh] + c // 512, c % 512:c % 512 + P], k["ident_b"][:], k["mask"][:],
                                                start=False, stop=True)
                    last.then_inc(sc_psum.sem, 1)

            def turn(it):
                pe.wait_ge(o_copied.sem, o_copied.at(it, 0))
                if not (isinstance(it, int) and it == JOBS):
                    pe.wait_ge(max_done.sem, max_done.at(it, len(units) - 1))
                for t in range(NT):
                    last = nc.tensor.transpose(ps[:, TURN_BANK + t // 4, t % 4 * P:(t % 4 + 1) * P], o_sb[:, t * P:(t + 1) * P],
                                               k["ident"][:])
                last.then_inc(oT_psum.sem, 1)

            def maxima_rows(it):
                pe.wait_ge(max_step.sem, max_step.at(it, 5))
                for t in range(NT):
                    last = nc.tensor.matmul(ps[:, MAX_BANK + t // 4, t % 4 * P:(t % 4 + 1) * P], mrows[:, t, :], k["ident_b"][:],
                                            start=True, stop=True)
                last.then_inc(rows_psum.sem, 1)

            def scores(b, it, n):
                sbk, hh = steps[n]
                if n == 0:
                    pe.wait_ge(max_added.sem, max_added.at(it, 1))
                if n >= 3:
                    pe.wait_ge(exp_done.sem, exp_done.at(it, n - 2))
                r = slice(32 * hh, 32 * hh + 32)
                width = T - sbk * P
                bank = 2 * (n % 3)
                for c in range(0, width, 512):
                    w = min(512, width - c)
                    last = nc.tensor.matmul(ps[:, bank + c // 512, 0:w], rk[r, b, sbk * P:(sbk + 1) * P],
                                            rq[r, b, sbk * P + c:sbk * P + c + w], start=True, stop=c > 0)
                    if c == 0:
                        last = nc.tensor.matmul(ps[:, bank, 0:P], k["ident_b"][:], k["mask_t"][:], start=False, stop=True)
                last.then_inc(st_psum.sem, 1)

            def values(it, n):
                sbk, hh = steps[n]
                if n == 0:
                    pe.wait_ge(v1_ready.sem, v1_ready.at(it, 1))
                pe.wait_ge(exp_done.sem, exp_done.at(it, n + 1))
                t0 = sbk * P
                for lo, hi in ((0, 512), (512, T)):
                    lo = max(lo, t0)
                    if lo < hi:
                        last = nc.tensor.matmul(ps[32 * hh:32 * hh + 32, O_BANK + lo // 512, lo % 512:(hi - 1) % 512 + 1],
                                                v1[:, sbk, hh // 2, :], ex[:, n % 4, lo - t0:hi - t0],
                                                start=sbk == 0, stop=sbk == (3 if hi == 512 else NT - 1))
                last.then_inc(av_done.sem, 1)

            def job(g, b, it, following):
                maxima_scores(b, it)
                maxima_rows(it)
                turn(it)
                for n in range(len(steps)):
                    if 2 * (n % 3) == TURN_BANK and n < 3:
                        pe.wait_ge(turned_ready.sem, turned_ready.at(it, 1))
                    scores(b, it, n)
                    if n >= LAG:
                        values(it, n - LAG)
                for n in range(len(steps) - LAG, len(steps)):
                    values(it, n)
                if following:
                    spread(*following, k["sel_q"], rows_q, Q_BANK)
                    spread(*following, k["sel_k"], rows_k, K_BANK)
            spread(0, 0, 0, k["sel_q"], rows_q, Q_BANK)
            spread(0, 0, 0, k["sel_k"], rows_k, K_BANK)
            assert base(len(units) - 1) != TURN_BANK == base(len(units) - 2)
            all_jobs(pe, job)
            turn(JOBS)

        @block.scalar
        def _(act):
            def rows(b, it):
                act.wait_ge(rows_psum.sem, rows_psum.at(it, 1))
                nc.scalar.copy(rq[:, b, :], pair(Q_BANK)).then_inc(rows_sb.sem, 1)
                act.wait_ge(rows_psum.sem, rows_psum.at(it, 2))
                nc.scalar.activation(rk[:, b, :], pair(K_BANK), ACT.Identity, bias=k["one_rows"][:]).then_inc(rows_sb.sem, 1)

            def take_turned(it):
                act.wait_ge(oT_psum.sem, oT_psum.at(it, 1))
                act.wait_ge(out_step.sem, out_step.at(it - 1, 0))
                nc.scalar.copy(turned[:].rearrange("p n c -> p (n c)"), pair(TURN_BANK)).then_inc(turned_ready.sem, 1)

            def job(g, b, it, following):
                for n, (sbk, hh) in enumerate(steps):
                    act.wait_ge(st_psum.sem, st_psum.at(it, n + 1))
                    if n >= 4:
                        act.wait_ge(av_done.sem, av_done.at(it, n - 3))
                    width = T - sbk * P
                    nc.scalar.activation(ex[:, n % 4, 0:width], pair(2 * (n % 3))[:, 0:width], ACT.Exp).then_inc(exp_done.sem, 1)
                    if n == 0:
                        take_turned(it)
                act.wait_ge(av_done.sem, av_done.at(it, len(steps)))
                nc.scalar.copy(o_sb[:], pair(O_BANK)).then_inc(o_copied.sem, 1)
                if following:
                    rows(*following[1:])

            act.sem_inc(o_copied.sem, 1)
            rows(0, 0)
            all_jobs(act, job)
            take_turned(JOBS)

        @block.vector
        def _(dve):
            dve.wait_ge(ready.sem, 3)
            dve.sem_inc(out_step.sem, out_step.first)

            def maxima(g, b, it, first=False):
                if not first:
                    dve.wait_ge(av_done.sem, av_done.at(it, 0))
                nc.vector.tensor_copy(
                    v1[:, :, :, 0:A_V],
                    v_nat[:, b * NT:(b + 1) * NT, bass.ds(g * 2 * A_V, 2 * A_V)].rearrange("p n (v c) -> p n v c", v=2)
                ).then_inc(v1_ready.sem, 1)
                for u, (t, heads) in enumerate(units):
                    dve.wait_ge(sc_psum.sem, sc_psum.at(it, u + 1))
                    n = (t + 1) * P
                    src = ps[:, base(u):base(u) + 4, :].rearrange("p (h a) c -> p h (a c)", h=len(heads))[:, :, 0:n]
                    nc.vector.tensor_reduce(negm[:, t, heads[0]:heads[-1] + 1], src, X, ALU.max, negate=True).then_inc(max_done.sem, 1)
                dve.wait_ge(max_done.sem, max_done.at(it, len(units)))
                max_step.n = 0
                for part in range(3):
                    dst = mrows[:].rearrange("p n (h r) -> p n h r", h=4)[:, :, :, M_ROW + part]
                    nc.vector.tensor_copy(dst, negm[:]).then_inc(max_step.sem, 1)
                    dve.wait_ge(max_step.sem, max_step.next(it))
                    if part < 2:
                        nc.vector.tensor_tensor(negm[:], negm[:], dst, ALU.subtract).then_inc(max_step.sem, 1)
                        dve.wait_ge(max_step.sem, max_step.next(it))
                max_step.check()
                dve.wait_ge(rows_psum.sem, rows_psum.at(it, 3))
                nc.vector.tensor_tensor(rq[:, b, :], rq[:, b, :], pair(MAX_BANK), ALU.add).then_inc(max_added.sem, 1)

            def normalise(g, b, it):
                dve.wait_ge(turned_ready.sem, turned_ready.at(it + 1, 1))
                out_step.n = 0
                o4 = turned[:].rearrange("p n (h c) -> p n h c", h=4)
                nc.vector.reciprocal(rd[:], o4[:, :, :, A_V]).then_inc(out_step.sem, 1)
                dve.wait_ge(out_step.sem, out_step.next(it))
                sub1 = rd[:].rearrange("p n (v s) -> p n v s", s=2)[:, :, :, 1]
                nc.vector.tensor_scalar(sub1, sub1, k["lam"][:], None, ALU.mult).then_inc(out_step.sem, 1)
                dve.wait_ge(out_step.sem, out_step.next(it))
                for n in range(0, NT, 2):
                    nc.vector.tensor_tensor(oh[:, n:n + 2], o4[:, n:n + 2, :, 0:A_V],
                                            rd[:, n:n + 2].unsqueeze(3).broadcast_to([P, 2, 4, A_V]),
                                            ALU.mult).then_inc(out_step.sem, 1)
                    dve.wait_ge(out_step.sem, out_step.next(it))
                oh5 = oh[:].rearrange("p n (v s) c -> p n v s c", s=2)
                dst = att[:, b * NT:(b + 1) * NT, bass.ds(g * 2 * A_V, 2 * A_V)].rearrange("p n (v c) -> p n v c", v=2)
                nc.vector.tensor_tensor(dst, oh5[:, :, :, 0, :], oh5[:, :, :, 1, :], ALU.subtract).then_inc(out_step.sem, 1)
                dve.wait_ge(out_step.sem, out_step.next(it))
                out_step.check()

            def job(g, b, it, following):
                if following:
                    maxima(*following)
                normalise(g, b, it)

            maxima(0, 0, 0, True)
            all_jobs(dve, job)


def phase_a3(nc, x_all, att, w_proj, ident, gamma8):
    S = TILES // FT
    HV = D // A_V
    with ExitStack() as ctx:
        sb = lambda n, s, d=F32: ctx.enter_context(nc.sbuf_tensor("a3_" + n, s, d))
        sem = lambda n, per: Count(ctx.enter_context(nc.semaphore("a3_" + n)), per)
        sq = sb("sq", [P, TILES * HV, A_V])
        ms = sb("ms", [P, 4, TILES * HV])
        nrm = sb("nrm", [P, TILES * HV, A_V])
        nT = sb("nT", [P, TILES * P])
        ps_t = ctx.enter_context(nc.psum_tensor("a3_ps_t", [P, TILES * P], F32))
        ps_o = ctx.enter_context(nc.psum_tensor("a3_ps_o", [P, TILES, D], F32))
        stat_step = sem("stat_step", 4)
        root_ready = sem("root_ready", 1)
        scaled = sem("scaled", 2 * S)
        nT_psum = sem("nT_psum", S)
        nT_ready = sem("nT_ready", S)
        o_psum = sem("o_psum", S)
        added = sem("added", S)
        block = ctx.enter_context(nc.Block())
        piece = lambda s: slice(s * FT, (s + 1) * FT)
        heads = lambda s: slice(s * FT * HV, (s + 1) * FT * HV)
        cols = lambda s: slice(s * FT * P, (s + 1) * FT * P)

        @block.vector
        def _(dve):
            a = att[:].rearrange("p n (h c) -> p (n h) c", c=A_V)
            nc.vector.tensor_tensor(sq[:], a, a, ALU.mult).then_inc(stat_step.sem, 1)
            dve.wait_ge(stat_step.sem, 1)
            nc.vector.tensor_reduce(ms[:, 0, :], sq[:], X, ALU.add).then_inc(stat_step.sem, 1)
            dve.wait_ge(stat_step.sem, 2)
            nc.vector.tensor_scalar(ms[:, 1, :], ms[:, 0, :], 1.0 / A_V, EPS, ALU.mult, ALU.add).then_inc(stat_step.sem, 1)
            dve.wait_ge(root_ready.sem, 1)
            nc.vector.reciprocal(ms[:, 3, :], ms[:, 2, :]).then_inc(stat_step.sem, 1)
            dve.wait_ge(stat_step.sem, 4)
            for s in range(S):
                nc.vector.tensor_tensor(nrm[:, heads(s)], a[:, heads(s)],
                                        ms[:, 3, heads(s)].unsqueeze(2).broadcast_to([P, FT * HV, A_V]), ALU.mult).then_inc(scaled.sem, 1)
                dve.wait_ge(scaled.sem, 2 * s + 1)
                nc.vector.tensor_tensor(nrm[:, heads(s)], nrm[:, heads(s)],
                                        gamma8[:].unsqueeze(1).broadcast_to([P, FT * HV, A_V]), ALU.mult).then_inc(scaled.sem, 1)
            for s in range(S):
                dve.wait_ge(o_psum.sem, s + 1)
                nc.vector.tensor_tensor(x_all[:, piece(s)], ps_o[:, piece(s)], x_all[:, piece(s)], ALU.add).then_inc(added.sem, 1)
            dve.wait_ge(added.sem, S)

        @block.scalar
        def _(act):
            act.wait_ge(stat_step.sem, 3)
            nc.scalar.activation(ms[:, 2, :], ms[:, 1, :], ACT.Sqrt).then_inc(root_ready.sem, 1)
            for s in range(S):
                act.wait_ge(nT_psum.sem, s + 1)
                nc.scalar.copy(nT[:, cols(s)], ps_t[:, cols(s)]).then_inc(nT_ready.sem, 1)

        @block.tensor
        def _(pe):
            for s in range(S):
                pe.wait_ge(scaled.sem, 2 * s + 2)
                for n in range(s * FT, (s + 1) * FT):
                    last = nc.tensor.transpose(ps_t[:, n * P:(n + 1) * P],
                                               nrm[:, n * HV:(n + 1) * HV, :].rearrange("p h c -> p (h c)"), ident[:])
                last.then_inc(nT_psum.sem, 1)
            for s in range(S):
                pe.wait_ge(nT_ready.sem, s + 1)
                for n in range(s * FT, (s + 1) * FT):
                    last = nc.tensor.matmul(ps_o[:, n, :], nT[:, n * P:(n + 1) * P], w_proj[:], start=True, stop=True)
                last.then_inc(o_psum.sem, 1)


def phase_f(nc, tag, x_all, k, out_dram):
    S = TILES // FT
    with ExitStack() as ctx:
        sb = lambda n, s, d=F32: ctx.enter_context(nc.sbuf_tensor(f"{tag}_{n}", s, d))
        sem = lambda n, per: Count(ctx.enter_context(nc.semaphore(f"{tag}_{n}")), per)
        xn = sb("xn", [P, TILES, D])
        sq = sb("sq", [P, TILES, D])
        st = sb("st", [P, 4, TILES])
        xnT = sb("xnT", [P, TILES * P])
        pr = sb("pr", [PROJ, 2, TILES * P])
        lg = sb("lg", [P, TILES, 8])
        g = sb("g", [P, 6, TILES, E])
        r1 = sb("r1", [P, 8, TILES])
        down = sb("down", [P, TILES, E, R_PAD])
        downT = sb("downT", [E * R_PAD, TILES * P])
        ps_a = ctx.enter_context(nc.psum_tensor(f"{tag}_ps_a", [P, TILES * P], F32))
        ps_b = ctx.enter_context(nc.psum_tensor(f"{tag}_ps_b", [P, TILES * P], F32))
        ps_d = ps_a[:, 0:TILES * E * R_PAD].rearrange("p (n c) -> p n c", n=TILES)
        ps_l = ps_a[:, 512:512 + TILES * 8].rearrange("p (n c) -> p n c", n=TILES)
        ps_o = ps_b[:].rearrange("p (n c) -> p n c", n=TILES)
        assert TILES * E * R_PAD <= 512
        stat_step = sem("stat_step", 5)
        rstd_ready = sem("rstd_ready", 1)
        xn_ready = sem("xn_ready", S)
        xnT_psum = sem("xnT_psum", S)
        xnT_ready = sem("xnT_ready", S)
        p_psum = sem("p_psum", S)
        pr_ready = sem("pr_ready", 2 * S)
        d_psum = sem("d_psum", 1)
        l_psum = sem("l_psum", 1)
        route_step = sem("route_step", 15)
        norm_ready = sem("norm_ready", 1)
        exp_done = sem("exp_done", 1)
        chosen = sem("chosen", 1)
        dT_psum = sem("dT_psum", S)
        dT_ready = sem("dT_ready", S)
        o_psum = sem("o_psum", S)
        added = sem("added", S)
        stored = ctx.enter_context(nc.semaphore(f"{tag}_stored"))
        block = ctx.enter_context(nc.Block())
        piece = lambda s: slice(s * FT, (s + 1) * FT)
        cols = lambda s: slice(s * FT * P, (s + 1) * FT * P)
        tile = lambda n: slice(n * P, (n + 1) * P)

        @block.vector
        def _(dve):
            row = lambda i: r1[:, i, :]
            bc = lambda i: r1[:, i, :].unsqueeze(2).broadcast_to([P, TILES, E])
            layernorm_statistics(nc, dve, stat_step, x_all[:], xn, sq, st, 0)
            dve.wait_ge(rstd_ready.sem, 1)
            for s in range(S):
                nc.vector.tensor_tensor(xn[:, piece(s)], xn[:, piece(s)],
                                        st[:, 3, piece(s)].unsqueeze(2).broadcast_to([P, FT, D]), ALU.mult).then_inc(xn_ready.sem, 1)
            for s in range(S):
                dve.wait_ge(p_psum.sem, s + 1)
                nc.vector.tensor_scalar(pr[:, 0, cols(s)], ps_b[0:PROJ, cols(s)], k["bp"][:], None, ALU.add).then_inc(pr_ready.sem, 1)
                dve.wait_ge(pr_ready.sem, 2 * s + 1)
                nc.vector.tensor_tensor(pr[:, 1, cols(s)], pr[:, 0, cols(s)], pr[:, 0, cols(s)], ALU.mult).then_inc(pr_ready.sem, 1)
            dve.wait_ge(l_psum.sem, 1)
            nc.vector.tensor_copy(lg[:, :, 0:E + 1], ps_l[:, :, 0:E + 1]).then_inc(route_step.sem, 1)
            dve.wait_ge(route_step.sem, route_step.next(0))
            dve.wait_ge(norm_ready.sem, 1)
            nc.vector.tensor_scalar(row(0), row(7), 1e-12, None, ALU.max).then_inc(route_step.sem, 1)
            dve.wait_ge(route_step.sem, route_step.next(0))
            nc.vector.reciprocal(row(1), row(0)).then_inc(route_step.sem, 1)
            dve.wait_ge(route_step.sem, route_step.next(0))
            nc.vector.tensor_tensor(g[:, 0], lg[:, :, 0:E], bc(1), ALU.mult).then_inc(route_step.sem, 1)
            dve.wait_ge(route_step.sem, route_step.next(0))
            nc.vector.tensor_reduce(row(2), g[:, 0], X, ALU.max).then_inc(route_step.sem, 1)
            dve.wait_ge(route_step.sem, route_step.next(0))
            nc.vector.tensor_tensor(g[:, 1], g[:, 0], bc(2), ALU.subtract).then_inc(route_step.sem, 1)
            dve.wait_ge(exp_done.sem, 1)
            route_step.next(0)
            nc.vector.tensor_reduce(row(3), g[:, 2], X, ALU.add).then_inc(route_step.sem, 1)
            dve.wait_ge(route_step.sem, route_step.next(0))
            nc.vector.reciprocal(row(4), row(3)).then_inc(route_step.sem, 1)
            dve.wait_ge(route_step.sem, route_step.next(0))
            nc.vector.tensor_tensor(g[:, 3], g[:, 2], bc(4), ALU.mult).then_inc(route_step.sem, 1)
            dve.wait_ge(route_step.sem, route_step.next(0))
            nc.vector.tensor_reduce(row(5), g[:, 3], X, ALU.max).then_inc(route_step.sem, 1)
            dve.wait_ge(route_step.sem, route_step.next(0))
            nc.vector.tensor_tensor(g[:, 4], g[:, 3], bc(5), ALU.is_equal).then_inc(route_step.sem, 1)
            dve.wait_ge(route_step.sem, route_step.next(0))
            nc.vector.tensor_tensor(g[:, 5], g[:, 4], k["rank4"][:].unsqueeze(1).broadcast_to([P, TILES, E]), ALU.mult).then_inc(route_step.sem, 1)
            dve.wait_ge(route_step.sem, route_step.next(0))
            nc.vector.tensor_reduce(row(6), g[:, 5], X, ALU.max).then_inc(route_step.sem, 1)
            dve.wait_ge(route_step.sem, route_step.next(0))
            nc.vector.tensor_tensor(g[:, 4], g[:, 5], bc(6), ALU.is_equal).then_inc(route_step.sem, 1)
            dve.wait_ge(route_step.sem, route_step.next(0))
            nc.vector.tensor_tensor(g[:, 5], g[:, 4], g[:, 3], ALU.mult).then_inc(route_step.sem, 1)
            dve.wait_ge(route_step.sem, route_step.next(0))
            route_step.check()
            nc.vector.tensor_tensor(down[:].rearrange("p n e r -> p (n e) r"),
                                    ps_d.rearrange("p n (e r) -> p (n e) r", e=E),
                                    g[:, 5].rearrange("p n e -> p (n e)").unsqueeze(2)
                                    .broadcast_to([P, TILES * E, R_PAD]), ALU.mult).then_inc(chosen.sem, 1)
            for s in range(S):
                dve.wait_ge(o_psum.sem, s + 1)
                nc.vector.tensor_tensor(x_all[:, piece(s)], ps_o[:, piece(s)], x_all[:, piece(s)], ALU.add).then_inc(added.sem, 1)
            dve.wait_ge(added.sem, S)

        @block.gpsimd
        def _(pool):
            pool.wait_ge(stat_step.sem, 5)
            nc.gpsimd.tensor_tensor(st[:, 3, :], st[:, 2, :], k["pw"][:, 0:TILES], ALU.pow).then_inc(rstd_ready.sem, 1)
            pool.wait_ge(route_step.sem, 1)
            nc.gpsimd.tensor_tensor(r1[:, 7, :], lg[:, :, E], k["ph"][:, 0:TILES], ALU.pow).then_inc(norm_ready.sem, 1)

        @block.scalar
        def _(act):
            for s in range(S):
                act.wait_ge(xnT_psum.sem, s + 1)
                nc.scalar.copy(xnT[:, cols(s)], ps_a[:, cols(s)]).then_inc(xnT_ready.sem, 1)
            act.wait_ge(route_step.sem, 6)
            nc.scalar.activation(g[:, 2], g[:, 1], ACT.Exp).then_inc(exp_done.sem, 1)
            for s in range(S):
                act.wait_ge(dT_psum.sem, s + 1)
                nc.scalar.copy(downT[:, cols(s)], ps_a[0:E * R_PAD, cols(s)]).then_inc(dT_ready.sem, 1)

        @block.tensor
        def _(pe):
            for s in range(S):
                pe.wait_ge(xn_ready.sem, s + 1)
                for n in range(s * FT, (s + 1) * FT):
                    last = nc.tensor.transpose(ps_a[:, tile(n)], xn[:, n, :], k["ident"][:])
                last.then_inc(xnT_psum.sem, 1)
            for s in range(S):
                pe.wait_ge(xnT_ready.sem, s + 1)
                nc.tensor.matmul(ps_b[0:PROJ, cols(s)], k["wpT"][:], xnT[:, cols(s)], start=True, stop=True).then_inc(p_psum.sem, 1)
            for n in range(TILES):
                nc.tensor.matmul(ps_d[:, n, :], xnT[:, tile(n)], k["wdT"][:], start=True, stop=True)
            for n in range(TILES):
                if n % FT == 0:
                    pe.wait_ge(pr_ready.sem, 2 * (n // FT) + 2)
                nc.tensor.matmul(ps_l[:, n, 0:E], pr[:, 0, tile(n)], k["simn"][:], start=True, stop=True)
                last = nc.tensor.matmul(ps_l[:, n, E:E + 1], pr[:, 1, tile(n)], k["ones32"][:, 0:1], start=True, stop=True)
            last.then_inc(l_psum.sem, 1)
            for n in range(TILES):
                nc.tensor.matmul(ps_o[:, n, :], xnT[:, tile(n)], k["wT"][:], start=n % FT == 0, stop=False)
            pe.wait_ge(chosen.sem, 1)
            for s in range(S):
                for n in range(s * FT, (s + 1) * FT):
                    last = nc.tensor.transpose(ps_a[0:E * R_PAD, tile(n)], down[:, n].rearrange("p e r -> p (e r)"), k["ident"][:])
                last.then_inc(dT_psum.sem, 1)
            for s in range(S):
                pe.wait_ge(dT_ready.sem, s + 1)
                for n in range(s * FT, (s + 1) * FT):
                    last = nc.tensor.matmul(ps_o[:, n, :], downT[:, tile(n)], k["wu"][:], start=False, stop=n % FT == FT - 1)
                last.then_inc(o_psum.sem, 1)

        if out_dram is not None:
            @block.sync
            def _(sp):
                for s in range(S):
                    sp.wait_ge(added.sem, s + 1)
                    sp.dma_start(out_dram[:, piece(s), :], x_all[:, piece(s), :]).then_inc(stored, 16)
                sp.wait_ge(stored, 16 * S)


def phase_b(nc, x_all, k):
    with ExitStack() as ctx:
        sb = lambda n, s, d=F32: ctx.enter_context(nc.sbuf_tensor("b_" + n, s, d))
        sem = lambda n, per: Count(ctx.enter_context(nc.semaphore("b_" + n)), per)
        xn = sb("xn", [P, 1, D])
        sq = sb("sq", [P, 1, D])
        st = sb("st", [P, 4, 1])
        xnT = sb("xnT", [P, P])
        q = sb("q", [P, 2, H, C])
        key = sb("key", [P, 2, H, C])
        val = sb("val", [P, 2, H, C])
        m = sb("m", [P, 2, H, C])
        kmin = sb("kmin", [P, H, C])
        sums = sb("sums", [P, 2, H, C])
        osum = sb("osum", [P, 1, D])
        p_ring = sb("p_ring", [P, P_RING // 2, H * JB * (C + JB)])
        ev_ring = sb("ev_ring", [P, EV_RING // 2, H * JB * (C + JB)])
        oT = sb("oT", [P, HID])
        acc = ctx.enter_context(nc.psum_tensor("b_acc", [P, 2, 4, H, C // 2], F32))
        stages = acc[:].rearrange("p b n h i -> p b n (h i)")
        xn_step = sem("xn_step", 6)
        m_step = sem("m_step", 5)
        sums_taken = sem("sums_taken", 2)
        divided = sem("divided", 2)
        x_step = sem("x_step", 2)
        rstd_ready = sem("rstd_ready", 1)
        xnT_psum = sem("xnT_psum", 1)
        xnT_ready = sem("xnT_ready", 1)
        qkv_psum = sem("qkv_psum", 3)
        qkv_taken = sem("qkv_taken", 3)
        product = sem("product", 2 * CHUNKS)
        shifted = sem("shifted", CHUNKS)
        exp_done = sem("exp_done", CHUNKS)
        ev_dve = sem("ev_dve", CHUNKS)
        ev_pool = sem("ev_pool", CHUNKS)
        folded = sem("folded", len(FOLD_EV) + len(FOLD_P))
        summed = sem("summed", CHUNKS)
        oT_psum = sem("oT_psum", 1)
        oT_ready = sem("oT_ready", 1)
        o_psum = sem("o_psum", 1)
        block = ctx.enter_context(nc.Block())
        DH = H - POOL_HEADS

        def all_tiles(eng, tile):
            tile(0, 0, True, False)
            with eng.Fori(0, (TILES - 2) // 2) as u:
                tile(2 * u + 1, 1, False, False)
                tile(2 * u + 2, 0, False, False)
            tile(TILES - 1, 1, False, True)

        def chunk_flat(ring, at):
            start = at % 2 * H * JB * (C - JB * ORDER[at - at % 2])
            return ring[:, at // 2 % ring.shape[1], start:start + H * JB * (C - JB * ORDER[at])]

        def chunk(ring, at):
            return chunk_flat(ring, at).rearrange("p (h j i) -> p h j i", h=H, j=JB)

        def freed(it, at, ring_size):
            return summed.at(it, at - ring_size + 1 + (at < ring_size and at % 2 == 0))

        def keys(t, buf, at, h=slice(0, H)):
            c = ORDER[at]
            n = C - JB * c
            return t[:, buf, h, JB * c:JB * c + JB].unsqueeze(3).broadcast_to([P, t[:, buf, h].shape[1], JB, n])

        def queries(t, buf, at):
            c = ORDER[at]
            n = C - JB * c
            return t[:, buf, :, JB * c:C].unsqueeze(2).broadcast_to([P, H, JB, n])

        def flat(t, buf):
            return t[:, buf].rearrange("p h c -> p (h c)")

        def folds_until(at):
            return sum((c in FOLD_EV) + (c in FOLD_P) for c in ORDER[:at + 1])

        def ahead_of(it, buf, last, c, lag):
            if c + lag < CHUNKS:
                return it, buf, c + lag
            return None if last else (it + 1, 1 - buf, c + lag - CHUNKS)

        @block.vector
        def _(dve):
            def multiply(it, buf, c, first):
                if c >= P_RING or not first:
                    dve.wait_ge(summed.sem, freed(it, c, P_RING))
                pc = chunk(p_ring, c)
                nc.vector.tensor_tensor(pc, queries(q, buf, c), keys(key, buf, c), ALU.mult).then_inc(product.sem, 1)

            def mask(it, c):
                dve.wait_ge(product.sem, product.at(it, 2 * c + 1))
                nc.vector.memset(chunk(p_ring, c)[:, :, 1, 0:1], MASKED).then_inc(product.sem, 1)

            def fold(it, c):
                if ORDER[c] in FOLD_EV or ORDER[c] in FOLD_P:
                    dve.wait_ge(ev_dve.sem, ev_dve.at(it, c + 1))
                    dve.wait_ge(ev_pool.sem, ev_pool.at(it, c + 1))
                for ring, which in ((ev_ring, FOLD_EV), (p_ring, FOLD_P)):
                    if ORDER[c] in which:
                        t = chunk(ring, c)
                        nc.vector.tensor_tensor(t[:, :, 0], t[:, :, 0], t[:, :, 1], ALU.add).then_inc(folded.sem, 1)

            def norm(it):
                layernorm_statistics(nc, dve, xn_step, x_all[:, bass.ds(it, 1), :], xn, sq, st, it)

            def scale(it):
                dve.wait_ge(rstd_ready.sem, rstd_ready.at(it, 1))
                nc.vector.tensor_tensor(xn[:], xn[:], st[:, 3, :].unsqueeze(2).broadcast_to([P, 1, D]), ALU.mult).then_inc(xn_step.sem, 1)

            def maxima(it, buf, part):
                if part == 0:
                    dve.wait_ge(qkv_taken.sem, qkv_taken.at(it, 2))
                    nc.vector.tensor_tensor_scan(flat(m, buf), k["reset_max"][:], flat(key, buf), 0.0,
                                                 ALU.min, ALU.max).then_inc(m_step.sem, 1)
                elif part == 1:
                    nc.vector.tensor_tensor_scan(kmin[:].rearrange("p h c -> p (h c)"), k["reset_min"][:], flat(key, buf), 0.0,
                                                 ALU.max, ALU.min).then_inc(m_step.sem, 1)
                else:
                    dve.wait_ge(m_step.sem, m_step.at(it, 2))
                    nc.vector.tensor_tensor(m[:, buf], m[:, buf], q[:, buf], ALU.mult).then_inc(m_step.sem, 1)
                    nc.vector.tensor_tensor(kmin[:], kmin[:], q[:, buf], ALU.mult).then_inc(m_step.sem, 1)
                    dve.wait_ge(m_step.sem, m_step.at(it, 4))
                    nc.vector.tensor_tensor(m[:, buf], m[:, buf], kmin[:], ALU.max).then_inc(m_step.sem, 1)
                    dve.wait_ge(m_step.sem, m_step.at(it, 5))

            def divide(it):
                dve.wait_ge(sums_taken.sem, sums_taken.at(it, 2))
                nc.vector.reciprocal(sums[:, 1], sums[:, 1]).then_inc(divided.sem, 1)
                dve.wait_ge(divided.sem, divided.at(it, 1))
                nc.vector.tensor_tensor(sums[:, 0], sums[:, 0], sums[:, 1], ALU.mult).then_inc(divided.sem, 1)

            def residual(it, buf):
                dve.wait_ge(o_psum.sem, o_psum.at(it, 1))
                nc.vector.tensor_tensor(osum[:, 0, :], stages[:, buf, 2, 0:D], k["bo"][:], ALU.add).then_inc(x_step.sem, 1)
                dve.wait_ge(x_step.sem, x_step.at(it, 1))
                xs = x_all[:, bass.ds(it, 1), :]
                nc.vector.tensor_tensor(xs, xs, osum[:], ALU.add).then_inc(x_step.sem, 1)

            def tile(it, buf, first, last):
                for c in range(CHUNKS):
                    coming = ahead_of(it, buf, last, c, MULTIPLY_AHEAD)
                    if coming:
                        multiply(*coming, first and c + MULTIPLY_AHEAD < CHUNKS)
                    pc, ev = chunk(p_ring, c), chunk(ev_ring, c)
                    if c == 0:
                        dve.wait_ge(qkv_taken.sem, qkv_taken.at(it, 3))
                    dve.wait_ge(exp_done.sem, exp_done.at(it, c + 1))
                    if c >= EV_RING or not first:
                        dve.wait_ge(summed.sem, freed(it, c, EV_RING))
                    nc.vector.tensor_tensor(ev[:, 0:DH], pc[:, 0:DH], keys(val, buf, c, slice(0, DH)),
                                            ALU.mult).then_inc(ev_dve.sem, 1)
                    if coming:
                        mask(coming[0], coming[2])
                    if c > 0:
                        fold(it, c - 1)
                    if not first and c == DIVIDE_AT:
                        divide(it - 1)
                    if not first and c == RESIDUAL_AT:
                        residual(it - 1, 1 - buf)
                    if last:
                        continue
                    if c == NORM_AT:
                        norm(it + 1)
                    if c == SCALE_AT:
                        scale(it + 1)
                    if c in MAX_AT:
                        maxima(it + 1, 1 - buf, MAX_AT.index(c))
                fold(it, CHUNKS - 1)

            norm(0)
            scale(0)
            for part in range(3):
                maxima(0, 0, part)
            for c in range(MULTIPLY_AHEAD):
                multiply(0, 0, c, True)
                mask(0, c)
            all_tiles(dve, tile)
            divide(TILES - 1)
            residual(TILES - 1, 1)

        @block.gpsimd
        def _(pool):
            def root(it):
                pool.wait_ge(xn_step.sem, xn_step.at(it, 5))
                nc.gpsimd.tensor_tensor(st[:, 3, :], st[:, 2, :], k["pw"][:, 0:1], ALU.pow).then_inc(rstd_ready.sem, 1)

            def shift(it, buf, c):
                pool.wait_ge(product.sem, product.at(it, 2 * c + 2))
                pc = chunk(p_ring, c)
                nc.gpsimd.tensor_tensor(pc, pc, queries(m, buf, c), ALU.subtract).then_inc(shifted.sem, 1)

            def tile(it, buf, first, last):
                for c in range(CHUNKS):
                    coming = ahead_of(it, buf, last, c, SHIFT_AHEAD)
                    if coming:
                        shift(*coming)
                    pool.wait_ge(exp_done.sem, exp_done.at(it, c + 1))
                    if c >= EV_RING or not first:
                        pool.wait_ge(summed.sem, freed(it, c, EV_RING))
                    pc, ev = chunk(p_ring, c), chunk(ev_ring, c)
                    nc.gpsimd.tensor_tensor(ev[:, DH:H], pc[:, DH:H], keys(val, buf, c, slice(DH, H)),
                                            ALU.mult).then_inc(ev_pool.sem, 1)
                    if not last and c == ROOT_AT:
                        root(it + 1)

            root(0)
            for c in range(SHIFT_AHEAD):
                shift(0, 0, c)
            all_tiles(pool, tile)

        @block.scalar
        def _(act):
            def copy_xnT(it, buf):
                act.wait_ge(xnT_psum.sem, xnT_psum.at(it, 1))
                nc.scalar.copy(xnT[:], stages[:, buf, 0, 0:P]).then_inc(xnT_ready.sem, 1)

            def take(it, buf, i):
                act.wait_ge(qkv_psum.sem, qkv_psum.at(it, i + 1))
                src = stages[:, buf, 2 * (i % 2):2 * (i % 2) + 2, :].rearrange("p a b -> p (a b)")
                nc.scalar.activation(flat((q, key, val)[i], buf), src, ACT.Copy,
                                     scale=0.125 if i == 0 else 1.0).then_inc(qkv_taken.sem, 1)

            def copy_oT(it, buf):
                act.wait_ge(oT_psum.sem, oT_psum.at(it, 1))
                nc.scalar.copy(oT[:], stages[:, buf, 0:2, :].rearrange("p a b -> p (a b)")).then_inc(oT_ready.sem, 1)

            def take_sums(it, buf):
                act.wait_ge(summed.sem, summed.at(it, CHUNKS))
                for w in range(2):
                    nc.scalar.copy(sums[:, w].rearrange("p h (a i) -> p a h i", a=2),
                                   acc[:, buf, 2 * w:2 * w + 2]).then_inc(sums_taken.sem, 1)

            def tile(it, buf, first, last):
                for c in range(CHUNKS):
                    act.wait_ge(shifted.sem, shifted.at(it, c + 1))
                    pc = chunk_flat(p_ring, c)
                    nc.scalar.activation(pc, pc, ACT.Exp).then_inc(exp_done.sem, 1)
                    if not first and c == TAKE_SUMS_AT:
                        take_sums(it - 1, 1 - buf)
                    if not first and c == COPY_O_AT:
                        copy_oT(it - 1, 1 - buf)
                    if not last and c == COPY_XN_AT:
                        copy_xnT(it + 1, 1 - buf)
                    if not last and c in TAKE_AT:
                        take(it + 1, 1 - buf, TAKE_AT.index(c))

            copy_xnT(0, 0)
            for i in range(3):
                take(0, 0, i)
            all_tiles(act, tile)
            take_sums(TILES - 1, 1)
            copy_oT(TILES - 1, 1)

        @block.tensor
        def _(pe):
            def turn_xn(it, buf):
                pe.wait_ge(xn_step.sem, xn_step.at(it, 6))
                nc.tensor.transpose(stages[:, buf, 0, 0:P], xn[:, 0, :], k["ident"][:]).then_inc(xnT_psum.sem, 1)

            def qkv(it, buf, i):
                pe.wait_ge(xnT_ready.sem, xnT_ready.at(it, 1))
                if i == 2:
                    pe.wait_ge(qkv_taken.sem, qkv_taken.at(it, 1))
                for half in range(2):
                    last = nc.tensor.matmul(stages[:, buf, 2 * (i % 2) + half, :], xnT[:],
                                            k["wqkv"][:, i, half * 512:(half + 1) * 512], start=True, stop=False)
                    last = nc.tensor.matmul(stages[:, buf, 2 * (i % 2) + half, :], k["ones3"][:],
                                            k["bias3"][:, i, half * 512:(half + 1) * 512], start=False, stop=True)
                last.then_inc(qkv_psum.sem, 1)

            def turn_o(it, buf):
                pe.wait_ge(divided.sem, divided.at(it, 2))
                of = sums[:, 0].rearrange("p h c -> p (h c)")
                for i in range(HID // P):
                    last = nc.tensor.transpose(stages[:, buf, i // 4, i % 4 * P:(i % 4 + 1) * P], of[:, i * P:(i + 1) * P],
                                               k["ident"][:])
                last.then_inc(oT_psum.sem, 1)

            def project(it, buf):
                pe.wait_ge(oT_ready.sem, oT_ready.at(it, 1))
                for i in range(HID // P):
                    last = nc.tensor.matmul(stages[:, buf, 2, 0:D], oT[:, i * P:(i + 1) * P], k["wo"][:, i, :],
                                            start=i == 0, stop=i == HID // P - 1)
                last.then_inc(o_psum.sem, 1)

            def tile(it, buf, first, last_tile):
                for c in range(CHUNKS):
                    if c == 0:
                        pe.wait_ge(qkv_taken.sem, qkv_taken.at(it, 3))
                    pe.wait_ge(ev_dve.sem, ev_dve.at(it, c + 1))
                    pe.wait_ge(ev_pool.sem, ev_pool.at(it, c + 1))
                    if ORDER[c] in FOLD_EV or ORDER[c] in FOLD_P:
                        pe.wait_ge(folded.sem, folded.at(it, folds_until(c)))
                    j0 = JB * ORDER[c]
                    for w, (ring, which) in enumerate(((ev_ring, FOLD_EV), (p_ring, FOLD_P))):
                        src = chunk(ring, c)
                        last_j = 0 if ORDER[c] in which else JB - 1
                        for half in range(2):
                            lo, hi = max(j0, half * 32), half * 32 + 32
                            if lo >= hi:
                                continue
                            closes = all(max(JB * d, half * 32) >= hi for d in ORDER[c + 1:])
                            for j in range(last_j + 1):
                                last = nc.tensor.matmul(acc[:, buf, 2 * w + half, :, lo - 32 * half:], k["ident"][:],
                                                        src[:, :, j, lo - j0:hi - j0],
                                                        start=c == 0 and j == 0, stop=closes and j == last_j)
                    last.then_inc(summed.sem, 1)
                    if not first and c == TURN_O_AT:
                        turn_o(it - 1, 1 - buf)
                    if not first and c == PROJECT_AT:
                        project(it - 1, 1 - buf)
                    if last_tile:
                        continue
                    if c == TURN_XN_AT:
                        turn_xn(it + 1, 1 - buf)
                    if c in QKV_AT:
                        qkv(it + 1, 1 - buf, QKV_AT.index(c))

            turn_xn(0, 0)
            for i in range(3):
                qkv(0, 0, i)
            all_tiles(pe, tile)
            turn_o(TILES - 1, 1)
            project(TILES - 1, 1)


def build(nc, a, out):
    with ExitStack() as ctx, ExitStack() as ctx_a:
        sb = lambda n, s, d=F32: ctx.enter_context(nc.sbuf_tensor(n, s, d))
        sb_a = lambda n, s, d=F32: ctx_a.enter_context(nc.sbuf_tensor(n, s, d))
        x_all = sb("x_all", [P, TILES, D])
        k = {}
        for name, shape, dt in (
            ("ident", [P, P], F32), ("wT", [P, D], F32), ("wpT", [P, PROJ], F32), ("wdT", [P, E * R_PAD], F32),
            ("wu", [E * R_PAD, D], F32), ("bp", [PROJ, 1], F32), ("sim", [PROJ, E], F32), ("temp", [PROJ, 1], F32),
            ("rank4", [P, E], F32), ("wqkv", [P, 3, HID], F32), ("bo", [P, D], F32), ("wo", [P, HID // P, D], F32),
            ("reset_max", [P, HID], BF16), ("reset_min", [P, HID], BF16),
        ):
            k[name] = sb("k_" + name, shape, dt)
        loads = list(k)
        for name, shape in (("pw", [P, 64]), ("ph", [P, 64]), ("ones32", [PROJ, PROJ]), ("simn", [PROJ, E]), ("lam", [P, 1]),
                            ("gamma8", [P, A_V]), ("tmp", [P, 4, A_HD])):
            k[name] = sb("k_" + name, shape)
        k["ones3"] = sb("ones3", [3, P], BF16)
        k["bias3"] = sb("bias3", [3, 3, HID], BF16)
        t32 = sb("t32", [PROJ, 6, E])
        for name, shape, dt in (
            ("w_attn", [P, 3 * D], F32), ("w_proj", [P, D], F32), ("ident_b", [P, P], BF16), ("mask", [P, P], BF16),
            ("mask_t", [P, P], BF16), ("sel_q", [P, 3, GROUPS * P], BF16), ("sel_k", [P, 3, GROUPS * P], BF16),
            ("one_rows", [P, 1], F32), ("bias", [1, 3 * HID], F32), ("lams", [P, 4, A_HD], F32), ("gamma", [P, A_V], F32),
        ):
            k[name] = sb_a("k_" + name, shape, dt)
            loads.append(name)
        rows_q = sb_a("rows_q", [P, 3, BATCH * T], BF16)
        rows_k = sb_a("rows_k", [P, 3, BATCH * T], BF16)
        v_nat = sb_a("v_nat", [P, TILES, D])
        att = sb_a("att", [P, TILES, D])
        phase_a1(nc, a, loads, x_all, k, t32, rows_q, rows_k, v_nat)
        phase_a2(nc, rows_q, rows_k, v_nat, att, k)
        phase_a3(nc, x_all, att, k["w_proj"], k["ident"], k["gamma8"])
        ctx_a.close()
        phase_f(nc, "f1", x_all, k, None)
        phase_b(nc, x_all, k)
        phase_f(nc, "f2", x_all, k, out)


def kernel(**inputs):
    import ml_dtypes
    import numpy as np
    import concourse.bacc as bacc
    from concourse.bass_utils import run_bass_kernel_spmd as run

    i = {n: np.asarray(v) for n, v in inputs.items()}
    A, B, F = "L0_attn_a_", "L0_attn_b_", "L0_ffn_"
    bf = ml_dtypes.bfloat16
    rows = lambda v, n=P: np.ascontiguousarray(np.broadcast_to(v, (n,) + v.shape))
    x = i[A + "x"]
    arrays = {
        "x": x, "w_attn": i[A + "w_attn"], "w_proj": i[A + "w_proj"],
        "lams": rows(np.stack([i[A + "lambda_q1"], i[A + "lambda_k1"], i[A + "lambda_q2"], i[A + "lambda_k2"]])),
        "gamma": rows(i[A + "gamma"]),
        "wT": i[F + "W"].T, "wpT": i[F + "Wp"].T, "bp": i[F + "bp"][:, None], "sim": i[F + "sim"],
        "temp": rows(i[F + "temp"], PROJ),
        "wqkv": np.stack([i[B + "Wq"], i[B + "Wk"], i[B + "Wv"]], 1),
        "bias": np.concatenate([i[B + "bq"], i[B + "bk"], i[B + "bv"]])[None], "bo": rows(i[B + "bo"]),
        "wo": i[B + "Wo"].reshape(HID // P, P, D).transpose(1, 0, 2),
    }
    wd = np.zeros((E, R_PAD, D), np.float32)
    wu = np.zeros((E, R_PAD, D), np.float32)
    for e in range(E):
        d, u = i[F + f"Wd{e}"], i[F + f"Wu{e}"]
        wd[e, :d.shape[0]] = d
        wu[e, :u.shape[1]] = u.T
    arrays["wdT"] = wd.reshape(E * R_PAD, D).T
    arrays["wu"] = wu.reshape(E * R_PAD, D)
    arrays["ident"] = np.eye(P, dtype=np.float32)
    arrays["ident_b"] = np.eye(P, dtype=np.float32).astype(bf)
    later = np.triu(np.ones((P, P), np.float32), 1)
    arrays["mask"] = (NEG * later).astype(bf)
    arrays["mask_t"] = (NEG * later.T).astype(bf)
    for name, terms in (("sel_q", TERM_Q), ("sel_k", TERM_K)):
        sel = np.zeros((P, 3, GROUPS, 4, 32), np.float32)
        for g in range(GROUPS):
            for h in range(4):
                for t, part in enumerate(terms):
                    for d in range(A_HD):
                        sel[(4 * g + h) * A_HD + d, part, g, h, t * A_HD + d] = 1.0
        arrays[name] = sel.reshape(P, 3, GROUPS * P).astype(bf)
    one = np.zeros((4, 32, 1), np.float32)
    one[:, M_ROW:M_ROW + 3] = 1.0
    arrays["one_rows"] = one.reshape(P, 1)
    arrays["rank4"] = rows(np.arange(E, 0, -1).astype(np.float32))
    first = (np.arange(HID) % C == 0)
    arrays["reset_max"] = rows(np.where(first, -BIG, BIG).astype(bf))
    arrays["reset_min"] = rows(np.where(first, BIG, -BIG).astype(bf))

    nc = bacc.Bacc("TRN2", target_bir_lowering=False, num_devices=1)
    feeds, args = {}, {}
    for name, v in arrays.items():
        v = np.ascontiguousarray(v)
        feeds[f"in_{name}"] = v
        args[name] = nc.dram_tensor(f"in_{name}", v.shape, mybir.dt.from_np(v.dtype), kind="ExternalInput").ap()
    args["x"] = args["x"].rearrange("b (n p) d -> p (b n) d", p=P)
    out = nc.dram_tensor("out", x.shape, F32, kind="ExternalOutput").ap()
    build(nc, args, out.rearrange("b (n p) d -> p (b n) d", p=P))
    r = run(nc, [feeds], core_ids=[0])
    return r.results[0]["out"]
```
